# Optimizing a Trainium2 kernel written in Bass

```python
import numpy as np
import jax
import jax.numpy as jnp

def _softmax(x, axis=-1):
    return jax.nn.softmax(x, axis=axis)

def _gelu(x):
    return jax.nn.gelu(x, approximate=True)

def _silu(x):
    return jax.nn.silu(x)

def _sigmoid(x):
    return jax.nn.sigmoid(x)

def _layernorm(x, axis=-1, eps=1e-05):
    m = jnp.mean(x, axis=axis, keepdims=True)
    v = jnp.var(x, axis=axis, keepdims=True)
    return (x - m) / jnp.sqrt(v + eps)

def _scatter_add(tgt, idx, src, axis=0):
    return tgt.at[idx].add(src)

def _segment_sum(src, seg, n):
    return jax.ops.segment_sum(src, seg, n)
kernel_name = 'mk_seq_preln_d2_jaxref_r8_83837e'

def setup_inputs(seed: int=0):
    np.random.seed(seed)
    _w = jnp.asarray

    def _L0_attn_setup():
        import jax, jax.numpy as jnp
        import numpy as np
        D_MODEL, D_STATE, D_CONV, D_INNER = (128, 16, 4, 256)
        BATCH, SEQ = (2, 256)
        key = jax.random.key(seed)
        ks = jax.random.split(key, 12)
        s = 0.02
        inp = {'x': jax.random.normal(ks[0], (BATCH, SEQ, D_MODEL), jnp.float32), 'W_in': jax.random.normal(ks[1], (D_MODEL, 2 * D_INNER), jnp.float32) * s, 'b_in': jnp.zeros((2 * D_INNER,), jnp.float32), 'conv_w': jax.random.normal(ks[2], (D_INNER, 1, D_CONV), jnp.float32) * s, 'conv_b': jnp.zeros((D_INNER,), jnp.float32), 'W_x': jax.random.normal(ks[3], (D_INNER, 2 * D_STATE), jnp.float32) * s, 'b_x': jnp.zeros((2 * D_STATE,), jnp.float32), 'W_dt': jax.random.normal(ks[4], (D_INNER, D_INNER), jnp.float32) * s, 'b_dt': jnp.zeros((D_INNER,), jnp.float32), 'A_log': jnp.log(jnp.tile(jnp.arange(1, D_STATE + 1, dtype=jnp.float32), (D_INNER, 1))), 'D': jnp.ones((D_INNER,), jnp.float32), 'W_out': jax.random.normal(ks[5], (D_INNER, D_MODEL), jnp.float32) * s, 'b_out': jnp.zeros((D_MODEL,), jnp.float32)}
        return inp
    _L0_attn_in = _L0_attn_setup()

    def _L0_ffn_setup():
        import math
        import jax, jax.numpy as jnp
        import numpy as np
        NUM_EXPERTS = 8
        CAPACITY_FACTOR = 1.5
        key = jax.random.key(seed)
        ks = jax.random.split(key, 4)
        B, T, D, F, E = (4, 256, 128, 512, NUM_EXPERTS)
        scale = 0.02
        return {'x': jax.random.normal(ks[0], (B, T, D), dtype=jnp.float32), 'router_w': jax.random.normal(ks[1], (E, D), dtype=jnp.float32) * scale, 'w1': jax.random.normal(ks[2], (E, D, F), dtype=jnp.float32) * scale, 'b1': jnp.zeros((E, F), dtype=jnp.float32), 'w2': jax.random.normal(ks[3], (E, F, D), dtype=jnp.float32) * scale, 'b2': jnp.zeros((E, D), dtype=jnp.float32)}
    _L0_ffn_in = _L0_ffn_setup()

    def _L1_attn_setup():
        import jax, jax.numpy as jnp
        import numpy as np
        D = 128
        H = 16
        S = 2
        MAX_LEN = 256
        HEAD_DIM = D // H // S
        DV = D // H
        SCALING = (D // H) ** (-0.5)
        key = jax.random.key(seed)
        k1, k2, k3, k4, k5, k6 = jax.random.split(key, 6)
        L, B = (2046, 4)
        input_tensor = jax.random.normal(k1, (L, B, D), dtype=jnp.float32)
        w_kv = jax.random.normal(k2, (MAX_LEN // S, MAX_LEN), dtype=jnp.float32) / np.sqrt(MAX_LEN)
        w_q = jax.random.normal(k3, (D // S, D), dtype=jnp.float32) / np.sqrt(D)
        b_q = jax.random.normal(k4, (D // S,), dtype=jnp.float32) * 0.01
        w_out = jax.random.normal(k5, (D, D), dtype=jnp.float32) / np.sqrt(D)
        b_out = jax.random.normal(k6, (D,), dtype=jnp.float32) * 0.01
        return {'input_tensor': input_tensor, 'w_kv': w_kv, 'w_q': w_q, 'b_q': b_q, 'w_out': w_out, 'b_out': b_out}
    _L1_attn_in = _L1_attn_setup()

    def _L1_ffn_setup():
        import jax, jax.numpy as jnp
        import numpy as np
        DIM = 128
        HIDDEN = 384
        SCALE = 1.0 / 127.0

        def _dequant(w_int, dtype):
            return w_int.astype(dtype) * jnp.asarray(SCALE, dtype)
        key = jax.random.key(seed)
        k_x, k_g, k_u, k_d = jax.random.split(key, 4)
        x = jax.random.normal(k_x, (4, 256, DIM), dtype=jnp.float32)
        w_gate = jax.random.randint(k_g, (HIDDEN, DIM), -127, 128, dtype=jnp.int32)
        w_up = jax.random.randint(k_u, (HIDDEN, DIM), -127, 128, dtype=jnp.int32)
        w_down = jax.random.randint(k_d, (DIM, HIDDEN), -127, 128, dtype=jnp.int32)
        return {'x': x, 'w_gate': w_gate, 'w_up': w_up, 'w_down': w_down}
    _L1_ffn_in = _L1_ffn_setup()
    _d = {'L0_attn_x': _L0_attn_in['x'], 'L0_attn_W_in': _L0_attn_in['W_in'], 'L0_attn_b_in': _L0_attn_in['b_in'], 'L0_attn_conv_w': _L0_attn_in['conv_w'], 'L0_attn_conv_b': _L0_attn_in['conv_b'], 'L0_attn_W_x': _L0_attn_in['W_x'], 'L0_attn_b_x': _L0_attn_in['b_x'], 'L0_attn_W_dt': _L0_attn_in['W_dt'], 'L0_attn_b_dt': _L0_attn_in['b_dt'], 'L0_attn_A_log': _L0_attn_in['A_log'], 'L0_attn_D': _L0_attn_in['D'], 'L0_attn_W_out': _L0_attn_in['W_out'], 'L0_attn_b_out': _L0_attn_in['b_out'], 'L0_ffn_router_w': _L0_ffn_in['router_w'], 'L0_ffn_w1': _L0_ffn_in['w1'], 'L0_ffn_b1': _L0_ffn_in['b1'], 'L0_ffn_w2': _L0_ffn_in['w2'], 'L0_ffn_b2': _L0_ffn_in['b2'], 'L1_attn_w_kv': _L1_attn_in['w_kv'], 'L1_attn_w_q': _L1_attn_in['w_q'], 'L1_attn_b_q': _L1_attn_in['b_q'], 'L1_attn_w_out': _L1_attn_in['w_out'], 'L1_attn_b_out': _L1_attn_in['b_out'], 'L1_ffn_w_gate': _L1_ffn_in['w_gate'], 'L1_ffn_w_up': _L1_ffn_in['w_up'], 'L1_ffn_w_down': _L1_ffn_in['w_down']}
    _x0 = _d['L0_attn_x']
    _d['L0_attn_x'] = jax.random.normal(jax.random.fold_in(jax.random.key(seed), 1), (16, 512, 128), dtype=_x0.dtype)
    del _x0
    return _d

def reference(L0_attn_x, L0_attn_W_in, L0_attn_b_in, L0_attn_conv_w, L0_attn_conv_b, L0_attn_W_x, L0_attn_b_x, L0_attn_W_dt, L0_attn_b_dt, L0_attn_A_log, L0_attn_D, L0_attn_W_out, L0_attn_b_out, L0_ffn_router_w, L0_ffn_w1, L0_ffn_b1, L0_ffn_w2, L0_ffn_b2, L1_attn_w_kv, L1_attn_w_q, L1_attn_b_q, L1_attn_w_out, L1_attn_b_out, L1_ffn_w_gate, L1_ffn_w_up, L1_ffn_w_down):

    def _L0_attn_ref(x, W_in, b_in, conv_w, conv_b, W_x, b_x, W_dt, b_dt, A_log, D, W_out, b_out):
        import jax, jax.numpy as jnp
        import numpy as np
        D_MODEL, D_STATE, D_CONV, D_INNER = (128, 16, 4, 256)
        BATCH, SEQ = (2, 256)
        d_inner, d_state = A_log.shape
        d_conv = conv_w.shape[-1]
        bsz, seq_len, _ = x.shape
        xz = x @ W_in + b_in
        xh, z = jnp.split(xz, 2, axis=-1)
        xc = jnp.transpose(xh, (0, 2, 1))
        xc = jax.lax.conv_general_dilated(xc, conv_w, window_strides=(1,), padding=[(d_conv - 1, 0)], dimension_numbers=('NCH', 'OIH', 'NCH'), feature_group_count=d_inner)
        xc = xc + conv_b[None, :, None]
        xh = jax.nn.silu(jnp.transpose(xc, (0, 2, 1)))
        A = -jnp.exp(A_log)
        x_dbl = xh @ W_x + b_x
        Bmat = x_dbl[..., d_state:]
        delta = jax.nn.softplus(xh @ W_dt + b_dt)

        def step(h, inp):
            d_t, b_t, u_t = inp
            dA = jnp.exp(d_t[:, :, None] * A)
            dBu = d_t[:, :, None] * b_t[:, None, :] * u_t[:, :, None]
            h = dA * h + dBu
            return (h, h.sum(-1))
        h0 = jnp.zeros((bsz, d_inner, d_state), x.dtype)
        _, ys = jax.lax.scan(step, h0, (jnp.swapaxes(delta, 0, 1), jnp.swapaxes(Bmat, 0, 1), jnp.swapaxes(xh, 0, 1)))
        y = jnp.swapaxes(ys, 0, 1) + xh * D
        y = y * jax.nn.silu(z)
        return y @ W_out + b_out

    def _L0_ffn_ref(x, router_w, w1, b1, w2, b2):
        import math
        import jax, jax.numpy as jnp
        import numpy as np
        NUM_EXPERTS = 8
        CAPACITY_FACTOR = 1.5
        B, T, D = x.shape
        E = router_w.shape[0]
        N = B * T
        C = max(math.ceil(CAPACITY_FACTOR * N / E), 1)
        x_flat = x.reshape(N, D)
        logits = x_flat @ router_w.T
        probs = jax.nn.softmax(logits, axis=-1)
        chosen_e = jnp.argmax(probs, axis=-1)
        chosen_p = jnp.max(probs, axis=-1)
        onehot = jax.nn.one_hot(chosen_e, E, dtype=jnp.float32)
        pos = jnp.take_along_axis(jnp.cumsum(onehot, axis=0), chosen_e[:, None], axis=1)[:, 0] - 1.0
        pos = pos.astype(jnp.int32)
        kept = pos < C
        pos_c = jnp.clip(pos, 0, C - 1)
        buf = jnp.zeros((E, C, D), dtype=x.dtype).at[chosen_e, pos_c].add(x_flat * kept[:, None].astype(x.dtype))
        h = jax.nn.gelu(jnp.einsum('ecd,edf->ecf', buf, w1) + b1[:, None, :], approximate=False)
        eo = jnp.einsum('ecf,efd->ecd', h, w2) + b2[:, None, :]
        y = eo[chosen_e, pos_c] * (chosen_p * kept.astype(x.dtype))[:, None]
        return y.reshape(B, T, D)

    def _L1_attn_ref(input_tensor, w_kv, w_q, b_q, w_out, b_out):
        import jax, jax.numpy as jnp
        import numpy as np
        D = 128
        H = 16
        S = 2
        MAX_LEN = 256
        HEAD_DIM = D // H // S
        DV = D // H
        SCALING = (D // H) ** (-0.5)
        L, B, _ = input_tensor.shape
        P = L // S + 1
        X = jnp.transpose(input_tensor, (1, 0, 2))
        q = X @ w_q.T + b_q
        Wp = w_kv.T[:L, :P]
        v = jnp.einsum('bld,lp->bdp', X, Wp)
        k = jnp.einsum('blc,lp->bcp', q, Wp)
        q = q * SCALING
        qh = q.reshape(B, L, H, HEAD_DIM).transpose(0, 2, 1, 3)
        kh = k.reshape(B, HEAD_DIM, H, P).transpose(0, 2, 1, 3)
        vh = v.reshape(B, DV, H, P).transpose(0, 2, 3, 1)
        attn = jnp.einsum('bhld,bhdp->bhlp', qh, kh)
        attn = jax.nn.softmax(attn.astype(jnp.float32), axis=-1).astype(attn.dtype)
        out = jnp.einsum('bhlp,bhpd->bhld', attn, vh)
        out = out.transpose(0, 2, 3, 1).reshape(B, L, D)
        out = out @ w_out.T + b_out
        return jnp.transpose(out, (1, 0, 2))

    def _L1_ffn_ref(x, w_gate, w_up, w_down):
        import jax, jax.numpy as jnp
        import numpy as np
        DIM = 128
        HIDDEN = 384
        SCALE = 1.0 / 127.0

        def _dequant(w_int, dtype):
            return w_int.astype(dtype) * jnp.asarray(SCALE, dtype)
        wg = _dequant(w_gate, x.dtype)
        wu = _dequant(w_up, x.dtype)
        wd = _dequant(w_down, x.dtype)
        gate = jnp.einsum('bsd,hd->bsh', x, wg)
        up = jnp.einsum('bsd,hd->bsh', x, wu)
        h = jax.nn.silu(gate) * up
        return jnp.einsum('bsh,dh->bsd', h, wd)
    x = L0_attn_x
    x = x + _L0_attn_ref(_layernorm(x, axis=-1), L0_attn_W_in, L0_attn_b_in, L0_attn_conv_w, L0_attn_conv_b, L0_attn_W_x, L0_attn_b_x, L0_attn_W_dt, L0_attn_b_dt, L0_attn_A_log, L0_attn_D, L0_attn_W_out, L0_attn_b_out)
    x = x + _L0_ffn_ref(_layernorm(x, axis=-1), L0_ffn_router_w, L0_ffn_w1, L0_ffn_b1, L0_ffn_w2, L0_ffn_b2)
    x = x + _L1_attn_ref(_layernorm(x, axis=-1), L1_attn_w_kv, L1_attn_w_q, L1_attn_b_q, L1_attn_w_out, L1_attn_b_out)
    x = x + _L1_ffn_ref(_layernorm(x, axis=-1), L1_ffn_w_gate, L1_ffn_w_up, L1_ffn_w_down)
    return x

_drawn_inputs = setup_inputs


def setup_inputs(seed=0):
    import zlib

    import numpy as np

    out = dict(_drawn_inputs(seed))
    spreads = {'L0_attn_b_in': (0.0, 0.8),
     'L0_attn_conv_b': (0.0, 0.8),
     'L0_attn_b_x': (0.0, 0.8),
     'L0_attn_b_dt': (0.0, 0.8),
     'L0_attn_D': (1.0, 0.6),
     'L0_attn_b_out': (0.0, 0.575),
     'L0_ffn_b1': (0.0, 2.0),
     'L0_ffn_b2': (0.0, 2.0)}
    factors = {'L0_attn_W_in': 8.0,
     'L0_attn_conv_w': 8.0,
     'L0_attn_W_x': 8.0,
     'L0_attn_W_dt': 8.0,
     'L0_attn_A_log': 8.0,
     'L0_attn_W_out': 8.0,
     'L0_ffn_w1': 4.25,
     'L0_ffn_w2': 3.904,
     'L1_attn_b_q': 64.0,
     'L1_attn_b_out': 26.696,
     'L1_attn_w_kv': 7.417,
     'L1_attn_w_q': 8.0,
     'L1_attn_w_out': 4.854}
    for name, (base, spread) in spreads.items():
        noise = np.random.default_rng([zlib.crc32(name.encode()), seed]).standard_normal(out[name].shape)
        drawn = base * np.exp(spread * noise) if base else spread * noise
        out[name] = jnp.asarray(drawn.astype(out[name].dtype))
    for name, factor in factors.items():
        out[name] = (out[name] * factor).astype(out[name].dtype)
    return out
```

```python
import concourse.bass as bass
from concourse import mybir
from contextlib import ExitStack


class Steps:

    def __init__(self, sem, names):
        self.sem, self.names, self.per = sem, list(names), len(names)

    def upto(self, group, name):
        return group * self.per + self.names.index(name) + 1


class Group:

    def __init__(self, off, reg=None, stride=2):
        self.off, self.reg, self.stride, self.par = off, reg, stride, off % 2

    def __add__(self, k):
        return Group(self.off + k, self.reg, self.stride)

    def __sub__(self, k):
        return self + -k

    def __mul__(self, k):
        return k * self.off if self.reg is None else self.reg * (self.stride * k) + k * self.off

    __rmul__ = __mul__

    def __floordiv__(self, k):
        return Group(self.off // k, self.reg, self.stride // k)

    def least(self, k):
        return self.off >= k


def prog(nc, P):
    fp32 = mybir.dt.float32
    bf16 = mybir.dt.bfloat16
    i32 = mybir.dt.int32
    u32 = mybir.dt.uint32
    ALU = mybir.AluOpType
    ACT = mybir.ActivationFunctionType
    AX = mybir.AxisListType

    x = P["L0_attn_x"]
    B, L, D = x.shape
    DI = P["L0_attn_W_dt"].shape[0]
    NH = DI // 128
    N = 16
    TOK = B * L
    TILES = TOK // 128
    E, FF = P["L0_ffn_b1"].shape
    CAP = -(-3 * TOK // (2 * E))
    SLOTS = E * CAP
    EPS = 1e-5
    SEQ = 2
    G = B // SEQ
    GT = SEQ * L
    KT = GT // 128
    TAPS = 4
    PAD = TAPS - 1

    HG = P["w_gateT"].shape[1]
    KH, KF = HG // 128, FF // 128
    HEADS = 16
    QD = D // 2
    QH, DV = QD // HEADS, D // HEADS
    SL = B // 2 + 1
    C8 = 8
    TB = L // 128
    BQ = 4

    ctx = ExitStack()
    with ctx:
        here = [ctx]

        def sb(n, s, d=fp32):
            return here[0].enter_context(nc.sbuf_tensor(n, s, d))

        def pb(n, s, d=fp32):
            return here[0].enter_context(nc.psum_tensor(n, s, d))

        def sem(n):
            return ctx.enter_context(nc.semaphore(n))

        slots_in = nc.dram_tensor("slots_in", (SLOTS, D), fp32, kind="Internal").ap()
        slots_out = nc.dram_tensor("slots_out", (SLOTS, D), fp32, kind="Internal").ap()

        xres = sb("xres", [128, TILES, D])
        halfs = sb("halfs", [128, B])
        gidx = sb("gidx", [128, TILES], i32)
        gwt = sb("gwt", [128, TILES])
        ident = sb("ident", [128, 128])
        ones = sb("ones", [128, 128])

        here[0] = ExitStack()
        w_in = sb("w_in", [128, 2 * DI])
        w_dt = sb("w_dt", [128, NH, DI])
        w_b = sb("w_b", [128, NH, 96])
        w_out = sb("w_out", [128, NH, D])
        b_out = sb("b_out", [1, D])
        cols = sb("cols", [128, P["cols"].shape[1]])
        c_bin = lambda c: cols[:, c:c + 1]
        c_cb = lambda h: cols[:, 4 + h:5 + h]
        c_bdt = lambda h: cols[:, 6 + h:7 + h]
        c_D = lambda h: cols[:, 8 + h:9 + h]
        c_bx = cols[:, 10:11]
        c_cw = lambda h, k: cols[:, 11 + TAPS * h + k:12 + TAPS * h + k]
        c_alog = cols[:, 19:19 + NH * N]
        rt_w = sb("rt_w", [128, E])
        A = sb("A", [128, NH * N])
        tapb = sb("tapb", [128, NH])
        tri = sb("tri", [128, 128])
        sel = sb("sel", [96, N, 128], bf16)
        half = halfs[:, 0:KT]
        w8 = sb("w8", [128, E])

        stat = sb("stat", [128, KT, 6])
        mv = sb("mv", [128, KT, 2])
        veps = sb("veps", [128, KT])
        nmean = sb("nmean", [128, KT])
        rstd = sb("rstd", [128, KT])
        nmr = sb("nmr", [128, KT])
        xn = sb("xn", [128, KT, D])
        xnT = sb("xnT", [128, GT])
        xhp = sb("xhp", [128, NH, SEQ, PAD + L])
        acc = sb("acc", [128, NH, SEQ, L])
        Bf = sb("Bf", [96, GT])
        Br = sb("Br", [96, GT])
        u = [sb(f"u{i}", [128, NH, GT]) for i in range(2)]
        zs = [sb(f"zs{i}", [128, NH, GT]) for i in range(2)]
        dl = [sb(f"dl{i}", [128, NH, GT]) for i in range(2)]
        wu = [sb(f"wu{i}", [128, NH, GT]) for i in range(2)]
        Bs = [sb(f"Bs{i}", [96, GT], bf16) for i in range(2)]
        NB = 4
        dA = [sb(f"dA{i}", [128, SEQ, L]) for i in range(NB)]
        dB = [sb(f"dB{i}", [128, GT]) for i in range(NH)]
        hs = [sb(f"hs{i}", [128, GT]) for i in range(NB)]
        yz = sb("yz", [128, NH, GT])
        zero = yz[:, :, :].rearrange("p h t -> p (h t)")[:, 0:SLOTS // 8 * D // 128]
        stat2 = sb("stat2", [128, KT, 6])
        mv2 = sb("mv2", [128, KT, 2])
        veps2 = sb("veps2", [128, KT])
        nmean2 = sb("nmean2", [128, KT])
        rstd2 = sb("rstd2", [128, KT])
        nmr2 = sb("nmr2", [128, KT])
        xn2 = sb("xn2", [128, KT, D])
        xn2T = sb("xn2T", [128, GT])
        mx = sb("mx", [128, KT])
        lm = sb("lm", [128, KT, E])
        ex = sb("ex", [128, KT, E])
        sm = sb("sm", [128, KT])
        pr = sb("pr", [128, KT])
        sc = sb("sc", [128, KT, E])
        ms = sb("ms", [128, KT])
        oh = sb("oh", [128, KT, E])
        pre = sb("pre", [128, KT + 1, E])
        oc = sb("oc", [128, KT, E])
        rank = sb("rank", [128, KT])
        base = sb("base", [128, KT])
        lost = sb("lost", [128, KT])
        kept = sb("kept", [128, KT])
        srow = sb("srow", [128, KT])
        grow = sb("grow", [128, KT])
        sidx = sb("sidx", [128, KT], i32)

        pY = [pb(f"pY{h}", [128, GT]) for h in range(NH)]
        pB = pb("pB", [128, GT])
        pJ = [pb(f"pJ{i}", [128, 512]) for i in range(2)]

        here[0].close()

        here[0] = ctx
        wq = sb("wq", [128, QD])
        bq = sb("bq", [1, QD])
        wo = sb("wo", [128, D])
        bo = sb("bo", [1, D])
        wkr = sb("wkr", [128, SL])
        mask8 = sb("mask8", [128, C8])
        wk = sb("wk", [128, C8, SL])
        gi = sb("gi", [128, HG], i32)
        ui = sb("ui", [128, HG], i32)
        di = sb("di", [128, KH, D], i32)
        wg = sb("wg", [128, HG])
        wup = sb("wup", [128, HG])
        wd = sb("wd", [128, KH, D])

        here[0] = ExitStack()
        w1 = [sb(f"w1{i}", [128, FF]) for i in range(2)]
        w2 = [sb(f"w2{i}", [128, KF, D]) for i in range(2)]
        b1 = [sb(f"b1{i}", [128, KF]) for i in range(2)]
        b2 = [sb(f"b2{i}", [128, D]) for i in range(2)]
        xe = [sb(f"xe{i}", [128, 4, D]) for i in range(2)]
        xeT = [sb(f"xeT{i}", [128, 512]) for i in range(2)]
        he = [sb(f"he{i}", [128, KF, 512]) for i in range(2)]
        ye = [sb(f"ye{i}", [128, 4, D]) for i in range(2)]
        pT = [pb(f"pT{i}", [128, 512]) for i in range(2)]
        pH = [pb(f"pH{i}", [128, 512]) for i in range(KF)]
        pE = [pb(f"pE{i}", [128, 512]) for i in range(2)]
        here[0].close()

        here[0] = ExitStack()
        gx = sb("gx", [128, B, D])
        stA = sb("stA", [128, B, 6])
        mvA = sb("mvA", [128, B, 2])
        veA = sb("veA", [128, B])
        nmA = sb("nmA", [128, B])
        rsA = sb("rsA", [128, B])
        nrA = sb("nrA", [128, B])
        xnA = sb("xnA", [128, B, D])
        xnAT = sb("xnAT", [128, B, 128])
        xnG = sb("xnG", [128, D // C8, 128])
        q = [sb(f"q{i}", [128, B, QD]) for i in range(2)]
        qG = sb("qG", [128, QD // C8, 128])
        kk = [sb(f"kk{i}", [128, QD, SL]) for i in range(2)]
        vv = [sb(f"vv{i}", [128, D, SL]) for i in range(2)]
        qk = [sb(f"qk{i}", [128, BQ, HEADS, SL]) for i in range(QH)]
        at = [sb(f"at{i}", [128, BQ * HEADS, SL]) for i in range(2)]
        am = sb("am", [128, BQ * HEADS])
        ad = sb("ad", [128, BQ * HEADS])
        ar = sb("ar", [128, BQ * HEADS])
        pv = [sb(f"pv{i}", [128, HEADS, DV, SL]) for i in range(2)]
        oo = [sb(f"oo{i}", [128, BQ, D]) for i in range(2)]
        on = [sb(f"on{i}", [128, BQ, D]) for i in range(2)]
        oT = sb("oT", [128, BQ * 128])
        stB = sb("stB", [128, BQ, 6])
        mvB = sb("mvB", [128, BQ, 2])
        veB = sb("veB", [128, BQ])
        nmB = sb("nmB", [128, BQ])
        rsB = sb("rsB", [128, BQ])
        nrB = sb("nrB", [128, BQ])
        xnB = sb("xnB", [128, BQ, D])
        xnBT = [sb(f"xnBT{i}", [128, BQ * 128]) for i in range(2)]
        sg = [sb(f"sg{i}", [128, BQ * 128]) for i in range(2)]
        hh = sb("hh", [128, KH, BQ * 128])
        pA = [pb(f"pA{i}", [128, 512]) for i in range(2)]
        pS1, pS2 = pb("pS1", [128, 512]), pb("pS2", [128, 512])
        pG = [pb(f"pG{i}", [128, 512]) for i in range(2)]
        pU = [pb(f"pU{i}", [128, 512]) for i in range(2)]
        here[0].close()
        here[0] = ctx

        s_w = sem("s_w")
        s_passed = sem("s_passed")
        s_x = sem("s_x")
        s_zero = sem("s_zero")
        s_cst = sem("s_cst")
        s_A = sem("s_A")
        s_sel = sem("s_sel")
        s_zr = sem("s_zr")
        s_out = sem("s_out")
        s_scat = sem("s_scat")

        PRE_DVE = Steps(sem("pre_dve"), ["stats", "aggr", "center"] +
                        [f"conv{h}_{k}" for h in range(NH) for k in range(TAPS - 1)] + ["delta", "w"])
        PRE_POOL = Steps(sem("pre_pool"), ["rstd", "nmr", "part2", "part3"])
        PRE_ACT = Steps(sem("pre_act"), ["norm", "t0", "t1", "xh0", "xh1", "xh2", "xh3", "u0", "u1",
                                         "z0", "z1", "z2", "z3", "dt0", "dt1", "dt2", "dt3", "b0", "b1",
                                         "cast1", "spexp", "spln", "cast2", "cast3"])
        PRE_PE = Steps(sem("pre_pe"), ["t0", "t1", "xh0", "xh1", "xh2", "xh3", "z0", "z1", "z2", "z3",
                                       "dt0", "dt1", "dt2", "dt3", "b0", "b1"])
        POST_DVE = Steps(sem("post_dve"), ["yt0", "yt1", "yz0", "yz1", "res0", "res1", "stats", "aggr", "center",
                                           "mx", "lm", "sm", "pr", "eq", "ms", "oh", "oc", "rank",
                                           "base", "kept", "lost", "srow", "sidx", "grow", "gidx", "gw"])
        POST_POOL = Steps(sem("post_pool"), ["rstd", "nmr", "carry"] + [f"pre{k}" for k in range(KT)])
        POST_ACT = Steps(sem("post_act"), ["norm", "t0", "t1", "ex"])
        POST_PE = Steps(sem("post_pe"), ["out0", "out1", "t0", "t1", "logits", "cum"])
        m_exp, m_mul, m_scan, m_bc, m_sum = (sem(n) for n in ("m_exp", "m_mul", "m_scan", "m_bc", "m_sum"))
        NS = NH * N

        UE = CAP // 512
        UNITS = E * UE
        s_we = [sem(f"s_we{i}") for i in range(2)]
        s_xe = [sem(f"s_xe{i}") for i in range(2)]
        s_ye = [sem(f"s_ye{i}") for i in range(2)]
        e_T, e_xT, e_h, e_gelu, e_y, e_add = (sem(n) for n in ("e_T", "e_xT", "e_h", "e_gelu", "e_y", "e_add"))

        s_w3 = sem("s_w3")
        s_wk = sem("s_wk")
        s_gx = [sem(f"s_gx{i}") for i in range(2)]
        s_fin = sem("s_fin")
        A_JOBS = [f"t{i}" for i in range(4)] + [f"g{i}" for i in range(4)] + ["q0", "q1", "v0", "v1", "v2", "r0", "r1", "k0", "k1"]
        A_DVE = Steps(sem("a_dve"), ["x2", "stats", "aggr", "center"])
        A_POOL = Steps(sem("a_pool"), ["rstd", "nmr"])
        A_ACT = Steps(sem("a_act"), ["norm"] + A_JOBS)
        A_PE = Steps(sem("a_pe"), A_JOBS)
        T_DVE = Steps(sem("t_dve"), [f"qk{d}" for d in range(QH)] + ["s01", "s23", "s", "max", "sub", "den", "rden"] +
                      [f"{n}{l}" for l in range(BQ) for n in ("pv", "o")] + ["norm"])
        T_ACT = Steps(sem("t_act"), ["exp"])
        B_DVE = Steps(sem("b_dve"), ["x3", "stats", "aggr", "center"])
        B_POOL = Steps(sem("b_pool"), ["rstd", "nmr"])
        B_ACT = Steps(sem("b_act"), ["oT", "norm", "xT"])
        B_PE = Steps(sem("b_pe"), ["oT", "proj", "xT"])
        F_PE = Steps(sem("f_pe"), [f"{n}{k}" for k in range(KH) for n in ("g", "u")] + ["down"])
        F_ACT = Steps(sem("f_act"), [f"silu{k}" for k in range(KH)])
        F_DVE = Steps(sem("f_dve"), [f"h{k}" for k in range(KH)] + ["x4"])
        TU = B // BQ * TB

        def run_units(eng, unit, last):
            body = 2 * UE
            for k in range(body):
                unit(Group(k))
            with eng.Fori(0, UNITS // body - 2) as i:
                for k in range(body):
                    unit(Group(body + k, i, body))
            for k in range(UNITS - body, UNITS):
                unit(Group(k))
            last(Group(UNITS))

        def a_jobs(c):
            return [(i, n) for i, n in enumerate(A_JOBS) if (2 if i < 8 else 3) == c]

        def run_last(att, b1_, b2_, a_):
            for c in range(BQ):
                a_(0, c)
            for t in range(TU + 2):
                att_first, att_last = att
                if t < TU:
                    att_first(t)
                if 0 <= t - 1 < TU:
                    b1_(t - 1)
                if 0 <= t - 2 < TU:
                    b2_(t - 2, 0)
                if t < TU:
                    att_last(t)
                if 0 <= t - 2 < TU:
                    b2_(t - 2, 1)
                if t // BQ + 1 < TB:
                    a_(t // BQ + 1, t % BQ)

        NW = P["n_weights"]
        block = ctx.enter_context(nc.Block())

        def tiles(ap):
            return ap.rearrange("b (j p) d -> p (b j) d", p=128)

        JOBS = ([("POST", f"out{c}", c, POST_DVE, f"res{c}") for c in range(2)] +
                [("PRE", n, i % 2, PRE_ACT, n) for i, n in enumerate(["t0", "t1", "xh0", "xh1", "xh2", "xh3"])] +
                [("POST", f"t{c}", c, POST_ACT, f"t{c}") for c in range(2)] +
                [("PRE", f"z{i}", i % 2, PRE_ACT, f"z{i}") for i in range(4)] +
                [("POST", "logits", 0, POST_DVE, "lm")] +
                [("PRE", n, (i + 1) % 2, PRE_ACT, n) for i, n in enumerate(["dt0", "dt1", "dt2", "dt3", "b0"])] +
                [("POST", "cum", 1, POST_DVE, "oc"), ("PRE", "b1", 0, PRE_ACT, "b1")])
        JOB_AT = {(j[0], j[1]): i for i, j in enumerate(JOBS)}

        def bank(stage, name):
            return pJ[JOBS[JOB_AT[stage, name]][2]][:, :]

        def after(eng, period, stage, name):
            at = JOB_AT[stage, name]
            back = [(period, j) for j in JOBS[:at][::-1]] + [(period - 1, j) for j in JOBS[::-1]] + [(period - 2, j) for j in JOBS[::-1]]
            for p, j in back:
                q = p + 1 if j[0] == "PRE" else p - 1
                exists = q.off >= 0 and (p.reg is not None or q.off < G)
                if j[2] == JOBS[at][2] and exists:
                    eng.wait_ge(j[3].sem, j[3].upto(q, j[4]))
                    return

        def settle(eng):
            eng.sem_inc(s_passed, 1)

        def run_groups(eng, main, pre_aux, post_aux):
            def period(g):
                for n in range(N):
                    if main:
                        main(g, n)
                    if g.off > 0:
                        post_aux(g - 1, n)
                    if g.reg is not None or g.off + 1 < G:
                        pre_aux(g + 1, n)

            for n in range(N):
                pre_aux(Group(0), n)
            period(Group(0))
            period(Group(1))
            with eng.Fori(0, (G - 4) // 2) as pair:
                period(Group(2, pair))
                period(Group(3, pair))
            period(Group(G - 2))
            period(Group(G - 1))
            for n in range(N):
                post_aux(Group(G - 1), n)

        @block.sync
        def _(sp):
            sp.dma_start(xres[:, 0:KT, :], tiles(x)[:, 0:KT, :]).then_inc(s_x, 16)
            sp.dma_start(cols[:, :], P["cols"]).then_inc(s_w, 16)
            sp.dma_start(w_in[:, :], P["L0_attn_W_in"]).then_inc(s_w, 16)
            sp.dma_start(w_dt[:, :, :], P["L0_attn_W_dt"].rearrange("(k p) n -> p k n", p=128)).then_inc(s_w, 16)
            for c in range(3):
                sp.dma_start(w_b[:, :, 32 * c:32 * c + N],
                             P["L0_attn_W_x"][:, N:2 * N].rearrange("(k p) n -> p k n", p=128)).then_inc(s_w, 16)
                sp.dma_start(w_b[:, :, 32 * c + N:32 * c + 2 * N],
                             P["L0_attn_W_x"][:, N:2 * N].rearrange("(k p) n -> p k n", p=128)).then_inc(s_w, 16)
            sp.dma_start(w_out[:, :, :], P["L0_attn_W_out"].rearrange("(k p) n -> p k n", p=128)).then_inc(s_w, 16)
            sp.dma_start(b_out[:, :], P["L0_attn_b_out"].rearrange("(a n) -> a n", a=1)).then_inc(s_w, 16)
            sp.dma_start(rt_w[:, :], P["router_wT"]).then_inc(s_w, 16)
            with sp.Fori(1, G) as g:
                sp.wait_ge(s_x, 16 * g)
                sp.dma_start(xres[:, bass.ds(g * KT, KT), :], tiles(x)[:, bass.ds(g * KT, KT), :]).then_inc(s_x, 16)
            sp.wait_ge(s_zr, 1)
            for k in range(8):
                sp.dma_start(slots_in[k * (SLOTS // 8):(k + 1) * (SLOTS // 8), :].rearrange("(p r) d -> p (r d)", p=128),
                             zero).then_inc(s_zero, 16)
            sp.wait_ge(POST_DVE.sem, POST_DVE.upto(G - 1, "gw"))
            sp.wait_ge(s_scat, 16 * TILES)

            def weights(e):
                par = e.par
                if e.least(2):
                    sp.wait_ge(e_add, (e - 1) * UE)
                one = lambda n: P[n][bass.ds(e * 1, 1)]
                sp.dma_start(w1[par][:, :], one("L0_ffn_w1").rearrange("a d f -> d (a f)")).then_inc(s_we[par], 16)
                sp.dma_start(w2[par][:, :, :], one("L0_ffn_w2").rearrange("a (k p) d -> p (a k) d", p=128)).then_inc(s_we[par], 16)
                sp.dma_start(b1[par][:, :], one("b1T").rearrange("a p k -> p (a k)")).then_inc(s_we[par], 16)
                sp.dma_start(b2[par][:, :], one("L0_ffn_b2").to_broadcast([128, D])).then_inc(s_we[par], 16)

            def load(t):
                if t.least(2):
                    sp.wait_ge(e_T, (t - 2) * 1 + 1)
                sp.dma_start(xe[t.par][:, :, :], slots_in[bass.ds(t * 512, 512), :].rearrange("(k p) d -> p k d", p=128)
                             ).then_inc(s_xe[t.par], 16)

            def unit(t):
                if t.off % UE == 0:
                    weights(t // UE)
                load(t)
            load_w3 = [(wq, "w_qT"), (bq, "bq"), (wo, "w_outT"), (bo, "bo"), (wkr, "wkr"), (mask8, "mask8"), (gi, "w_gateT"), (ui, "w_upT")]
            for dst, name in load_w3:
                sp.dma_start(dst[:, :], P[name]).then_inc(s_w3, 16)
            sp.dma_start(di[:, :, :], P["w_downT"].rearrange("(k p) d -> p k d", p=128)).then_inc(s_w3, 16)
            run_units(sp, unit, lambda t: None)
            for t in range(TU):
                j, c = t // BQ, t % BQ
                sp.wait_ge(F_DVE.sem, F_DVE.upto(t, "x4"))
                src = xres[:, :, :].rearrange("p (b j) d -> p b j d", j=TB)[:, BQ * c:BQ * c + BQ, j, :]
                sp.dma_start(P["out"][BQ * c:BQ * c + BQ, 128 * j:128 * j + 128, :].rearrange("b p d -> p b d"), src).then_inc(s_out, 16)
            sp.wait_ge(s_out, 16 * TU)

        @block.gpsimd
        def _(pool):
            pool.memset(ident[:, :], 0.0)
            pool.memset(tri[:, :], 1.0)
            pool.memset(ones[:, :], 1.0)
            pool.memset(halfs[:, :], -0.5)
            pool.memset(sel[:, :, :], 0.0)
            pool.memset(pre[:, :, :], 0.0)
            for h in range(NH):
                pool.memset(xhp[:, h, :, 0:PAD], 0.0)
            for b in range(NB):
                pool.memset(dA[b][:, :, 0:1], 0.0)
            pool.iota(w8[:, :], pattern=[[-1, E]], base=E, channel_multiplier=0,
                      allow_small_or_imprecise_dtypes=True).then_inc(s_cst, 1)
            pool.memset(zero, 0.0).then_inc(s_zr, 1)
            pool.wait_ge(s_cst, 1)
            pool.affine_select(out=ident[:, :], in_=ident[:, :], compare_op=ALU.not_equal, fill=1.0,
                               base=0, pattern=[[-1, 128]], channel_multiplier=1)
            pool.affine_select(out=tri[:, :], in_=tri[:, :], compare_op=ALU.is_ge, fill=0.0,
                               base=0, pattern=[[1, 128]], channel_multiplier=-1)
            for c in range(3):
                if c:
                    pool.wait_ge(s_sel, c)
                last = pool.affine_select(out=sel[:, :, :], in_=sel[:, :, :], compare_op=ALU.not_equal, fill=1.0,
                                          base=-32 * c, pattern=[[-1, N], [0, 128]], channel_multiplier=1)
                last.then_inc(s_sel, 1)

            def pre_aux(q, slot):
                if slot == 0:
                    pool.wait_ge(PRE_DVE.sem, PRE_DVE.upto(q, "center"))
                    pool.tensor_tensor(rstd[:, :], veps[:, :], half, ALU.pow).then_inc(PRE_POOL.sem, 1)
                    pool.wait_ge(PRE_POOL.sem, PRE_POOL.upto(q, "rstd"))
                    pool.tensor_tensor(nmr[:, :], nmean[:, :], rstd[:, :], ALU.mult).then_inc(PRE_POOL.sem, 1)
                if slot == 13:
                    pool.wait_ge(PRE_ACT.sem, PRE_ACT.upto(q, "cast1"))
                    pool.tensor_tensor(Br[:, :], Bf[:, :], Bs[q.par][:, :], ALU.subtract).then_inc(PRE_POOL.sem, 1)
                if slot == 14:
                    pool.wait_ge(PRE_ACT.sem, PRE_ACT.upto(q, "cast2"))
                    pool.tensor_tensor(Br[:, :], Br[:, :], Bs[q.par][:, :], ALU.subtract).then_inc(PRE_POOL.sem, 1)

            def post_aux(q, slot):
                if slot == 3:
                    pool.wait_ge(POST_DVE.sem, POST_DVE.upto(q, "center"))
                    pool.tensor_tensor(rstd2[:, :], veps2[:, :], half, ALU.pow).then_inc(POST_POOL.sem, 1)
                    pool.wait_ge(POST_POOL.sem, POST_POOL.upto(q, "rstd"))
                    pool.tensor_tensor(nmr2[:, :], nmean2[:, :], rstd2[:, :], ALU.mult).then_inc(POST_POOL.sem, 1)
                if slot == 10:
                    pool.wait_ge(POST_DVE.sem, POST_DVE.upto(q, "oh"))
                    if q.least(1):
                        pool.wait_ge(POST_PE.sem, POST_PE.upto(q - 1, "cum"))
                        pool.wait_ge(POST_POOL.sem, POST_POOL.upto(q - 1, f"pre{KT - 1}"))
                    settle(pool)
                    pool.tensor_copy(pre[:, 0, :], pre[:, KT, :]).then_inc(POST_POOL.sem, 1)
                    for k in range(KT):
                        pool.wait_ge(POST_POOL.sem, POST_POOL.upto(q, f"pre{k - 1}" if k else "carry"))
                        pool.tensor_tensor(pre[:, k + 1, :], pre[:, k, :], oh[:, k, :], ALU.add).then_inc(POST_POOL.sem, 1)
                if slot == 12:
                    if not q.least(1):
                        pool.wait_ge(s_zero, 16 * 8)
                    pool.wait_ge(POST_ACT.sem, POST_ACT.upto(q, "norm"))
                    pool.wait_ge(POST_DVE.sem, POST_DVE.upto(q, "sidx"))
                    settle(pool)
                    for k in range(KT):
                        pool.indirect_dma_start(out=slots_in, out_offset=bass.IndirectOffsetOnAxis(ap=sidx[:, k:k + 1], axis=0),
                                                in_=xn2[:, k, :], in_offset=None,
                                                bounds_check=SLOTS - 1, oob_is_err=False).then_inc(s_scat, 16)
            run_groups(pool, None, pre_aux, post_aux)

            def unit(t):
                if t.least(1):
                    store(t - 1)

            def store(t):
                pool.wait_ge(e_add, (t + 1) * 1)
                settle(pool)
                pool.dma_start(slots_out[bass.ds(t * 512, 512), :].rearrange("(k p) d -> p k d", p=128),
                               ye[t.par][:, :, :]).then_inc(s_ye[t.par], 16)
            run_units(pool, unit, lambda t: store(t - 1))

            pool.wait_ge(s_ye[0], 16 * (UNITS // 2))
            pool.wait_ge(s_ye[1], 16 * (UNITS // 2))

            def blk(j, c):
                if c == 0:
                    if j >= 1:
                        pool.wait_ge(A_DVE.sem, A_DVE.upto(j - 1, "x2"))
                    for l in range(B):
                        pool.indirect_dma_start(out=gx[:, l, :], out_offset=None, in_=slots_out,
                                                in_offset=bass.IndirectOffsetOnAxis(ap=gidx[:, TB * l + j:TB * l + j + 1], axis=0),
                                                bounds_check=SLOTS - 1, oob_is_err=False).then_inc(s_gx[j % 2], 16)
                if c == 1:
                    pool.wait_ge(A_DVE.sem, A_DVE.upto(j, "center"))
                    pool.tensor_tensor(rsA[:, :], veA[:, :], halfs[:, :], ALU.pow).then_inc(A_POOL.sem, 1)
                    pool.wait_ge(A_POOL.sem, A_POOL.upto(j, "rstd"))
                    pool.tensor_tensor(nrA[:, :], nmA[:, :], rsA[:, :], ALU.mult).then_inc(A_POOL.sem, 1)

            def norm_b(t):
                pool.wait_ge(B_DVE.sem, B_DVE.upto(t, "center"))
                pool.tensor_tensor(rsB[:, :], veB[:, :], halfs[:, 0:BQ], ALU.pow).then_inc(B_POOL.sem, 1)
                pool.wait_ge(B_POOL.sem, B_POOL.upto(t, "rstd"))
                pool.tensor_tensor(nrB[:, :], nmB[:, :], rsB[:, :], ALU.mult).then_inc(B_POOL.sem, 1)
            run_last((lambda t: None, lambda t: None), norm_b, lambda t, part: None, blk)

        @block.scalar
        def _(act):
            act.wait_ge(s_w, 16 * NW)
            act.activation(A[:, :], c_alog, ACT.Exp).then_inc(s_A, 1)
            act.wait_ge(s_A, 1)
            act.mul(A[:, :], A[:, :], -1.0)
            for h in range(NH):
                last = act.mul(tapb[:, h:h + 1], c_bin(h), c_cw(h, TAPS - 1))
            last.then_inc(s_A, 1)
            act.wait_ge(s_A, 2)
            act.wait_ge(s_cst, 1)

            def main(g, n):
                for h in range(NH):
                    s = NH * n + h
                    if s == 0:
                        act.wait_ge(PRE_DVE.sem, PRE_DVE.upto(g, "delta"))
                    if g.least(1) or s >= NB:
                        act.wait_ge(m_scan, g * NS + s - NB + 1)
                    act.activation(dA[s % NB][:, :, 1:L], dl[g.par][:, h, :].rearrange("p (b t) -> p b t", b=SEQ)[:, :, 1:L],
                                   ACT.Exp, scale=A[:, N * h + n:N * h + n + 1]).then_inc(m_exp, 1)

            def pre_aux(q, slot):
                par = q.par
                done = lambda i: i.then_inc(PRE_ACT.sem, 1)
                if slot == 1:
                    act.wait_ge(PRE_POOL.sem, PRE_POOL.upto(q, "nmr"))
                    for k in range(KT):
                        last = act.activation(xn[:, k, :], xres[:, bass.ds(q * KT + k, 1), :], ACT.Identity,
                                              bias=nmr[:, k:k + 1], scale=rstd[:, k:k + 1])
                    done(last)
                if slot == 3:
                    for c in range(2):
                        act.wait_ge(PRE_PE.sem, PRE_PE.upto(q, f"t{c}"))
                        done(act.copy(xnT[:, c * 512:(c + 1) * 512], bank("PRE", f"t{c}")))
                if slot in (4, 5):
                    for j in (2 * slot - 8, 2 * slot - 7):
                        h, c = j // 2, j % 2
                        act.wait_ge(PRE_PE.sem, PRE_PE.upto(q, f"xh{j}"))
                        act.activation(xhp[:, h, c, PAD:PAD + L], bank("PRE", f"xh{j}"), ACT.Identity, bias=c_bin(h))
                        done(act.activation(acc[:, h, c, :], bank("PRE", f"xh{j}"), ACT.Identity, bias=tapb[:, h:h + 1],
                                            scale=c_cw(h, TAPS - 1)))
                if slot == 7:
                    act.wait_ge(PRE_DVE.sem, PRE_DVE.upto(q, f"conv{NH - 1}_{TAPS - 2}"))
                    if q.least(2):
                        act.wait_ge(POST_DVE.sem, POST_DVE.upto(q - 2, "yz1"))
                    for h in range(NH):
                        done(act.activation(u[par][:, h, :].rearrange("p (b t) -> p b t", b=SEQ), acc[:, h, :, :],
                                            ACT.Silu, bias=c_cb(h)))
                if slot in (7, 8):
                    for j in (2 * slot - 14, 2 * slot - 13):
                        h, c = j // 2, j % 2
                        act.wait_ge(PRE_PE.sem, PRE_PE.upto(q, f"z{j}"))
                        done(act.activation(zs[par][:, h, c * 512:(c + 1) * 512], bank("PRE", f"z{j}"), ACT.Silu, bias=c_bin(2 + h)))
                if slot == 9:
                    if q.least(2):
                        act.wait_ge(m_mul, (q - 1) * NS)
                if slot in (9, 10, 11):
                    for j in {9: (0,), 10: (1, 2), 11: (3,)}[slot]:
                        h, c = j // 2, j % 2
                        act.wait_ge(PRE_PE.sem, PRE_PE.upto(q, f"dt{j}"))
                        act.activation(dl[par][:, h, c * 512:(c + 1) * 512], bank("PRE", f"dt{j}"), ACT.Abs, bias=c_bdt(h))
                        done(act.activation(wu[par][:, h, c * 512:(c + 1) * 512], bank("PRE", f"dt{j}"), ACT.Relu, bias=c_bdt(h)))
                if slot in (11, 12):
                    for c in (slot - 11,):
                        act.wait_ge(PRE_PE.sem, PRE_PE.upto(q, f"b{c}"))
                        done(act.activation(Bf[:, c * 512:(c + 1) * 512], bank("PRE", f"b{c}")[0:96, :], ACT.Identity, bias=c_bx[0:96]))
                if slot == 12:
                    act.wait_ge(PRE_ACT.sem, PRE_ACT.upto(q, "b1"))
                    if q.least(2):
                        act.wait_ge(m_bc, (q - 1) * N)
                    done(act.copy(Bs[par][:, :], Bf[:, :]))
                    done(act.activation(dl[par][:, :, :], dl[par][:, :, :], ACT.Exp, scale=-1.0))
                    act.wait_ge(PRE_ACT.sem, PRE_ACT.upto(q, "spexp"))
                    done(act.activation(dl[par][:, :, :], dl[par][:, :, :], ACT.Ln, bias=1.0))
                if slot == 13:
                    act.wait_ge(PRE_POOL.sem, PRE_POOL.upto(q, "part2"))
                    for c in range(1, 3):
                        last = act.copy(Bs[par][32 * c:32 * c + 32, :], Br[32 * c:32 * c + 32, :])
                    done(last)
                if slot == 14:
                    act.wait_ge(PRE_POOL.sem, PRE_POOL.upto(q, "part3"))
                    done(act.copy(Bs[par][64:96, :], Br[64:96, :]))

            def post_aux(q, slot):
                done = lambda i: i.then_inc(POST_ACT.sem, 1)
                if slot == 4:
                    act.wait_ge(POST_POOL.sem, POST_POOL.upto(q, "nmr"))
                    if q.least(1):
                        act.wait_ge(s_scat, 16 * KT * q)
                    for k in range(KT):
                        last = act.activation(xn2[:, k, :], xres[:, bass.ds(q * KT + k, 1), :], ACT.Identity,
                                              bias=nmr2[:, k:k + 1], scale=rstd2[:, k:k + 1])
                    done(last)
                if slot == 6:
                    for c in range(2):
                        act.wait_ge(POST_PE.sem, POST_PE.upto(q, f"t{c}"))
                        done(act.copy(xn2T[:, c * 512:(c + 1) * 512], bank("POST", f"t{c}")))
                if slot == 9:
                    act.wait_ge(POST_DVE.sem, POST_DVE.upto(q, "lm"))
                    done(act.activation(ex[:, :, :], lm[:, :, :], ACT.Exp))
            run_groups(act, main, pre_aux, post_aux)

            def unit(t):
                if t.off % UE == 0:
                    act.wait_ge(s_we[(t // UE).par], (t // UE // 2 + 1) * 64)
                if t.least(2):
                    act.wait_ge(e_y, (t - 1) * 1)
                for k in range(KF):
                    act.wait_ge(e_h, t * KF + k + 1)
                    act.activation(he[t.par][:, k, :], pH[k][:, :], ACT.Gelu,
                                   bias=b1[(t // UE).par][:, k:k + 1]).then_inc(e_gelu, 1)
            run_units(act, unit, lambda t: None)

            def blk(j, c):
                done = lambda i: i.then_inc(A_ACT.sem, 1)
                if c == 1:
                    act.wait_ge(A_POOL.sem, A_POOL.upto(j, "nmr"))
                    for l in range(B):
                        last = act.activation(xnA[:, l, :], xres[:, TB * l + j, :], ACT.Identity,
                                              bias=nrA[:, l:l + 1], scale=rsA[:, l:l + 1])
                    done(last)
                out = {}
                for i in range(4):
                    out[f"t{i}"] = (xnAT[:, 4 * i:4 * i + 4, :].rearrange("p l b -> p (l b)"), 1.0, 512)
                    out[f"g{i}"] = (xnG[:, 4 * i:4 * i + 4, :].rearrange("p l b -> p (l b)"), 1.0, 512)
                for i in range(2):
                    out[f"q{i}"] = (q[j % 2][:, 8 * i:8 * i + 8, :].rearrange("p l c -> p (l c)"), 1.0, 512)
                    out[f"r{i}"] = (qG[:, 4 * i:4 * i + 4, :].rearrange("p g b -> p (g b)"), 1.0, 512)
                    out[f"k{i}"] = (kk[j % 2][:, :, :].rearrange("p (c g) s -> p g c s", c=C8)[:, 4 * i:4 * i + 4, :, :],
                                     float(DV) ** -0.5, 32 * SL)
                for i in range(3):
                    n = min(7 * C8, D - 7 * C8 * i)
                    out[f"v{i}"] = (vv[j % 2][:, 7 * C8 * i:7 * C8 * i + n, :].rearrange("p c s -> p (c s)"), 1.0, n * SL)
                for i, name in a_jobs(c):
                    act.wait_ge(A_PE.sem, A_PE.upto(j, name))
                    dst, scale, n = out[name]
                    if name == "q0" and j >= 2:
                        act.wait_ge(T_DVE.sem, T_DVE.upto(BQ * (j - 1) - 1, "norm"))
                    src = pA[i % 2][:, 0:n]
                    if name[0] == "k":
                        src = src.rearrange("p (g c s) -> p g c s", c=C8, s=SL)
                    done(act.activation(dst, src, ACT.Copy, scale=scale))

            def att_first(t):
                act.wait_ge(T_DVE.sem, T_DVE.upto(t, "sub"))
                act.activation(at[t % 2][:, :, :], at[t % 2][:, :, :], ACT.Exp).then_inc(T_ACT.sem, 1)

            def proj(t):
                done = lambda i: i.then_inc(B_ACT.sem, 1)
                act.wait_ge(B_PE.sem, B_PE.upto(t, "oT"))
                done(act.copy(oT[:, :], pS1[:, :]))
                act.wait_ge(B_POOL.sem, B_POOL.upto(t, "nmr"))
                for i in range(BQ):
                    l = TB * (BQ * (t % BQ) + i) + t // BQ
                    last = act.activation(xnB[:, i, :], xres[:, l, :], ACT.Identity, bias=nrB[:, i:i + 1], scale=rsB[:, i:i + 1])
                done(last)
                act.wait_ge(B_PE.sem, B_PE.upto(t, "xT"))
                done(act.copy(xnBT[t % 2][:, :], pS1[:, :]))

            def gated(t, part):
                if part == 0:
                    for k in range(KH):
                        n = KH * t + k
                        act.wait_ge(F_PE.sem, F_PE.upto(t, f"g{k}"))
                        if n >= 2:
                            act.wait_ge(F_DVE.sem, F_DVE.upto(t - (k < 2), f"h{(k - 2) % KH}"))
                        act.activation(sg[n % 2][:, :], pG[n % 2][:, :], ACT.Silu).then_inc(F_ACT.sem, 1)
            run_last((att_first, lambda t: None), proj, gated, blk)

        @block.vector
        def _(dve):
            def stats(src, st, m, ve, nm, S, q):
                done = lambda i: i.then_inc(S.sem, 1)
                settle(dve)
                for k in range(KT):
                    last = dve.bn_stats(st[:, k, :], src(k))
                done(last)
                dve.wait_ge(S.sem, S.upto(q, "stats"))
                settle(dve)
                for k in range(KT):
                    last = dve.bn_aggr(m[:, k, :], st[:, k, :])
                done(last)
                dve.wait_ge(S.sem, S.upto(q, "aggr"))
                dve.tensor_scalar(ve[:, :], m[:, :, 1], EPS, None, ALU.add)
                done(dve.tensor_scalar(nm[:, :], m[:, :, 0], -1.0, None, ALU.mult))

            def main(g, n):
                par = g.par
                dve.wait_ge(m_bc, g * N + n + 1)
                if n == 0:
                    dve.wait_ge(PRE_DVE.sem, PRE_DVE.upto(g, "w"))
                for h in range(NH):
                    if g.least(1) or n:
                        dve.wait_ge(m_scan, g * NS + NH * (n - 1) + h + 1)
                    dve.tensor_tensor(dB[h][:, :], wu[par][:, h, :], pB[:, :], ALU.mult).then_inc(m_mul, 1)
                for h in range(NH):
                    s = NH * n + h
                    dve.wait_ge(m_exp, g * NS + s + 1)
                    dve.wait_ge(m_mul, g * NS + s + 1)
                    if g.least(1) or s >= NB:
                        dve.wait_ge(m_sum, g * NS + s - NB + 1)
                    dve.tensor_tensor_scan(hs[s % NB][:, :], dA[s % NB][:, :, :].rearrange("p b t -> p (b t)"), dB[h][:, :], 0.0,
                                           ALU.mult, ALU.add).then_inc(m_scan, 1)

            def pre_aux(q, slot):
                par = q.par
                done = lambda i: i.then_inc(PRE_DVE.sem, 1)
                if slot == 0:
                    dve.wait_ge(s_x, 16 * (q + 1))
                    stats(lambda k: xres[:, bass.ds(q * KT + k, 1), :], stat, mv, veps, nmean, PRE_DVE, q)
                if slot in (5, 6):
                    h = slot - 5
                    dve.wait_ge(PRE_ACT.sem, PRE_ACT.upto(q, f"xh{2 * h + 1}"))
                    for k in range(TAPS - 1):
                        if k:
                            dve.wait_ge(PRE_DVE.sem, PRE_DVE.upto(q, f"conv{h}_{k - 1}"))
                        done(dve.scalar_tensor_tensor(out=acc[:, h, :, :], in0=xhp[:, h, :, k:k + L], scalar=c_cw(h, k),
                                                      in1=acc[:, h, :, :], op0=ALU.mult, op1=ALU.add))
                if slot == 13:
                    dve.wait_ge(PRE_ACT.sem, PRE_ACT.upto(q, "spln"))
                    done(dve.tensor_tensor(dl[par][:, :, :], dl[par][:, :, :], wu[par][:, :, :], ALU.add))
                    dve.wait_ge(PRE_DVE.sem, PRE_DVE.upto(q, "delta"))
                    done(dve.tensor_tensor(wu[par][:, :, :], dl[par][:, :, :], u[par][:, :, :], ALU.mult))

            def post_aux(q, slot):
                par = q.par
                done = lambda i: i.then_inc(POST_DVE.sem, 1)
                own = lambda name: dve.wait_ge(POST_DVE.sem, POST_DVE.upto(q, name))
                row = slice(None)
                here = bass.ds(q * KT, KT)
                if slot == 0:
                    dve.wait_ge(m_sum, (q + 1) * NS)
                    if not q.least(1):
                        dve.wait_ge(s_zero, 16 * 8)
                    if q.least(1):
                        dve.wait_ge(POST_PE.sem, POST_PE.upto(q - 1, "out1"))
                    for h in range(NH):
                        done(dve.scalar_tensor_tensor(out=yz[:, h, :], in0=u[par][:, h, :], scalar=c_D(h), in1=pY[h][:, :],
                                                      op0=ALU.mult, op1=ALU.add))
                    for h in range(NH):
                        own(f"yt{h}")
                        done(dve.tensor_tensor(yz[:, h, :], yz[:, h, :], zs[par][:, h, :], ALU.mult))
                if slot == 2:
                    for c in range(2):
                        dve.wait_ge(POST_PE.sem, POST_PE.upto(q, f"out{c}"))
                        xs = xres[:, bass.ds(q * KT + 4 * c, 4), :]
                        done(dve.tensor_tensor(xs, xs, bank("POST", f"out{c}").rearrange("p (k d) -> p k d", d=D), ALU.add))
                if slot == 3:
                    own("res1")
                    stats(lambda k: xres[:, bass.ds(q * KT + k, 1), :], stat2, mv2, veps2, nmean2, POST_DVE, q)
                by_expert = lambda name: bank("POST", name)[:, 0:KT * E].rearrange("p (k e) -> p k e", e=E)
                bc = lambda t: t[:, :].unsqueeze(2).to_broadcast([128, KT, E])
                if slot == 9:
                    pL = by_expert("logits")
                    dve.wait_ge(POST_PE.sem, POST_PE.upto(q, "logits"))
                    done(dve.tensor_reduce(mx[:, :], pL, AX.X, ALU.max))
                    own("mx")
                    done(dve.tensor_tensor(lm[:, :, :], pL, bc(mx), ALU.subtract))
                if slot == 10:
                    dve.wait_ge(POST_ACT.sem, POST_ACT.upto(q, "ex"))
                    done(dve.tensor_reduce(sm[:, :], ex[:, :, :], AX.X, ALU.add))
                    own("sm")
                    done(dve.reciprocal(pr[:, :], sm[:, :]))
                    own("lm")
                    done(dve.scalar_tensor_tensor(out=sc[:, :, :], in0=ex[:, :, :], scalar=1.0,
                                                  in1=w8[:, :].unsqueeze(1).to_broadcast([128, KT, E]),
                                                  op0=ALU.is_ge, op1=ALU.mult))
                    own("eq")
                    done(dve.tensor_reduce(ms[:, :], sc[:, :, :], AX.X, ALU.max))
                    own("ms")
                    done(dve.tensor_tensor(oh[:, :, :], sc[:, :, :], bc(ms), ALU.is_equal))
                if slot == 12:
                    dve.wait_ge(POST_PE.sem, POST_PE.upto(q, "cum"))
                    done(dve.tensor_tensor(oc[:, :, :], oh[:, :, :], by_expert("cum"), ALU.mult))
                    own("oc")
                    done(dve.tensor_reduce(rank[:, :], oc[:, :, :], AX.X, ALU.add))
                    done(dve.tensor_scalar(base[:, :], ms[:, :], float(-CAP), float(E * CAP - 1), ALU.mult, ALU.add))
                    own("base")
                    done(dve.tensor_scalar(kept[:, :], rank[:, :], float(CAP), None, ALU.is_le))
                    done(dve.tensor_scalar(lost[:, :], rank[:, :], float(CAP), float(SLOTS), ALU.is_gt, ALU.mult))
                    done(dve.tensor_tensor(srow[:, :], base[:, :], rank[:, :], ALU.add))
                    own("srow")
                    if q.least(1):
                        dve.wait_ge(s_scat, 16 * KT * q)
                    done(dve.tensor_tensor(sidx[:, :], srow[:, :], lost[:, :], ALU.add))
                    done(dve.scalar_tensor_tensor(out=grow[:, :], in0=rank[:, :], scalar=float(CAP), in1=base[:, :],
                                                  op0=ALU.min, op1=ALU.add))
                    own("grow")
                    done(dve.tensor_copy(gidx[:, here], grow[:, :]))
                    done(dve.tensor_tensor(gwt[:, here], pr[:, :], kept[:, :], ALU.mult))
            dve.wait_ge(s_w, 16 * NW)
            dve.wait_ge(s_cst, 1)
            run_groups(dve, main, pre_aux, post_aux)

            def unit(t):
                if not t.least(1):
                    rows_in(t)
                rows_in(t + 1)
                if t.least(1):
                    rows_out(t - 1)

            def rows_in(t):
                dve.wait_ge(e_T, (t + 1) * 1)
                if t.least(2):
                    dve.wait_ge(e_h, (t - 1) * KF)
                dve.tensor_copy(xeT[t.par][:, :], pT[t.par][:, :]).then_inc(e_xT, 1)

            def rows_out(t):
                dve.wait_ge(e_y, (t + 1) * 1)
                if t.least(2):
                    dve.wait_ge(s_ye[t.par], t // 2 * 16)
                dve.tensor_tensor(ye[t.par][:, :, :], pE[t.par][:, :].rearrange("p (k d) -> p k d", d=D),
                                  b2[(t // UE).par][:, :].unsqueeze(1).to_broadcast([128, 4, D]), ALU.add).then_inc(e_add, 1)

            def unit_last(t):
                if t.least(UNITS - 1) and t.reg is None:
                    rows_out(t - 1)
                else:
                    unit(t)
            run_units(dve, unit_last, lambda t: rows_out(t - 1))

            dve.wait_ge(s_w3, 16 * 9)
            dve.tensor_scalar(wg[:, :], gi[:, :], 1.0 / 127.0, None, ALU.mult)
            dve.tensor_scalar(wup[:, :], ui[:, :], 1.0 / 127.0, None, ALU.mult)
            dve.tensor_scalar(wd[:, :, :], di[:, :, :], 1.0 / 127.0, None, ALU.mult)
            dve.tensor_tensor(wk[:, :, :], mask8[:, :].unsqueeze(2).to_broadcast([128, C8, SL]),
                              wkr[:, :].unsqueeze(1).to_broadcast([128, C8, SL]), ALU.mult).then_inc(s_wk, 1)

            def block_stats(S, j, n, tile, st, m, ve, nm):
                done = lambda i: i.then_inc(S.sem, 1)
                for i in range(n):
                    last = dve.bn_stats(st[:, i, :], xres[:, tile(i), :])
                done(last)
                dve.wait_ge(S.sem, S.upto(j, "stats"))
                for i in range(n):
                    last = dve.bn_aggr(m[:, i, :], st[:, i, :])
                done(last)
                dve.wait_ge(S.sem, S.upto(j, "aggr"))
                dve.tensor_scalar(ve[:, :], m[:, :, 1], EPS, None, ALU.add)
                done(dve.tensor_scalar(nm[:, :], m[:, :, 0], -1.0, None, ALU.mult))

            def blk(j, c):
                if c == 1:
                    dve.wait_ge(s_gx[j % 2], 16 * B * (j // 2 + 1))
                    for l in range(B):
                        at_ = TB * l + j
                        last = dve.scalar_tensor_tensor(out=xres[:, at_, :], in0=gx[:, l, :], scalar=gwt[:, at_:at_ + 1],
                                                        in1=xres[:, at_, :], op0=ALU.mult, op1=ALU.add)
                    last.then_inc(A_DVE.sem, 1)
                    dve.wait_ge(A_DVE.sem, A_DVE.upto(j, "x2"))
                    if j >= 1:
                        dve.wait_ge(A_POOL.sem, A_POOL.upto(j - 1, "nmr"))
                    block_stats(A_DVE, j, B, lambda i: TB * i + j, stA, mvA, veA, nmA)

            def att_first(t):
                j, c = t // BQ, t % BQ
                done = lambda i: i.then_inc(T_DVE.sem, 1)
                own = lambda n: dve.wait_ge(T_DVE.sem, T_DVE.upto(t, n))
                dve.wait_ge(A_ACT.sem, A_ACT.upto(j, "k1"))
                if t >= 1:
                    dve.wait_ge(T_DVE.sem, T_DVE.upto(t - 1, "norm"))
                for d in range(QH):
                    qd = q[j % 2][:, BQ * c:BQ * c + BQ, :].rearrange("p l (h d) -> p l h d", d=QH)[:, :, :, d]
                    kd = kk[j % 2][:, HEADS * d:HEADS * d + HEADS, :]
                    done(dve.tensor_tensor(qk[d][:, :, :, :], qd.unsqueeze(3).to_broadcast([128, BQ, HEADS, SL]),
                                           kd.unsqueeze(1).to_broadcast([128, BQ, HEADS, SL]), ALU.mult))
                flat = lambda x_: x_[:, :, :, :].rearrange("p l h s -> p (l h s)")
                own("qk1")
                done(dve.tensor_tensor(flat(qk[0]), flat(qk[0]), flat(qk[1]), ALU.add))
                own("qk3")
                done(dve.tensor_tensor(flat(qk[2]), flat(qk[2]), flat(qk[3]), ALU.add))
                own("s23")
                done(dve.tensor_tensor(flat(qk[0]), flat(qk[0]), flat(qk[2]), ALU.add))
                own("s")
                s_ = qk[0][:, :, :, :].rearrange("p l h s -> p (l h) s")
                done(dve.tensor_reduce(am[:, :], s_, AX.X, ALU.max))
                own("max")
                done(dve.tensor_tensor(at[t % 2][:, :, :], s_, am[:, :].unsqueeze(2).to_broadcast([128, BQ * HEADS, SL]), ALU.subtract))

            def att_last(t):
                j = t // BQ
                done = lambda i: i.then_inc(T_DVE.sem, 1)
                own = lambda n: dve.wait_ge(T_DVE.sem, T_DVE.upto(t, n))
                a = at[t % 2]
                dve.wait_ge(T_ACT.sem, T_ACT.upto(t, "exp"))
                done(dve.tensor_reduce(ad[:, :], a[:, :, :], AX.X, ALU.add))
                own("den")
                done(dve.reciprocal(ar[:, :], ad[:, :]))
                for l in range(BQ):
                    if l >= 2:
                        own(f"o{l - 2}")
                    done(dve.tensor_tensor(pv[l % 2][:, :, :, :],
                                           a[:, HEADS * l:HEADS * l + HEADS, :].unsqueeze(2).to_broadcast([128, HEADS, DV, SL]),
                                           vv[j % 2][:, :, :].rearrange("p (h v) s -> p h v s", h=HEADS), ALU.mult))
                    own(f"pv{l}")
                    done(dve.tensor_reduce(oo[t % 2][:, l, :].rearrange("p (v h) -> p h v", h=HEADS), pv[l % 2][:, :, :, :], AX.X, ALU.add))
                own(f"o{BQ - 1}")
                own("rden")
                if t >= 2:
                    dve.wait_ge(B_PE.sem, B_PE.upto(t - 2, "oT"))
                done(dve.tensor_tensor(on[t % 2][:, :, :].rearrange("p l (v h) -> p l v h", h=HEADS),
                                       oo[t % 2][:, :, :].rearrange("p l (v h) -> p l v h", h=HEADS),
                                       ar[:, :].rearrange("p (l h) -> p l h", h=HEADS).unsqueeze(2).to_broadcast([128, BQ, DV, HEADS]), ALU.mult))

            def tiles_of(t):
                j, c = t // BQ, t % BQ
                return xres[:, :, :].rearrange("p (b j) d -> p b j d", j=TB)[:, BQ * c:BQ * c + BQ, j, :]

            def proj(t):
                dve.wait_ge(B_PE.sem, B_PE.upto(t, "proj"))
                dve.tensor_tensor(tiles_of(t), tiles_of(t), pS2[:, :].rearrange("p (l d) -> p l d", d=D), ALU.add).then_inc(B_DVE.sem, 1)
                dve.wait_ge(B_DVE.sem, B_DVE.upto(t, "x3"))
                if t >= 1:
                    dve.wait_ge(B_POOL.sem, B_POOL.upto(t - 1, "nmr"))
                block_stats(B_DVE, t, BQ, lambda i: TB * (BQ * (t % BQ) + i) + t // BQ, stB, mvB, veB, nmB)

            def gated(t, part):
                if part == 0:
                    for k in range(KH):
                        n = KH * t + k
                        dve.wait_ge(F_ACT.sem, F_ACT.upto(t, f"silu{k}"))
                        dve.wait_ge(F_PE.sem, F_PE.upto(t, f"u{k}"))
                        if k == 0 and t >= 1:
                            dve.wait_ge(F_PE.sem, F_PE.upto(t - 1, "down"))
                        dve.tensor_tensor(hh[:, k, :], sg[n % 2][:, :], pU[n % 2][:, :], ALU.mult).then_inc(F_DVE.sem, 1)
                else:
                    dve.wait_ge(F_PE.sem, F_PE.upto(t, "down"))
                    dve.tensor_tensor(tiles_of(t), tiles_of(t), pS2[:, :].rearrange("p (l d) -> p l d", d=D), ALU.add).then_inc(F_DVE.sem, 1)
            run_last((att_first, att_last), proj, gated, blk)

        @block.tensor
        def _(pe):
            pe.wait_ge(s_w, 16 * NW)
            pe.wait_ge(s_sel, 3)

            def bcast(g, n):
                if g.least(1) or n:
                    pe.wait_ge(m_mul, g * NS + NH * n)
                if n == 0:
                    pe.wait_ge(PRE_ACT.sem, PRE_ACT.upto(g, "cast3"))
                for c in range(2):
                    last = pe.matmul(pB[:, c * 512:(c + 1) * 512], sel[:, n, :], Bs[g.par][:, c * 512:(c + 1) * 512],
                                     start=True, stop=True)
                last.then_inc(m_bc, 1)

            def main(g, n):
                if n == 0:
                    bcast(g, 0)
                if n + 1 < N:
                    bcast(g, n + 1)
                if n == 0 and g.least(1):
                    pe.wait_ge(POST_DVE.sem, POST_DVE.upto(g - 1, "yt1"))
                for h in range(NH):
                    s = NH * n + h
                    pe.wait_ge(m_scan, g * NS + s + 1)
                    for c in range(2):
                        last = pe.matmul(pY[h][:, c * 512:(c + 1) * 512], ident[:, :], hs[s % NB][:, c * 512:(c + 1) * 512],
                                         start=(n == 0), stop=(n == N - 1))
                    last.then_inc(m_sum, 1)

            def job(q, stage, name, emit):
                after(pe, q - 1 if stage == "PRE" else q + 1, stage, name)
                emit(bank(stage, name)).then_inc((PRE_PE if stage == "PRE" else POST_PE).sem, 1)

            def transposed(src, c):
                def emit(out):
                    for k in range(4):
                        last = pe.transpose(out[:, k * 128:(k + 1) * 128], src[:, 4 * c + k, :], ident[:, :])
                    return last
                return emit

            def projected(w, src, c, rows=128):
                def emit(out):
                    for k in range(len(w)):
                        last = pe.matmul(out[0:rows, :], w[k], src[k][:, c * 512:(c + 1) * 512],
                                         start=(k == 0), stop=(k == len(w) - 1))
                    return last
                return emit

            def pre_aux(q, slot):
                us = [u[q.par][:, k, :] for k in range(NH)]
                if slot == 2:
                    pe.wait_ge(PRE_ACT.sem, PRE_ACT.upto(q, "norm"))
                    for c in range(2):
                        job(q, "PRE", f"t{c}", transposed(xn, c))
                if slot in (3, 4):
                    if slot == 3:
                        pe.wait_ge(PRE_ACT.sem, PRE_ACT.upto(q, "t1"))
                    h = slot - 3
                    for c in range(2):
                        job(q, "PRE", f"xh{2 * h + c}", projected([w_in[:, h * 128:(h + 1) * 128]], [xnT[:, :]], c))
                if slot in (6, 7):
                    h = slot - 6
                    for c in range(2):
                        job(q, "PRE", f"z{2 * h + c}", projected([w_in[:, DI + h * 128:DI + (h + 1) * 128]], [xnT[:, :]], c))
                for j in {8: (0,), 9: (1, 2), 10: (3,)}.get(slot, ()):
                    if j == 0:
                        pe.wait_ge(PRE_ACT.sem, PRE_ACT.upto(q, "u1"))
                    h, c = j // 2, j % 2
                    job(q, "PRE", f"dt{j}", projected([w_dt[:, k, h * 128:(h + 1) * 128] for k in range(NH)], us, c))
                if slot in (10, 11):
                    job(q, "PRE", f"b{slot - 10}", projected([w_b[:, k, :] for k in range(NH)], us, slot - 10, 96))

            def post_aux(q, slot):
                if slot == 1:
                    pe.wait_ge(POST_DVE.sem, POST_DVE.upto(q, "yz1"))
                    for c in range(2):
                        def emit(out):
                            for k in range(4):
                                o = out[:, k * 128:(k + 1) * 128]
                                for h in range(NH):
                                    pe.matmul(o, yz[:, h, (4 * c + k) * 128:(4 * c + k + 1) * 128], w_out[:, h, :], start=(h == 0), stop=False)
                                last = pe.matmul(o, ones[0:1, :], b_out[:, :], start=False, stop=True)
                            return last
                        job(q, "POST", f"out{c}", emit)
                if slot == 5:
                    pe.wait_ge(POST_ACT.sem, POST_ACT.upto(q, "norm"))
                    for c in range(2):
                        job(q, "POST", f"t{c}", transposed(xn2, c))
                if slot == 8:
                    pe.wait_ge(POST_ACT.sem, POST_ACT.upto(q, "t1"))

                    def emit(out):
                        for k in range(KT):
                            last = pe.matmul(out[:, k * E:(k + 1) * E], xn2T[:, k * 128:(k + 1) * 128], rt_w[:, :], start=True, stop=True)
                        return last
                    job(q, "POST", "logits", emit)
                if slot == 11:
                    pe.wait_ge(POST_DVE.sem, POST_DVE.upto(q, "oh"))
                    pe.wait_ge(POST_POOL.sem, POST_POOL.upto(q, f"pre{KT - 1}"))

                    def emit(out):
                        pe.matmul(out[:, 0:KT * E], tri[:, :], oh[:, :, :].rearrange("p k e -> p (k e)"), start=True, stop=False)
                        return pe.matmul(out[:, 0:KT * E], ones[:, :], pre[:, 0:KT, :].rearrange("p k e -> p (k e)"),
                                         start=False, stop=True)
                    job(q, "POST", "cum", emit)
            run_groups(pe, main, pre_aux, post_aux)

            def unit(t):
                if not t.least(1):
                    turn(t)
                up(t)
                turn(t + 1)
                if t.least(1):
                    down(t - 1)

            def turn(t):
                pe.wait_ge(s_xe[t.par], (t // 2 + 1) * 16)
                if t.least(2):
                    pe.wait_ge(e_xT, (t - 1) * 1)
                for k in range(4):
                    last = pe.transpose(pT[t.par][:, k * 128:(k + 1) * 128], xe[t.par][:, k, :], ident[:, :])
                last.then_inc(e_T, 1)

            def up(t):
                par = (t // UE).par
                pe.wait_ge(e_xT, (t + 1) * 1)
                if t.off % UE == 0:
                    pe.wait_ge(s_we[par], (t // UE // 2 + 1) * 64)
                for k in range(KF):
                    if t.least(1):
                        pe.wait_ge(e_gelu, (t - 1) * KF + k + 1)
                    pe.matmul(pH[k][:, :], w1[par][:, k * 128:(k + 1) * 128], xeT[t.par][:, :], start=True, stop=True).then_inc(e_h, 1)

            def down(t):
                par = (t // UE).par
                pe.wait_ge(e_gelu, (t + 1) * KF)
                if t.least(2):
                    pe.wait_ge(e_add, (t - 1) * 1)
                for i in range(4):
                    for k in range(KF):
                        last = pe.matmul(pE[t.par][:, i * 128:(i + 1) * 128], he[t.par][:, k, i * 128:(i + 1) * 128], w2[par][:, k, :],
                                         start=(k == 0), stop=(k == KF - 1))
                last.then_inc(e_y, 1)

            def unit_last(t):
                if t.least(UNITS - 1) and t.reg is None:
                    up(t)
                    down(t - 1)
                else:
                    unit(t)
            run_units(pe, unit_last, lambda t: down(t - 1))

            pe.wait_ge(s_w3, 16 * 9)
            pe.wait_ge(s_wk, 1)

            def blk(j, c):
                if c == 2:
                    pe.wait_ge(A_ACT.sem, A_ACT.upto(j, "norm"))
                for i, name in a_jobs(c):
                    o = pA[i % 2]
                    kind, n = name[0], int(name[1])
                    if i >= 2:
                        pe.wait_ge(A_ACT.sem, A_ACT.upto(j, A_JOBS[i - 2]))
                    elif j >= 1:
                        pe.wait_ge(A_ACT.sem, A_ACT.upto(j - 1, A_JOBS[-1]))
                    if kind == "t":
                        for m in range(4):
                            last = pe.transpose(o[:, m * 128:(m + 1) * 128], xnA[:, 4 * n + m, :], ident[:, :])
                    if kind == "g":
                        for m in range(4):
                            last = pe.transpose(o[:, m * 128:(m + 1) * 128],
                                                xnA[:, :, :].rearrange("p l (c g) -> p g (l c)", c=C8)[:, 4 * n + m, :], ident[:, :])
                    if kind == "q":
                        for m in range(8):
                            o_ = o[:, m * QD:(m + 1) * QD]
                            pe.matmul(o_, xnAT[:, 8 * n + m, :], wq[:, :], start=True, stop=False)
                            last = pe.matmul(o_, ones[0:1, :], bq[:, :], start=False, stop=True)
                    if kind == "v":
                        if n == 0:
                            pe.wait_ge(A_ACT.sem, A_ACT.upto(j, "g3"))
                        for m in range(min(7, D // C8 - 7 * n)):
                            last = pe.matmul(o[:, m * C8 * SL:(m + 1) * C8 * SL], xnG[:, 7 * n + m, :],
                                             wk[:, :, :].rearrange("p c s -> p (c s)"), start=True, stop=True)
                    if kind == "r":
                        if n == 0:
                            pe.wait_ge(A_ACT.sem, A_ACT.upto(j, "q1"))
                        for m in range(4):
                            last = pe.transpose(o[:, m * 128:(m + 1) * 128],
                                                q[j % 2][:, :, :].rearrange("p l (c g) -> p g (l c)", c=C8)[:, 4 * n + m, :], ident[:, :])
                    if kind == "k":
                        pe.wait_ge(A_ACT.sem, A_ACT.upto(j, "r1"))
                        for m in range(4):
                            last = pe.matmul(o[:, m * C8 * SL:(m + 1) * C8 * SL], qG[:, 4 * n + m, :],
                                             wk[:, :, :].rearrange("p c s -> p (c s)"), start=True, stop=True)
                    last.then_inc(A_PE.sem, 1)

            def proj(t):
                pe.wait_ge(T_DVE.sem, T_DVE.upto(t, "norm"))
                if t >= 1:
                    pe.wait_ge(B_ACT.sem, B_ACT.upto(t - 1, "xT"))
                for i in range(BQ):
                    last = pe.transpose(pS1[:, i * 128:(i + 1) * 128], on[t % 2][:, i, :], ident[:, :])
                last.then_inc(B_PE.sem, 1)
                pe.wait_ge(B_ACT.sem, B_ACT.upto(t, "oT"))
                if t >= 2:
                    pe.wait_ge(F_DVE.sem, F_DVE.upto(t - 2, "x4"))
                for i in range(BQ):
                    o_ = pS2[:, i * 128:(i + 1) * 128]
                    pe.matmul(o_, oT[:, i * 128:(i + 1) * 128], wo[:, :], start=True, stop=False)
                    last = pe.matmul(o_, ones[0:1, :], bo[:, :], start=False, stop=True)
                last.then_inc(B_PE.sem, 1)
                pe.wait_ge(B_ACT.sem, B_ACT.upto(t, "norm"))
                for i in range(BQ):
                    last = pe.transpose(pS1[:, i * 128:(i + 1) * 128], xnB[:, i, :], ident[:, :])
                last.then_inc(B_PE.sem, 1)

            def gated(t, part):
                if part == 0:
                    pe.wait_ge(B_ACT.sem, B_ACT.upto(t, "xT"))
                    for k in range(KH):
                        n = KH * t + k
                        if n >= 2:
                            pe.wait_ge(F_DVE.sem, F_DVE.upto(t - (k < 2), f"h{(k - 2) % KH}"))
                        for w_, o_ in ((wg, pG), (wup, pU)):
                            pe.matmul(o_[n % 2][:, :], w_[:, k * 128:(k + 1) * 128], xnBT[t % 2][:, :], start=True, stop=True).then_inc(F_PE.sem, 1)
                else:
                    pe.wait_ge(F_DVE.sem, F_DVE.upto(t, f"h{KH - 1}"))
                    nxt = min(t + 1, TU - 1)
                    pe.wait_ge(B_DVE.sem, B_DVE.upto(nxt, "x3"))
                    for i in range(BQ):
                        for k in range(KH):
                            last = pe.matmul(pS2[:, i * 128:(i + 1) * 128], hh[:, k, i * 128:(i + 1) * 128], wd[:, k, :],
                                             start=(k == 0), stop=(k == KH - 1))
                    last.then_inc(F_PE.sem, 1)
            run_last((lambda t: None, lambda t: None), proj, gated, blk)


_NAMES = ["L0_attn_x", "L0_attn_W_in", "L0_attn_W_dt", "L0_attn_W_x", "L0_attn_W_out", "L0_attn_b_out", "L0_ffn_b1",
          "L0_ffn_w1", "L0_ffn_w2", "L0_ffn_b2"]


def kernel(**inputs):
    import numpy as _np
    import concourse.bacc as _bacc
    from concourse import mybir as _mybir
    from concourse.bass_utils import run_bass_kernel_spmd as _run

    nc = _bacc.Bacc("TRN2", target_bir_lowering=False, num_devices=1)
    a = {k: _np.ascontiguousarray(v) for k, v in inputs.items()}
    put = {n: a[n] for n in _NAMES}
    cont = _np.ascontiguousarray
    by_col = lambda v: v.reshape(-1, 128).T
    b_x = _np.tile(_np.tile(a["L0_attn_b_x"][16:32], 2), 4).reshape(128, 1)
    put["cols"] = cont(_np.concatenate([
        by_col(a["L0_attn_b_in"]), by_col(a["L0_attn_conv_b"]), by_col(a["L0_attn_b_dt"]), by_col(a["L0_attn_D"]), b_x,
        a["L0_attn_conv_w"].reshape(2, 128, 4).transpose(1, 0, 2).reshape(128, 8),
        a["L0_attn_A_log"].reshape(2, 128, 16).transpose(1, 0, 2).reshape(128, 32)], axis=1))
    put["router_wT"] = cont(a["L0_ffn_router_w"].T)
    put["b1T"] = cont(a["L0_ffn_b1"].reshape(8, 4, 128).transpose(0, 2, 1))
    put["w_qT"] = cont(a["L1_attn_w_q"].T)
    put["bq"] = a["L1_attn_b_q"].reshape(1, -1)
    put["w_outT"] = cont(a["L1_attn_w_out"].T)
    put["bo"] = a["L1_attn_b_out"].reshape(1, -1)
    put["wkr"] = cont(_np.repeat(a["L1_attn_w_kv"][0:9, 0:16].T, 8, axis=0))
    put["mask8"] = _np.tile(_np.eye(8, dtype=_np.float32), (16, 1))
    put["w_gateT"] = cont(a["L1_ffn_w_gate"].T)
    put["w_upT"] = cont(a["L1_ffn_w_up"].T)
    put["w_downT"] = cont(a["L1_ffn_w_down"].T)
    P = {n: nc.dram_tensor(f"in_{n}_dram", v.shape, _mybir.dt.from_np(v.dtype), kind="ExternalInput").ap() for n, v in put.items()}
    P["out"] = nc.dram_tensor("out_0_dram", (16, 512, 128), _mybir.dt.float32, kind="ExternalOutput").ap()
    P["n_weights"] = 12
    prog(nc, P)
    r = _run(nc, [{f"in_{n}_dram": v for n, v in put.items()}], core_ids=[0])
    return r.results[0]["out_0_dram"]
```

```python
import concourse.bass as bass
from concourse import mybir
from contextlib import ExitStack


class Steps:

    def __init__(self, sem, names):
        self.sem, self.names, self.per = sem, list(names), len(names)

    def upto(self, group, name):
        return group * self.per + self.names.index(name) + 1


class Group:

    def __init__(self, off, reg=None, stride=2):
        self.off, self.reg, self.stride, self.par = off, reg, stride, off % 2

    def __add__(self, k):
        return Group(self.off + k, self.reg, self.stride)

    def __sub__(self, k):
        return self + -k

    def __mul__(self, k):
        return k * self.off if self.reg is None else self.reg * (self.stride * k) + k * self.off

    __rmul__ = __mul__

    def __floordiv__(self, k):
        return Group(self.off // k, self.reg, self.stride // k)

    def least(self, k):
        return self.off >= k


def prog(nc, P):
    fp32 = mybir.dt.float32
    bf16 = mybir.dt.bfloat16
    i32 = mybir.dt.int32
    u32 = mybir.dt.uint32
    ALU = mybir.AluOpType
    ACT = mybir.ActivationFunctionType
    AX = mybir.AxisListType

    x = P["L0_attn_x"]
    B, L, D = x.shape
    DI = P["L0_attn_W_dt"].shape[0]
    NH = DI // 128
    N = 16
    TOK = B * L
    TILES = TOK // 128
    E, FF = P["L0_ffn_b1"].shape
    CAP = -(-3 * TOK // (2 * E))
    SLOTS = E * CAP
    EPS = 1e-5
    SEQ = 2
    G = B // SEQ
    GT = SEQ * L
    KT = GT // 128
    TAPS = 4
    PAD = TAPS - 1

    HG = P["w_gateT"].shape[1]
    KH, KF = HG // 128, FF // 128
    HEADS = 16
    QD = D // 2
    QH, DV = QD // HEADS, D // HEADS
    SL = B // 2 + 1
    C8 = 8
    TB = L // 128
    BQ = 4

    ctx = ExitStack()
    with ctx:
        here = [ctx]

        def sb(n, s, d=fp32):
            return here[0].enter_context(nc.sbuf_tensor(n, s, d))

        def pb(n, s, d=fp32):
            return here[0].enter_context(nc.psum_tensor(n, s, d))

        def sem(n):
            return ctx.enter_context(nc.semaphore(n))

        slots_in = nc.dram_tensor("slots_in", (SLOTS, D), fp32, kind="Internal").ap()
        slots_out = nc.dram_tensor("slots_out", (SLOTS, D), fp32, kind="Internal").ap()

        xres = sb("xres", [128, TILES, D])
        halfs = sb("halfs", [128, B])
        gidx = sb("gidx", [128, TILES], i32)
        gwt = sb("gwt", [128, TILES])
        ident = sb("ident", [128, 128])
        ones = sb("ones", [128, 128])
        ones3 = sb("ones3", [3, 128], bf16)
        bias3 = sb("bias3", [3, 2 * D + D // 2], bf16)
        three = lambda at, n, times: bias3[:, at:at + n].unsqueeze(1).to_broadcast([3, times, n])

        here[0] = ExitStack()
        NA, NB = 8, 4
        dA = [sb(f"dA{i}", [128, SEQ, L]) for i in range(NA)]
        dB = [sb(f"dB{i}", [128, GT]) for i in range(NH)]
        hs = [sb(f"hs{i}", [128, GT]) for i in range(NB)]
        w_in = sb("w_in", [128, 2 * DI])
        w_dt = sb("w_dt", [128, NH, DI])
        w_b = sb("w_b", [128, NH, 96])
        w_out = sb("w_out", [128, NH, D])
        cols = sb("cols", [128, P["cols"].shape[1]])
        c_bin = lambda c: cols[:, c:c + 1]
        c_cb = lambda h: cols[:, 4 + h:5 + h]
        c_bdt = lambda h: cols[:, 6 + h:7 + h]
        c_D = lambda h: cols[:, 8 + h:9 + h]
        c_bx = cols[:, 10:11]
        c_cw = lambda h, k: cols[:, 11 + TAPS * h + k:12 + TAPS * h + k]
        c_alog = cols[:, 19:19 + NH * N]
        c_row = [cols[0:3, 53 + i:54 + i] for i in range(2)]
        c_cut = [cols[:, 51 + i:52 + i] for i in range(2)]
        rt_w = sb("rt_w", [128, E])
        A = sb("A", [128, NH * N])
        tapb = sb("tapb", [128, NH])
        tri = sb("tri", [128, 128])
        sel = sb("sel", [96, N, 128], bf16)
        half = halfs[:, 0:KT]
        w8 = sb("w8", [128, E])

        stat = sb("stat", [128, KT, 6])
        mv = sb("mv", [128, KT, 2])
        veps = sb("veps", [128, KT])
        nmean = sb("nmean", [128, KT])
        rstd = sb("rstd", [128, KT])
        nmr = sb("nmr", [128, KT])
        xn = sb("xn", [128, KT, D])
        biasf = xn[0:3, :, :].rearrange("p k d -> p (k d)")[:, 0:2 * D + D // 2]
        xnT = sb("xnT", [128, GT])
        xhp = sb("xhp", [128, NH, SEQ, PAD + L])
        acc = sb("acc", [128, NH, SEQ, L])
        Bf = acc[0:96, 0, :, :].rearrange("p b t -> p (b t)")
        Br = acc[0:96, 1, :, :].rearrange("p b t -> p (b t)")
        u = [sb(f"u{i}", [128, NH, GT]) for i in range(2)]
        zs = [sb(f"zs{i}", [128, NH, GT]) for i in range(2)]
        dl = [sb(f"dl{i}", [128, NH, GT]) for i in range(2)]
        wu = [sb(f"wu{i}", [128, NH, GT]) for i in range(2)]
        Bs = [sb(f"Bs{i}", [96, GT], bf16) for i in range(2)]
        yz = sb("yz", [128, NH, GT])
        zero = yz[:, :, :].rearrange("p h t -> p (h t)")[:, 0:SLOTS // 8 * D // 128]
        stat2 = sb("stat2", [128, KT, 6])
        mv2 = sb("mv2", [128, KT, 2])
        veps2 = sb("veps2", [128, KT])
        nmean2 = sb("nmean2", [128, KT])
        rstd2 = sb("rstd2", [128, KT])
        nmr2 = sb("nmr2", [128, KT])
        xn2 = sb("xn2", [128, KT, D])
        xn2T = xn[:, :, :].rearrange("p k d -> p (k d)")
        mx = sb("mx", [128, KT])
        lm = sb("lm", [128, KT, E])
        ex = sb("ex", [128, KT, E])
        sm = sb("sm", [128, KT])
        pr = sb("pr", [128, KT])
        sc = sb("sc", [128, KT, E])
        ms = sb("ms", [128, KT])
        oh = sb("oh", [128, KT, E])
        pre = sb("pre", [128, KT + 1, E])
        oc = sb("oc", [128, KT, E])
        rank = sb("rank", [128, KT])
        base = sb("base", [128, KT])
        lost = sb("lost", [128, KT])
        kept = sb("kept", [128, KT])
        srow = sb("srow", [128, KT])
        grow = sb("grow", [128, KT])
        sidx = sb("sidx", [128, KT], i32)

        pY = [pb(f"pY{h}", [128, GT]) for h in range(NH)]
        pB = pb("pB", [128, GT])
        pJ = [pb(f"pJ{i}", [128, 512]) for i in range(2)]

        here[0].close()

        here[0] = ctx
        wq = sb("wq", [128, QD])
        wo = sb("wo", [128, D])
        wkr = sb("wkr", [128, SL])
        mask8 = sb("mask8", [128, C8])
        wk = sb("wk", [128, C8, SL])
        gi = sb("gi", [128, HG], i32)
        ui = sb("ui", [128, HG], i32)
        di = sb("di", [128, KH, D], i32)
        wg = sb("wg", [128, HG])
        wup = sb("wup", [128, HG])
        wd = sb("wd", [128, KH, D])

        here[0] = ExitStack()
        w1 = [sb(f"w1{i}", [128, FF]) for i in range(2)]
        w2 = [sb(f"w2{i}", [128, KF, D]) for i in range(2)]
        b1 = [sb(f"b1{i}", [128, KF]) for i in range(2)]
        b2 = [sb(f"b2{i}", [128, D]) for i in range(2)]
        xe = [sb(f"xe{i}", [128, 4, D]) for i in range(2)]
        xeT = [sb(f"xeT{i}", [128, 512]) for i in range(2)]
        he = [sb(f"he{i}", [128, KF, 512]) for i in range(2)]
        ye = [sb(f"ye{i}", [128, 4, D]) for i in range(2)]
        pT = [pb(f"pT{i}", [128, 512]) for i in range(2)]
        pH = [pb(f"pH{i}", [128, 512]) for i in range(KF)]
        pE = [pb(f"pE{i}", [128, 512]) for i in range(2)]
        here[0].close()

        here[0] = ExitStack()
        gx = sb("gx", [128, B, D])
        stA = sb("stA", [128, B, 6])
        mvA = sb("mvA", [128, B, 2])
        veA = sb("veA", [128, B])
        nmA = sb("nmA", [128, B])
        rsA = sb("rsA", [128, B])
        nrA = sb("nrA", [128, B])
        xnA = sb("xnA", [128, B, D])
        xnAT = sb("xnAT", [128, B, 128])
        xnG = sb("xnG", [128, D // C8, 128])
        q = [sb(f"q{i}", [128, B, QD]) for i in range(2)]
        qG = sb("qG", [128, QD // C8, 128])
        kk = [sb(f"kk{i}", [128, QD, SL]) for i in range(2)]
        vv = [sb(f"vv{i}", [128, D, SL]) for i in range(2)]
        qk = [sb(f"qk{i}", [128, BQ, HEADS, SL]) for i in range(QH)]
        at = [sb(f"at{i}", [128, BQ * HEADS, SL]) for i in range(2)]
        am = sb("am", [128, BQ * HEADS])
        ad = sb("ad", [128, BQ * HEADS])
        ar = sb("ar", [128, BQ * HEADS])
        pv = [sb(f"pv{i}", [128, HEADS, DV, SL]) for i in range(2)]
        oo = [sb(f"oo{i}", [128, BQ, D]) for i in range(2)]
        on = [sb(f"on{i}", [128, BQ, D]) for i in range(2)]
        oT = sb("oT", [128, BQ * 128])
        stB = sb("stB", [128, BQ, 6])
        mvB = sb("mvB", [128, BQ, 2])
        veB = sb("veB", [128, BQ])
        nmB = sb("nmB", [128, BQ])
        rsB = sb("rsB", [128, BQ])
        nrB = sb("nrB", [128, BQ])
        xnB = sb("xnB", [128, BQ, D])
        xnBT = [sb(f"xnBT{i}", [128, BQ * 128]) for i in range(2)]
        sg = [sb(f"sg{i}", [128, BQ * 128]) for i in range(KH)]
        hh = sb("hh", [128, KH, BQ * 128])
        pA = [pb(f"pA{i}", [128, 512]) for i in range(2)]
        pT3, pP, pD, pG = (pb(n, [128, 512]) for n in ("pT3", "pP", "pD", "pG"))
        pU = [pb(f"pU{i}", [128, 512]) for i in range(2)]
        here[0].close()
        here[0] = ctx

        s_w = sem("s_w")
        s_passed = sem("s_passed")
        s_x = sem("s_x")
        s_zero = sem("s_zero")
        s_cst = sem("s_cst")
        s_A = sem("s_A")
        s_sel = sem("s_sel")
        s_bias = sem("s_bias")
        s_zr = sem("s_zr")
        s_out = sem("s_out")
        s_scat = sem("s_scat")

        NRM_DVE = Steps(sem("nrm_dve"), ["stats", "aggr", "center"])
        NRM_POOL = Steps(sem("nrm_pool"), ["rstd", "nmr"])
        NRM_ACT = Steps(sem("nrm_act"), ["norm", "t0", "t1"])
        NRM_PE = Steps(sem("nrm_pe"), ["t0", "t1"])
        PRE_DVE = Steps(sem("pre_dve"), [f"conv{h}_{k}" for h in range(NH) for k in range(TAPS - 1)] +
                        ["delta0", "delta1", "w0", "w1"])
        PRE_POOL = Steps(sem("pre_pool"), ["part2", "cut2", "part3", "cast3"])
        PRE_ACT = Steps(sem("pre_act"), ["xh0", "xh1", "xh2", "xh3", "u0", "u1", "z0", "z1", "z2", "z3", "b0", "b1", "cut1",
                                         "dt0", "dt1", "spexp0", "dt2", "dt3", "spexp1", "spln0", "spln1"])
        PRE_PE = Steps(sem("pre_pe"), ["xh0", "xh1", "xh2", "xh3", "z0", "z1", "z2", "z3", "b0", "b1",
                                       "dt0", "dt1", "dt2", "dt3"])
        Z_ACT = Steps(sem("z_act"), ["silu"])
        POST_DVE = Steps(sem("post_dve"), ["yt0", "yt1", "yz0", "yz1", "res0", "res1", "stats", "aggr", "center",
                                           "mx", "lm", "sm", "pr", "eq", "ms", "oh", "oc", "rank",
                                           "base", "kept", "lost", "srow", "sidx", "grow", "gidx", "gw"])
        POST_POOL = Steps(sem("post_pool"), ["rstd", "nmr", "carry"] + [f"pre{k}" for k in range(KT)])
        POST_ACT = Steps(sem("post_act"), ["norm", "t0", "t1", "ex"])
        POST_PE = Steps(sem("post_pe"), ["out0", "out1", "t0", "t1", "logits", "cum"])
        m_exp, m_mul, m_scan, m_bc, m_sum = (sem(n) for n in ("m_exp", "m_mul", "m_scan", "m_bc", "m_sum"))
        NS = NH * N

        UE = CAP // 512
        UNITS = E * UE
        s_we = [sem(f"s_we{i}") for i in range(2)]
        s_xe = [sem(f"s_xe{i}") for i in range(2)]
        s_ye = [sem(f"s_ye{i}") for i in range(2)]
        e_T, e_xT, e_h, e_gelu, e_y, e_add = (sem(n) for n in ("e_T", "e_xT", "e_h", "e_gelu", "e_y", "e_add"))

        s_w3 = sem("s_w3")
        s_wk = sem("s_wk")
        s_gx = [sem(f"s_gx{i}") for i in range(B // BQ)]
        s_fin = sem("s_fin")
        A_JOBS = "t0 t1 q0 t2 t3 q1 r0 r1 k0 k1 g0 g1 g2 g3 v0 v1 v2".split()
        A_DVE = Steps(sem("a_dve"), [f"{n}{i}" for i in range(B // BQ) for n in ("x2_", "stats", "aggr", "center")])
        A_POOL = Steps(sem("a_pool"), [f"{n}{i}" for i in range(B // BQ) for n in ("rstd", "nmr")])
        A_NRM = Steps(sem("a_nrm"), [f"norm{i}" for i in range(B // BQ)])
        A_ACT = Steps(sem("a_act"), A_JOBS)
        A_PE = Steps(sem("a_pe"), A_JOBS)
        T_DVE = Steps(sem("t_dve"), [f"qk{d}" for d in range(QH)] + ["s01", "s23", "s", "max", "sub", "den", "rden"] +
                      [f"{n}{l}" for l in range(BQ) for n in ("pv", "o")] + ["norm"])
        T_ACT = Steps(sem("t_act"), ["exp"])
        B_DVE = Steps(sem("b_dve"), ["x3", "stats", "aggr", "center"])
        B_POOL = Steps(sem("b_pool"), ["rstd", "nmr"])
        B_ACT = Steps(sem("b_act"), ["oT", "norm", "xT"])
        B_PE = Steps(sem("b_pe"), ["oT", "proj", "xT"])
        F_PE = Steps(sem("f_pe"), ["g0", "u0", "g1", "u1", "g2", "u2"])
        D_PE = Steps(sem("d_pe"), ["down"])
        F_ACT = Steps(sem("f_act"), [f"silu{k}" for k in range(KH)])
        F_DVE = Steps(sem("f_dve"), [f"h{k}" for k in range(KH)] + ["x4"])
        TU = B // BQ * TB

        def run_units(eng, unit, last):
            body = 2 * UE
            for k in range(body):
                unit(Group(k))
            with eng.Fori(0, UNITS // body - 2) as i:
                for k in range(body):
                    unit(Group(body + k, i, body))
            for k in range(UNITS - body, UNITS):
                unit(Group(k))
            last(Group(UNITS))

        A_PLACES = {1: ["t0", "t1", "q0", ""], 2: ["t2 t3", "q1", "r0 r1", "k0 k1"], 3: ["g0 g1", "g2 g3", "v0 v1", "v2"]}

        def run_last(chunk, job, unit, rows_ahead=0):
            for i in range(B // BQ):
                chunk(0, i)
                for name in ["t0", "t1 q0", "t2", "t3"][i].split():
                    job(0, name)
            for j in range(1, 1 + rows_ahead):
                for i in range(B // BQ):
                    chunk(j, i)
            for name in A_JOBS[A_JOBS.index("q1"):]:
                job(0, name)

            def places(t):
                nxt, c = t // BQ + 1, t % BQ

                def row_chunk(i):
                    if rows_ahead < nxt < TB and c < 2:
                        chunk(nxt, 2 * c + i)

                def jobs(place):
                    if nxt < TB and c >= 1:
                        for name in A_PLACES[c][place].split():
                            job(nxt, name)
                return row_chunk, jobs

            for t in range(TU + 2):
                unit(t, *places(t))

        NW = P["n_weights"]
        block = ctx.enter_context(nc.Block())

        def tiles(ap):
            return ap.rearrange("b (j p) d -> p (b j) d", p=128)

        JOBS = ([("PRE", f"xh{i}", i % 2, PRE_ACT, f"xh{i}") for i in range(4)] +
                [("POST", f"out{c}", c, POST_DVE, f"res{c}") for c in range(2)] +
                [("PRE", f"z{i}", i % 2, PRE_ACT, f"z{i}") for i in range(4)] +
                [("PRE", f"b{i}", i, PRE_ACT, f"b{i}") for i in range(2)] +
                [("POST", "t0", 0, POST_ACT, "t0"), ("PRE", "dt0", 1, PRE_ACT, "dt0"),
                 ("POST", "t1", 0, POST_ACT, "t1"), ("PRE", "dt1", 1, PRE_ACT, "dt1"),
                 ("POST", "logits", 0, POST_DVE, "lm"), ("PRE", "dt2", 1, PRE_ACT, "dt2"),
                 ("PRE", "dt3", 1, PRE_ACT, "dt3"),
                 ("NRM", "t0", 0, NRM_ACT, "t0"), ("NRM", "t1", 1, NRM_ACT, "t1"),
                 ("POST", "cum", 0, POST_DVE, "oc")])
        AHEAD = {"POST": -1, "PRE": 1, "NRM": 2, "Z": 0}
        JOB_AT = {(j[0], j[1]): i for i, j in enumerate(JOBS)}

        def bank(stage, name):
            return pJ[JOBS[JOB_AT[stage, name]][2]][:, :]

        def after(eng, period, stage, name):
            at = JOB_AT[stage, name]
            back = [(period, j) for j in JOBS[:at][::-1]] + [(period - 1, j) for j in JOBS[::-1]] + [(period - 2, j) for j in JOBS[::-1]] + [(period - 3, j) for j in JOBS[::-1]]
            for p, j in back:
                q = p + AHEAD[j[0]]
                exists = q.off >= 0 and (p.reg is not None or q.off < G)
                if j[2] == JOBS[at][2] and exists:
                    eng.wait_ge(j[3].sem, j[3].upto(q, j[4]))
                    return

        def settle(eng):
            eng.sem_inc(s_passed, 1)

        def run_groups(eng, main, stages, lead=0):
            def period(g):
                for n in range(N):
                    at = g + (n + lead) // N
                    if main and (at.reg is not None or 0 <= at.off < G):
                        main(at, (n + lead) % N)
                    for stage, aux in stages:
                        q = g + AHEAD[stage]
                        if q.off >= 0 and (q.reg is not None or q.off < G):
                            aux(q, n)

            for g in range(-2, 2):
                period(Group(g))
            with eng.Fori(0, (G - 4) // 2) as pair:
                period(Group(2, pair))
                period(Group(3, pair))
            for g in range(G - 2, G + 1):
                period(Group(g))

        @block.sync
        def _(sp):
            sp.dma_start(xres[:, 0:KT, :], tiles(x)[:, 0:KT, :]).then_inc(s_x, 16)
            sp.dma_start(cols[:, :], P["cols"]).then_inc(s_w, 16)
            sp.dma_start(w_in[:, :], P["L0_attn_W_in"]).then_inc(s_w, 16)
            sp.dma_start(w_dt[:, :, :], P["L0_attn_W_dt"].rearrange("(k p) n -> p k n", p=128)).then_inc(s_w, 16)
            for c in range(3):
                sp.dma_start(w_b[:, :, 32 * c:32 * c + N],
                             P["L0_attn_W_x"][:, N:2 * N].rearrange("(k p) n -> p k n", p=128)).then_inc(s_w, 16)
                sp.dma_start(w_b[:, :, 32 * c + N:32 * c + 2 * N],
                             P["L0_attn_W_x"][:, N:2 * N].rearrange("(k p) n -> p k n", p=128)).then_inc(s_w, 16)
            sp.dma_start(w_out[:, :, :], P["L0_attn_W_out"].rearrange("(k p) n -> p k n", p=128)).then_inc(s_w, 16)
            sp.dma_start(biasf, P["bias3"]).then_inc(s_w, 16)
            sp.dma_start(rt_w[:, :], P["router_wT"]).then_inc(s_w, 16)
            with sp.Fori(1, G) as g:
                sp.wait_ge(s_x, 16 * g)
                sp.dma_start(xres[:, bass.ds(g * KT, KT), :], tiles(x)[:, bass.ds(g * KT, KT), :]).then_inc(s_x, 16)
            sp.wait_ge(s_zr, 1)
            for k in range(8):
                sp.dma_start(slots_in[k * (SLOTS // 8):(k + 1) * (SLOTS // 8), :].rearrange("(p r) d -> p (r d)", p=128),
                             zero).then_inc(s_zero, 16)
            sp.wait_ge(m_scan, G * NS)
            sp.wait_ge(m_sum, G * NS)

            def weights(e):
                par = e.par
                if e.least(2):
                    sp.wait_ge(e_add, (e - 1) * UE)
                one = lambda n: P[n][bass.ds(e * 1, 1)]
                sp.dma_start(w1[par][:, :], one("L0_ffn_w1").rearrange("a d f -> d (a f)")).then_inc(s_we[par], 16)
                sp.dma_start(w2[par][:, :, :], one("L0_ffn_w2").rearrange("a (k p) d -> p (a k) d", p=128)).then_inc(s_we[par], 16)
                sp.dma_start(b1[par][:, :], one("b1T").rearrange("a p k -> p (a k)")).then_inc(s_we[par], 16)
                sp.dma_start(b2[par][:, :], one("L0_ffn_b2").to_broadcast([128, D])).then_inc(s_we[par], 16)

            def load(t):
                if t.least(2):
                    sp.wait_ge(e_T, (t - 2) * 1 + 1)
                sp.dma_start(xe[t.par][:, :, :], slots_in[bass.ds(t * 512, 512), :].rearrange("(k p) d -> p k d", p=128)
                             ).then_inc(s_xe[t.par], 16)

            def unit(t):
                load(t)
                if t.off % UE == 1 and (t.reg is not None or t.off < UNITS - UE):
                    weights(t // UE + 1)
            weights(Group(0))
            load_w3 = [(wq, "w_qT"), (wo, "w_outT"), (wkr, "wkr"), (mask8, "mask8"), (gi, "w_gateT"), (ui, "w_upT")]
            for dst, name in load_w3:
                sp.dma_start(dst[:, :], P[name]).then_inc(s_w3, 16)
            sp.dma_start(di[:, :, :], P["w_downT"].rearrange("(k p) d -> p k d", p=128)).then_inc(s_w3, 16)
            sp.wait_ge(s_scat, 16 * TILES)
            run_units(sp, unit, lambda t: None)
            for t in range(TU):
                j, c = t // BQ, t % BQ
                sp.wait_ge(F_DVE.sem, F_DVE.upto(t, "x4"))
                src = xres[:, :, :].rearrange("p (b j) d -> p b j d", j=TB)[:, BQ * c:BQ * c + BQ, j, :]
                sp.dma_start(P["out"][BQ * c:BQ * c + BQ, 128 * j:128 * j + 128, :].rearrange("b p d -> p b d"), src).then_inc(s_out, 16)
            sp.wait_ge(s_out, 16 * TU)

        @block.gpsimd
        def _(pool):
            pool.memset(ident[:, :], 0.0)
            pool.memset(tri[:, :], 1.0)
            pool.memset(ones[:, :], 1.0)
            pool.memset(ones3[:, :], 1.0)
            pool.memset(halfs[:, :], -0.5)
            pool.memset(sel[:, :, :], 0.0)
            pool.memset(pre[:, :, :], 0.0)
            for h in range(NH):
                pool.memset(xhp[:, h, :, 0:PAD], 0.0)
            for b in range(NA):
                pool.memset(dA[b][:, :, 0:1], 0.0)
            pool.iota(w8[:, :], pattern=[[-1, E]], base=E, channel_multiplier=0,
                      allow_small_or_imprecise_dtypes=True).then_inc(s_cst, 1)
            pool.memset(zero, 0.0).then_inc(s_zr, 1)
            pool.wait_ge(s_cst, 1)
            pool.affine_select(out=ident[:, :], in_=ident[:, :], compare_op=ALU.not_equal, fill=1.0,
                               base=0, pattern=[[-1, 128]], channel_multiplier=1)
            pool.affine_select(out=tri[:, :], in_=tri[:, :], compare_op=ALU.is_ge, fill=0.0,
                               base=0, pattern=[[1, 128]], channel_multiplier=-1)
            for c in range(3):
                if c:
                    pool.wait_ge(s_sel, c)
                last = pool.affine_select(out=sel[:, :, :], in_=sel[:, :, :], compare_op=ALU.not_equal, fill=1.0,
                                          base=-32 * c, pattern=[[-1, N], [0, 128]], channel_multiplier=1)
                last.then_inc(s_sel, 1)

            def nrm_aux(q, slot):
                if slot == 10:
                    pool.wait_ge(NRM_DVE.sem, NRM_DVE.upto(q, "center"))
                    pool.tensor_tensor(rstd[:, :], veps[:, :], half, ALU.pow).then_inc(NRM_POOL.sem, 1)
                    pool.wait_ge(NRM_POOL.sem, NRM_POOL.upto(q, "rstd"))
                    pool.tensor_tensor(nmr[:, :], nmean[:, :], rstd[:, :], ALU.mult).then_inc(NRM_POOL.sem, 1)

            def pre_aux(q, slot):
                if slot == 8:
                    own = lambda name: pool.wait_ge(PRE_POOL.sem, PRE_POOL.upto(q, name))
                    done = lambda i: i.then_inc(PRE_POOL.sem, 1)
                    bs = Bs[q.par]
                    pool.wait_ge(PRE_ACT.sem, PRE_ACT.upto(q, "cut1"))
                    done(pool.tensor_tensor(Br, Bf, bs[:, :], ALU.add))
                    own("part2")
                    settle(pool)
                    done(pool.tensor_scalar(bs[:, :], Br, c_cut[1][0:96], None, ALU.mult))
                    own("cut2")
                    done(pool.tensor_tensor(Br, Br, bs[:, :], ALU.add))
                    own("part3")
                    settle(pool)
                    done(pool.tensor_copy(bs[:, :], Br))

            def post_aux(q, slot):
                if slot == 5:
                    pool.wait_ge(POST_DVE.sem, POST_DVE.upto(q, "center"))
                    pool.tensor_tensor(rstd2[:, :], veps2[:, :], half, ALU.pow).then_inc(POST_POOL.sem, 1)
                    pool.wait_ge(POST_POOL.sem, POST_POOL.upto(q, "rstd"))
                    pool.tensor_tensor(nmr2[:, :], nmean2[:, :], rstd2[:, :], ALU.mult).then_inc(POST_POOL.sem, 1)
                if slot == 13:
                    pool.wait_ge(POST_DVE.sem, POST_DVE.upto(q, "oh"))
                    if q.least(1):
                        pool.wait_ge(POST_PE.sem, POST_PE.upto(q - 1, "cum"))
                        pool.wait_ge(POST_POOL.sem, POST_POOL.upto(q - 1, f"pre{KT - 1}"))
                    settle(pool)
                    pool.tensor_copy(pre[:, 0, :], pre[:, KT, :]).then_inc(POST_POOL.sem, 1)
                    for k in range(KT):
                        pool.wait_ge(POST_POOL.sem, POST_POOL.upto(q, f"pre{k - 1}" if k else "carry"))
                        pool.tensor_tensor(pre[:, k + 1, :], pre[:, k, :], oh[:, k, :], ALU.add).then_inc(POST_POOL.sem, 1)
                if slot == 15:
                    if not q.least(1):
                        pool.wait_ge(s_zero, 16 * 8)
                    pool.wait_ge(POST_ACT.sem, POST_ACT.upto(q, "norm"))
                    pool.wait_ge(POST_DVE.sem, POST_DVE.upto(q, "sidx"))
                    settle(pool)
                    for k in range(KT):
                        pool.indirect_dma_start(out=slots_in, out_offset=bass.IndirectOffsetOnAxis(ap=sidx[:, k:k + 1], axis=0),
                                                in_=xn2[:, k, :], in_offset=None,
                                                bounds_check=SLOTS - 1, oob_is_err=False).then_inc(s_scat, 16)
            run_groups(pool, None, [("POST", post_aux), ("PRE", pre_aux), ("NRM", nrm_aux)])

            def unit(t):
                if t.least(1):
                    store(t - 1)

            def store(t):
                pool.wait_ge(e_add, (t + 1) * 1)
                settle(pool)
                pool.dma_start(slots_out[bass.ds(t * 512, 512), :].rearrange("(k p) d -> p k d", p=128),
                               ye[t.par][:, :, :]).then_inc(s_ye[t.par], 16)
            run_units(pool, unit, lambda t: store(t - 1))

            pool.wait_ge(s_ye[0], 16 * (UNITS // 2))
            pool.wait_ge(s_ye[1], 16 * (UNITS // 2))

            def gather(j, i):
                if j >= 1:
                    pool.wait_ge(A_DVE.sem, A_DVE.upto(j - 1, f"x2_{i}"))
                for l in range(BQ * i, BQ * i + BQ):
                    pool.indirect_dma_start(out=gx[:, l, :], out_offset=None, in_=slots_out,
                                            in_offset=bass.IndirectOffsetOnAxis(ap=gidx[:, TB * l + j:TB * l + j + 1], axis=0),
                                            bounds_check=SLOTS - 1, oob_is_err=False).then_inc(s_gx[i], 16)

            def chunk(j, i):
                four = slice(BQ * i, BQ * i + BQ)
                pool.wait_ge(A_DVE.sem, A_DVE.upto(j, f"center{i}"))
                if j >= 1:
                    pool.wait_ge(A_NRM.sem, A_NRM.upto(j - 1, f"norm{i}"))
                pool.tensor_tensor(rsA[:, four], veA[:, four], halfs[:, four], ALU.pow).then_inc(A_POOL.sem, 1)
                pool.wait_ge(A_POOL.sem, A_POOL.upto(j, f"rstd{i}"))
                pool.tensor_tensor(nrA[:, four], nmA[:, four], rsA[:, four], ALU.mult).then_inc(A_POOL.sem, 1)
                if j == 0:
                    if i < 2:
                        gather(0, i + 2)
                    if i == 3:
                        for k in range(4):
                            gather(1, k)
                elif j < TB - 1:
                    gather(j + 1, i)

            def norm_b(t):
                pool.wait_ge(B_DVE.sem, B_DVE.upto(t, "center"))
                pool.tensor_tensor(rsB[:, :], veB[:, :], halfs[:, 0:BQ], ALU.pow).then_inc(B_POOL.sem, 1)
                pool.wait_ge(B_POOL.sem, B_POOL.upto(t, "rstd"))
                pool.tensor_tensor(nrB[:, :], nmB[:, :], rsB[:, :], ALU.mult).then_inc(B_POOL.sem, 1)

            def last_unit(t, row_chunk, jobs):
                if 1 <= t <= TU:
                    norm_b(t - 1)
                row_chunk(0)
                row_chunk(1)
            gather(0, 0)
            gather(0, 1)
            run_last(chunk, lambda j, name: None, last_unit)

        @block.scalar
        def _(act):
            act.wait_ge(s_w, 16 * NW)
            act.activation(A[:, :], c_alog, ACT.Exp).then_inc(s_A, 1)
            act.wait_ge(s_A, 1)
            act.mul(A[:, :], A[:, :], -1.0)
            for h in range(NH):
                last = act.mul(tapb[:, h:h + 1], c_bin(h), c_cw(h, TAPS - 1))
            last.then_inc(s_A, 1)
            act.wait_ge(s_A, 2)
            act.wait_ge(s_cst, 1)
            act.wait_ge(s_bias, 5)

            def main(g, n):
                for h in range(NH):
                    s = NH * n + h
                    if s == 0:
                        act.wait_ge(PRE_DVE.sem, PRE_DVE.upto(g, "delta1"))
                    if g.least(1) or s >= NA:
                        act.wait_ge(m_scan, g * NS + s - NA + 1)
                    act.activation(dA[s % NA][:, :, 1:L], dl[g.par][:, h, :].rearrange("p (b t) -> p b t", b=SEQ)[:, :, 1:L],
                                   ACT.Exp, scale=A[:, N * h + n:N * h + n + 1]).then_inc(m_exp, 1)

            def nrm_aux(q, slot):
                done = lambda i: i.then_inc(NRM_ACT.sem, 1)
                if slot == 12:
                    act.wait_ge(NRM_POOL.sem, NRM_POOL.upto(q, "nmr"))
                    if q.least(3):
                        act.wait_ge(POST_PE.sem, POST_PE.upto(q - 3, "logits"))
                    for k in range(KT):
                        last = act.activation(xn[:, k, :], xres[:, bass.ds(q * KT + k, 1), :], ACT.Identity,
                                              bias=nmr[:, k:k + 1], scale=rstd[:, k:k + 1])
                    done(last)
                if slot == 13:
                    for c in range(2):
                        act.wait_ge(NRM_PE.sem, NRM_PE.upto(q, f"t{c}"))
                        if q.least(1):
                            act.wait_ge(PRE_PE.sem, PRE_PE.upto(q - 1, "z3"))
                        done(act.copy(xnT[:, c * 512:(c + 1) * 512], bank("NRM", f"t{c}")))

            def z_aux(q, slot):
                if slot == 5:
                    act.wait_ge(PRE_ACT.sem, PRE_ACT.upto(q, "z3"))
                    d = zs[q.par][:, 1, :]
                    act.activation(d, d, ACT.Silu).then_inc(Z_ACT.sem, 1)

            def pre_aux(q, slot):
                par = q.par
                done = lambda i: i.then_inc(PRE_ACT.sem, 1)
                if slot in (1, 2):
                    if slot == 1 and q.least(1):
                        act.wait_ge(PRE_POOL.sem, PRE_POOL.upto(q - 1, "cast3"))
                    for j in (2 * slot - 2, 2 * slot - 1):
                        h, c = j // 2, j % 2
                        act.wait_ge(PRE_PE.sem, PRE_PE.upto(q, f"xh{j}"))
                        act.activation(xhp[:, h, c, PAD:PAD + L], bank("PRE", f"xh{j}"), ACT.Identity, bias=c_bin(h))
                        done(act.activation(acc[:, h, c, :], bank("PRE", f"xh{j}"), ACT.Identity, bias=tapb[:, h:h + 1],
                                            scale=c_cw(h, TAPS - 1)))
                if slot == 5:
                    act.wait_ge(PRE_DVE.sem, PRE_DVE.upto(q, f"conv{NH - 1}_{TAPS - 2}"))
                    if q.least(2):
                        act.wait_ge(POST_DVE.sem, POST_DVE.upto(q - 2, "yz1"))
                    for h in range(NH):
                        done(act.activation(u[par][:, h, :].rearrange("p (b t) -> p b t", b=SEQ), acc[:, h, :, :],
                                            ACT.Silu, bias=c_cb(h)))
                if slot in (5, 6):
                    for j in (2 * slot - 10, 2 * slot - 9):
                        h, c = j // 2, j % 2
                        act.wait_ge(PRE_PE.sem, PRE_PE.upto(q, f"z{j}"))
                        done(act.activation(zs[par][:, h, c * 512:(c + 1) * 512], bank("PRE", f"z{j}"),
                                            ACT.Identity if h else ACT.Silu, bias=c_bin(2 + h)))

                def b_out(c):
                    act.wait_ge(PRE_PE.sem, PRE_PE.upto(q, f"b{c}"))
                    done(act.activation(Bf[:, c * 512:(c + 1) * 512], bank("PRE", f"b{c}")[0:96, :], ACT.Identity, bias=c_bx[0:96]))

                def dt_out(j):
                    h, c = j // 2, j % 2
                    act.wait_ge(PRE_PE.sem, PRE_PE.upto(q, f"dt{j}"))
                    act.activation(dl[par][:, h, c * 512:(c + 1) * 512], bank("PRE", f"dt{j}"), ACT.Abs, bias=c_bdt(h))
                    done(act.activation(wu[par][:, h, c * 512:(c + 1) * 512], bank("PRE", f"dt{j}"), ACT.Relu, bias=c_bdt(h)))

                def softplus(h, func, scale, bias, wait):
                    d = dl[par][:, h, :]
                    act.wait_ge(PRE_ACT.sem, PRE_ACT.upto(q, wait))
                    done(act.activation(d, d, func, scale=scale, bias=bias))
                if slot == 7:
                    act.wait_ge(PRE_ACT.sem, PRE_ACT.upto(q, "u1"))
                    b_out(0)
                if slot == 8:
                    b_out(1)
                    act.wait_ge(PRE_ACT.sem, PRE_ACT.upto(q, "b1"))
                    if q.least(2):
                        act.wait_ge(m_bc, (q - 1) * N)
                    done(act.activation(Bs[par][:, :], Bf, ACT.Copy, scale=c_cut[0][0:96]))
                if slot == 9:
                    if q.least(2):
                        act.wait_ge(m_mul, (q - 1) * NS)
                    dt_out(0)
                if slot == 10:
                    dt_out(1)
                    softplus(0, ACT.Exp, -1.0, 0.0, "dt1")
                if slot == 11:
                    dt_out(2)
                if slot == 12:
                    dt_out(3)
                    softplus(1, ACT.Exp, -1.0, 0.0, "dt3")
                    for h in range(NH):
                        softplus(h, ACT.Ln, 1.0, 1.0, f"spexp{h}")

            def post_aux(q, slot):
                done = lambda i: i.then_inc(POST_ACT.sem, 1)
                if slot == 7:
                    act.wait_ge(POST_POOL.sem, POST_POOL.upto(q, "nmr"))
                    if q.least(1):
                        act.wait_ge(s_scat, 16 * KT * q)
                    for k in range(KT):
                        last = act.activation(xn2[:, k, :], xres[:, bass.ds(q * KT + k, 1), :], ACT.Identity,
                                              bias=nmr2[:, k:k + 1], scale=rstd2[:, k:k + 1])
                    done(last)
                if slot in (9, 10):
                    for c in (slot - 9,):
                        act.wait_ge(POST_PE.sem, POST_PE.upto(q, f"t{c}"))
                        done(act.copy(xn2T[:, c * 512:(c + 1) * 512], bank("POST", f"t{c}")))
                if slot == 12:
                    act.wait_ge(POST_DVE.sem, POST_DVE.upto(q, "lm"))
                    done(act.activation(ex[:, :, :], lm[:, :, :], ACT.Exp))
            run_groups(act, main, [("POST", post_aux), ("PRE", pre_aux), ("Z", z_aux), ("NRM", nrm_aux)], lead=2)

            def unit(t):
                if t.off % UE == 0:
                    act.wait_ge(s_we[(t // UE).par], (t // UE // 2 + 1) * 64)
                if t.least(2):
                    act.wait_ge(e_y, (t - 1) * 1)
                for k in range(KF):
                    act.wait_ge(e_h, t * KF + k + 1)
                    act.activation(he[t.par][:, k, :], pH[k][:, :], ACT.Gelu,
                                   bias=b1[(t // UE).par][:, k:k + 1]).then_inc(e_gelu, 1)
            run_units(act, unit, lambda t: None)

            def chunk(j, i):
                act.wait_ge(A_POOL.sem, A_POOL.upto(j, f"nmr{i}"))
                for l in range(BQ * i, BQ * i + BQ):
                    last = act.activation(xnA[:, l, :], xres[:, TB * l + j, :], ACT.Identity,
                                          bias=nrA[:, l:l + 1], scale=rsA[:, l:l + 1])
                last.then_inc(A_NRM.sem, 1)

            def job(j, name):
                kind, n = name[0], int(name[1])
                four = slice(4 * n, 4 * n + 4)
                scale, size = 1.0, 512
                if kind == "t":
                    dst = xnAT[:, four, :].rearrange("p l b -> p (l b)")
                if kind == "g":
                    dst = xnG[:, four, :].rearrange("p l b -> p (l b)")
                if kind == "q":
                    dst = q[j % 2][:, 8 * n:8 * n + 8, :].rearrange("p l c -> p (l c)")
                if kind == "r":
                    dst = qG[:, four, :].rearrange("p g b -> p (g b)")
                if kind == "v":
                    w = min(7 * C8, D - 7 * C8 * n)
                    dst, size = vv[j % 2][:, 7 * C8 * n:7 * C8 * n + w, :].rearrange("p c s -> p (c s)"), w * SL
                if kind == "k":
                    dst = kk[j % 2][:, :, :].rearrange("p (c g) s -> p g c s", c=C8)[:, four, :, :]
                    scale, size = float(DV) ** -0.5, 32 * SL
                act.wait_ge(A_PE.sem, A_PE.upto(j, name))
                if name == "q0" and j >= 2:
                    act.wait_ge(T_DVE.sem, T_DVE.upto(BQ * (j - 1) - 1, "norm"))
                src = pA[A_JOBS.index(name) % 2][:, 0:size]
                if kind == "k":
                    src = src.rearrange("p (g c s) -> p g c s", c=C8, s=SL)
                act.activation(dst, src, ACT.Copy, scale=scale).then_inc(A_ACT.sem, 1)

            def exp(t):
                act.wait_ge(T_DVE.sem, T_DVE.upto(t, "sub"))
                act.activation(at[t % 2][:, :, :], at[t % 2][:, :, :], ACT.Exp).then_inc(T_ACT.sem, 1)

            def turned(t):
                act.wait_ge(B_PE.sem, B_PE.upto(t, "oT"))
                act.copy(oT[:, :], pT3[:, :]).then_inc(B_ACT.sem, 1)

            def norm(t):
                act.wait_ge(B_POOL.sem, B_POOL.upto(t, "nmr"))
                for i in range(BQ):
                    l = TB * (BQ * (t % BQ) + i) + t // BQ
                    last = act.activation(xnB[:, i, :], xres[:, l, :], ACT.Identity, bias=nrB[:, i:i + 1], scale=rsB[:, i:i + 1])
                last.then_inc(B_ACT.sem, 1)

            def norm_turned(t):
                act.wait_ge(B_PE.sem, B_PE.upto(t, "xT"))
                act.copy(xnBT[t % 2][:, :], pT3[:, :]).then_inc(B_ACT.sem, 1)

            def silu(t, k):
                act.wait_ge(F_PE.sem, F_PE.upto(t, f"g{k}"))
                if t >= 1:
                    act.wait_ge(F_DVE.sem, F_DVE.upto(t - 1, f"h{k}"))
                act.activation(sg[k][:, :], pG[:, :], ACT.Silu).then_inc(F_ACT.sem, 1)

            def last_unit(t, row_chunk, jobs):
                attn = 1 <= t <= TU
                if attn:
                    turned(t - 1)
                if t >= 2:
                    silu(t - 2, 2)
                if t < TU:
                    exp(t)
                if attn:
                    norm(t - 1)
                jobs(0)
                row_chunk(0)
                if attn:
                    norm_turned(t - 1)
                jobs(1)
                row_chunk(1)
                if attn:
                    silu(t - 1, 0)
                jobs(2)
                if attn:
                    silu(t - 1, 1)
                jobs(3)
            run_last(chunk, job, last_unit)

        @block.vector
        def _(dve):
            def stats(src, st, m, ve, nm, S, q):
                done = lambda i: i.then_inc(S.sem, 1)
                settle(dve)
                for k in range(KT):
                    last = dve.bn_stats(st[:, k, :], src(k))
                done(last)
                dve.wait_ge(S.sem, S.upto(q, "stats"))
                settle(dve)
                for k in range(KT):
                    last = dve.bn_aggr(m[:, k, :], st[:, k, :])
                done(last)
                dve.wait_ge(S.sem, S.upto(q, "aggr"))
                dve.tensor_scalar(ve[:, :], m[:, :, 1], EPS, None, ALU.add)
                done(dve.tensor_scalar(nm[:, :], m[:, :, 0], -1.0, None, ALU.mult))

            def main(g, n):
                par = g.par
                dve.wait_ge(m_bc, g * N + n + 1)
                if n == 0:
                    dve.wait_ge(PRE_DVE.sem, PRE_DVE.upto(g, "w1"))
                for h in range(NH):
                    if g.least(1) or n:
                        dve.wait_ge(m_scan, g * NS + NH * (n - 1) + h + 1)
                    dve.tensor_tensor(dB[h][:, :], wu[par][:, h, :], pB[:, :], ALU.mult).then_inc(m_mul, 1)
                for h in range(NH):
                    s = NH * n + h
                    dve.wait_ge(m_exp, g * NS + s + 1)
                    dve.wait_ge(m_mul, g * NS + s + 1)
                    if g.least(1) or s >= NB:
                        dve.wait_ge(m_sum, g * NS + s - NB + 1)
                    dve.tensor_tensor_scan(hs[s % NB][:, :], dA[s % NA][:, :, :].rearrange("p b t -> p (b t)"), dB[h][:, :], 0.0,
                                           ALU.mult, ALU.add).then_inc(m_scan, 1)

            def nrm_aux(q, slot):
                if slot == 10:
                    dve.wait_ge(s_x, 16 * (q + 1))
                    stats(lambda k: xres[:, bass.ds(q * KT + k, 1), :], stat, mv, veps, nmean, NRM_DVE, q)

            def pre_aux(q, slot):
                par = q.par
                done = lambda i: i.then_inc(PRE_DVE.sem, 1)
                if slot in (2, 3):
                    h = slot - 2
                    dve.wait_ge(PRE_ACT.sem, PRE_ACT.upto(q, f"xh{2 * h + 1}"))
                    for k in range(TAPS - 1):
                        if k:
                            dve.wait_ge(PRE_DVE.sem, PRE_DVE.upto(q, f"conv{h}_{k - 1}"))
                        done(dve.scalar_tensor_tensor(out=acc[:, h, :, :], in0=xhp[:, h, :, k:k + L], scalar=c_cw(h, k),
                                                      in1=acc[:, h, :, :], op0=ALU.mult, op1=ALU.add))
                if slot == 13:
                    for h in range(NH):
                        dve.wait_ge(PRE_ACT.sem, PRE_ACT.upto(q, f"spln{h}"))
                        done(dve.tensor_tensor(dl[par][:, h, :], dl[par][:, h, :], wu[par][:, h, :], ALU.add))
                    for h in range(NH):
                        dve.wait_ge(PRE_DVE.sem, PRE_DVE.upto(q, f"delta{h}"))
                        done(dve.tensor_tensor(wu[par][:, h, :], dl[par][:, h, :], u[par][:, h, :], ALU.mult))

            def post_aux(q, slot):
                par = q.par
                done = lambda i: i.then_inc(POST_DVE.sem, 1)
                own = lambda name: dve.wait_ge(POST_DVE.sem, POST_DVE.upto(q, name))
                row = slice(None)
                here = bass.ds(q * KT, KT)
                if slot == 0:
                    dve.wait_ge(m_sum, (q + 1) * NS)
                    if not q.least(1):
                        dve.wait_ge(s_zero, 16 * 8)
                    if q.least(1):
                        dve.wait_ge(POST_PE.sem, POST_PE.upto(q - 1, "out1"))
                    dve.wait_ge(Z_ACT.sem, Z_ACT.upto(q, "silu"))
                    for h in range(NH):
                        done(dve.scalar_tensor_tensor(out=yz[:, h, :], in0=u[par][:, h, :], scalar=c_D(h), in1=pY[h][:, :],
                                                      op0=ALU.mult, op1=ALU.add))
                    for h in range(NH):
                        own(f"yt{h}")
                        done(dve.tensor_tensor(yz[:, h, :], yz[:, h, :], zs[par][:, h, :], ALU.mult))
                if slot in (3, 4):
                    for c in (slot - 3,):
                        dve.wait_ge(POST_PE.sem, POST_PE.upto(q, f"out{c}"))
                        xs = xres[:, bass.ds(q * KT + 4 * c, 4), :]
                        done(dve.tensor_tensor(xs, xs, bank("POST", f"out{c}").rearrange("p (k d) -> p k d", d=D), ALU.add))
                if slot == 5:
                    own("res1")
                    stats(lambda k: xres[:, bass.ds(q * KT + k, 1), :], stat2, mv2, veps2, nmean2, POST_DVE, q)
                by_expert = lambda name: bank("POST", name)[:, 0:KT * E].rearrange("p (k e) -> p k e", e=E)
                bc = lambda t: t[:, :].unsqueeze(2).to_broadcast([128, KT, E])
                if slot == 11:
                    pL = by_expert("logits")
                    dve.wait_ge(POST_PE.sem, POST_PE.upto(q, "logits"))
                    done(dve.tensor_reduce(mx[:, :], pL, AX.X, ALU.max))
                    own("mx")
                    done(dve.tensor_tensor(lm[:, :, :], pL, bc(mx), ALU.subtract))
                if slot == 13:
                    dve.wait_ge(POST_ACT.sem, POST_ACT.upto(q, "ex"))
                    done(dve.tensor_reduce(sm[:, :], ex[:, :, :], AX.X, ALU.add))
                    own("sm")
                    done(dve.reciprocal(pr[:, :], sm[:, :]))
                    own("lm")
                    done(dve.scalar_tensor_tensor(out=sc[:, :, :], in0=ex[:, :, :], scalar=1.0,
                                                  in1=w8[:, :].unsqueeze(1).to_broadcast([128, KT, E]),
                                                  op0=ALU.is_ge, op1=ALU.mult))
                    own("eq")
                    done(dve.tensor_reduce(ms[:, :], sc[:, :, :], AX.X, ALU.max))
                    own("ms")
                    done(dve.tensor_tensor(oh[:, :, :], sc[:, :, :], bc(ms), ALU.is_equal))
                if slot == 15:
                    dve.wait_ge(POST_PE.sem, POST_PE.upto(q, "cum"))
                    done(dve.tensor_tensor(oc[:, :, :], oh[:, :, :], by_expert("cum"), ALU.mult))
                    own("oc")
                    done(dve.tensor_reduce(rank[:, :], oc[:, :, :], AX.X, ALU.add))
                    done(dve.tensor_scalar(base[:, :], ms[:, :], float(-CAP), float(E * CAP - 1), ALU.mult, ALU.add))
                    own("base")
                    done(dve.tensor_scalar(kept[:, :], rank[:, :], float(CAP), None, ALU.is_le))
                    done(dve.tensor_scalar(lost[:, :], rank[:, :], float(CAP), float(SLOTS), ALU.is_gt, ALU.mult))
                    done(dve.tensor_tensor(srow[:, :], base[:, :], rank[:, :], ALU.add))
                    own("srow")
                    if q.least(1):
                        dve.wait_ge(s_scat, 16 * KT * q)
                    done(dve.tensor_tensor(sidx[:, :], srow[:, :], lost[:, :], ALU.add))
                    done(dve.scalar_tensor_tensor(out=grow[:, :], in0=rank[:, :], scalar=float(CAP), in1=base[:, :],
                                                  op0=ALU.min, op1=ALU.add))
                    own("grow")
                    done(dve.tensor_copy(gidx[:, here], grow[:, :]))
                    done(dve.tensor_tensor(gwt[:, here], pr[:, :], kept[:, :], ALU.mult))
            dve.wait_ge(s_w, 16 * NW)
            dve.wait_ge(s_cst, 1)
            for i in range(2):
                if i:
                    dve.wait_ge(s_bias, 2 * i)
                dve.tensor_copy(bias3[:, :], biasf).then_inc(s_bias, 1)
                dve.wait_ge(s_bias, 2 * i + 1)
                dve.scalar_tensor_tensor(out=biasf, in0=bias3[:, :], scalar=c_row[i], in1=biasf,
                                         op0=ALU.mult, op1=ALU.add).then_inc(s_bias, 1)
            dve.wait_ge(s_bias, 4)
            dve.tensor_copy(bias3[:, :], biasf).then_inc(s_bias, 1)
            run_groups(dve, main, [("POST", post_aux), ("PRE", pre_aux), ("NRM", nrm_aux)])

            def unit(t):
                if not t.least(1):
                    rows_in(t)
                rows_in(t + 1)
                if t.least(1):
                    rows_out(t - 1)

            def rows_in(t):
                dve.wait_ge(e_T, (t + 1) * 1)
                if t.least(2):
                    dve.wait_ge(e_h, (t - 1) * KF)
                dve.tensor_copy(xeT[t.par][:, :], pT[t.par][:, :]).then_inc(e_xT, 1)

            def rows_out(t):
                dve.wait_ge(e_y, (t + 1) * 1)
                if t.least(2):
                    dve.wait_ge(s_ye[t.par], t // 2 * 16)
                dve.tensor_tensor(ye[t.par][:, :, :], pE[t.par][:, :].rearrange("p (k d) -> p k d", d=D),
                                  b2[(t // UE).par][:, :].unsqueeze(1).to_broadcast([128, 4, D]), ALU.add).then_inc(e_add, 1)

            def unit_last(t):
                if t.least(UNITS - 1) and t.reg is None:
                    rows_out(t - 1)
                else:
                    unit(t)
            run_units(dve, unit_last, lambda t: rows_out(t - 1))

            dve.wait_ge(s_w3, 16 * 7)
            dve.tensor_scalar(wg[:, :], gi[:, :], 1.0 / 127.0, None, ALU.mult)
            dve.tensor_scalar(wup[:, :], ui[:, :], 1.0 / 127.0, None, ALU.mult)
            dve.tensor_scalar(wd[:, :, :], di[:, :, :], 1.0 / 127.0, None, ALU.mult)
            dve.tensor_tensor(wk[:, :, :], mask8[:, :].unsqueeze(2).to_broadcast([128, C8, SL]),
                              wkr[:, :].unsqueeze(1).to_broadcast([128, C8, SL]), ALU.mult).then_inc(s_wk, 1)

            def block_stats(S, j, part, tile, st, m, ve, nm):
                done = lambda i: i.then_inc(S.sem, 1)
                for i in range(BQ):
                    last = dve.bn_stats(st[:, i, :], xres[:, tile(i), :])
                done(last)
                dve.wait_ge(S.sem, S.upto(j, "stats" + part))
                for i in range(BQ):
                    last = dve.bn_aggr(m[:, i, :], st[:, i, :])
                done(last)
                dve.wait_ge(S.sem, S.upto(j, "aggr" + part))
                dve.tensor_scalar(ve, m[:, :, 1], EPS, None, ALU.add)
                done(dve.tensor_scalar(nm, m[:, :, 0], -1.0, None, ALU.mult))

            def chunk(j, i):
                dve.wait_ge(s_gx[i], 16 * BQ * (j + 1))
                for l in range(BQ * i, BQ * i + BQ):
                    at_ = TB * l + j
                    last = dve.scalar_tensor_tensor(out=xres[:, at_, :], in0=gx[:, l, :], scalar=gwt[:, at_:at_ + 1],
                                                    in1=xres[:, at_, :], op0=ALU.mult, op1=ALU.add)
                last.then_inc(A_DVE.sem, 1)
                dve.wait_ge(A_DVE.sem, A_DVE.upto(j, f"x2_{i}"))
                if j >= 1:
                    dve.wait_ge(A_POOL.sem, A_POOL.upto(j - 1, f"nmr{i}"))
                four = slice(BQ * i, BQ * i + BQ)
                block_stats(A_DVE, j, str(i), lambda k: TB * (BQ * i + k) + j, stA[:, four, :], mvA[:, four, :], veA[:, four], nmA[:, four])

            def scores(t):
                j, c = t // BQ, t % BQ
                done = lambda i: i.then_inc(T_DVE.sem, 1)
                own = lambda n: dve.wait_ge(T_DVE.sem, T_DVE.upto(t, n))
                dve.wait_ge(A_ACT.sem, A_ACT.upto(j, "k1"))
                if t >= 1:
                    dve.wait_ge(T_DVE.sem, T_DVE.upto(t - 1, "norm"))
                for d in range(QH):
                    qd = q[j % 2][:, BQ * c:BQ * c + BQ, :].rearrange("p l (h d) -> p l h d", d=QH)[:, :, :, d]
                    kd = kk[j % 2][:, HEADS * d:HEADS * d + HEADS, :]
                    done(dve.tensor_tensor(qk[d][:, :, :, :], qd.unsqueeze(3).to_broadcast([128, BQ, HEADS, SL]),
                                           kd.unsqueeze(1).to_broadcast([128, BQ, HEADS, SL]), ALU.mult))
                flat = lambda x_: x_[:, :, :, :].rearrange("p l h s -> p (l h s)")
                own("qk1")
                done(dve.tensor_tensor(flat(qk[0]), flat(qk[0]), flat(qk[1]), ALU.add))
                own("qk3")
                done(dve.tensor_tensor(flat(qk[2]), flat(qk[2]), flat(qk[3]), ALU.add))
                own("s23")
                done(dve.tensor_tensor(flat(qk[0]), flat(qk[0]), flat(qk[2]), ALU.add))
                own("s")
                s_ = qk[0][:, :, :, :].rearrange("p l h s -> p (l h) s")
                done(dve.tensor_reduce(am[:, :], s_, AX.X, ALU.max))
                own("max")
                done(dve.tensor_tensor(at[t % 2][:, :, :], s_, am[:, :].unsqueeze(2).to_broadcast([128, BQ * HEADS, SL]), ALU.subtract))

            def weigh(t, l):
                done = lambda i: i.then_inc(T_DVE.sem, 1)
                own = lambda n: dve.wait_ge(T_DVE.sem, T_DVE.upto(t, n))
                a = at[t % 2]
                if l == 0:
                    dve.wait_ge(A_ACT.sem, A_ACT.upto(t // BQ, "v2"))
                    dve.wait_ge(T_ACT.sem, T_ACT.upto(t, "exp"))
                    done(dve.tensor_reduce(ad[:, :], a[:, :, :], AX.X, ALU.add))
                    own("den")
                    done(dve.reciprocal(ar[:, :], ad[:, :]))
                if l >= 2:
                    own(f"o{l - 2}")
                done(dve.tensor_tensor(pv[l % 2][:, :, :, :],
                                       a[:, HEADS * l:HEADS * l + HEADS, :].unsqueeze(2).to_broadcast([128, HEADS, DV, SL]),
                                       vv[t // BQ % 2][:, :, :].rearrange("p (h v) s -> p h v s", h=HEADS), ALU.mult))
                own(f"pv{l}")
                done(dve.tensor_reduce(oo[t % 2][:, l, :].rearrange("p (v h) -> p h v", h=HEADS), pv[l % 2][:, :, :, :], AX.X, ALU.add))
                if l == BQ - 1:
                    own(f"o{l}")
                    if t >= 2:
                        dve.wait_ge(B_PE.sem, B_PE.upto(t - 2, "oT"))
                    done(dve.tensor_tensor(on[t % 2][:, :, :].rearrange("p l (v h) -> p l v h", h=HEADS),
                                           oo[t % 2][:, :, :].rearrange("p l (v h) -> p l v h", h=HEADS),
                                           ar[:, :].rearrange("p (l h) -> p l h", h=HEADS).unsqueeze(2).to_broadcast([128, BQ, DV, HEADS]), ALU.mult))

            def tiles_of(t):
                j, c = t // BQ, t % BQ
                return xres[:, :, :].rearrange("p (b j) d -> p b j d", j=TB)[:, BQ * c:BQ * c + BQ, j, :]

            def x3(t):
                dve.wait_ge(B_PE.sem, B_PE.upto(t, "proj"))
                dve.tensor_tensor(tiles_of(t), tiles_of(t), pP[:, :].rearrange("p (l d) -> p l d", d=D), ALU.add).then_inc(B_DVE.sem, 1)
                dve.wait_ge(B_DVE.sem, B_DVE.upto(t, "x3"))
                if t >= 1:
                    dve.wait_ge(B_POOL.sem, B_POOL.upto(t - 1, "nmr"))
                block_stats(B_DVE, t, "", lambda i: TB * (BQ * (t % BQ) + i) + t // BQ, stB[:, :, :], mvB[:, :, :], veB[:, :], nmB[:, :])

            def hidden(t, k):
                dve.wait_ge(F_ACT.sem, F_ACT.upto(t, f"silu{k}"))
                dve.wait_ge(F_PE.sem, F_PE.upto(t, f"u{k}"))
                if k == 0 and t >= 1:
                    dve.wait_ge(D_PE.sem, D_PE.upto(t - 1, "down"))
                dve.tensor_tensor(hh[:, k, :], sg[k][:, :], pU[(KH * t + k) % 2][:, :], ALU.mult).then_inc(F_DVE.sem, 1)

            def x4(t):
                dve.wait_ge(D_PE.sem, D_PE.upto(t, "down"))
                dve.tensor_tensor(tiles_of(t), tiles_of(t), pD[:, :].rearrange("p (l d) -> p l d", d=D), ALU.add).then_inc(F_DVE.sem, 1)

            def last_unit(t, row_chunk, jobs):
                if t < TU:
                    scores(t)
                if t >= 3:
                    x4(t - 3)
                if 1 <= t <= TU:
                    x3(t - 1)
                if t >= 2:
                    hidden(t - 2, 0)
                row_chunk(0)
                for l in range(BQ):
                    if t < TU:
                        weigh(t, l)
                    if t >= 2 and l + 1 < KH:
                        hidden(t - 2, l + 1)
                    if l == 1:
                        row_chunk(1)
                if t == TU + 1:
                    x4(t - 2)
            run_last(chunk, lambda j, name: None, last_unit)

        @block.tensor
        def _(pe):
            pe.wait_ge(s_w, 16 * NW)
            pe.wait_ge(s_sel, 3)
            pe.wait_ge(s_bias, 5)

            def bcast(g, n):
                if g.least(1) or n:
                    pe.wait_ge(m_mul, g * NS + NH * n)
                if n == 0:
                    pe.wait_ge(PRE_POOL.sem, PRE_POOL.upto(g, "cast3"))
                for c in range(2):
                    last = pe.matmul(pB[:, c * 512:(c + 1) * 512], sel[:, n, :], Bs[g.par][:, c * 512:(c + 1) * 512],
                                     start=True, stop=True)
                last.then_inc(m_bc, 1)

            def main(g, n):
                if n == 0 and not g.least(1):
                    bcast(g, 0)
                if n + 1 < N:
                    bcast(g, n + 1)
                elif g.reg is not None or g.off + 1 < G:
                    bcast(g + 1, 0)
                for h in range(NH):
                    if n == 0 and g.least(1):
                        pe.wait_ge(POST_DVE.sem, POST_DVE.upto(g - 1, f"yt{h}"))
                    s = NH * n + h
                    pe.wait_ge(m_scan, g * NS + s + 1)
                    for c in range(2):
                        last = pe.matmul(pY[h][:, c * 512:(c + 1) * 512], ident[:, :], hs[s % NB][:, c * 512:(c + 1) * 512],
                                         start=(n == 0), stop=(n == N - 1))
                    last.then_inc(m_sum, 1)

            def job(q, stage, name, emit):
                after(pe, q - AHEAD[stage], stage, name)
                emit(bank(stage, name)).then_inc({"NRM": NRM_PE, "PRE": PRE_PE, "POST": POST_PE}[stage].sem, 1)

            def transposed(src, c):
                def emit(out):
                    for k in range(4):
                        last = pe.transpose(out[:, k * 128:(k + 1) * 128], src[:, 4 * c + k, :], ident[:, :])
                    return last
                return emit

            def projected(w, src, c, rows=128):
                def emit(out):
                    for k in range(len(w)):
                        last = pe.matmul(out[0:rows, :], w[k], src[k][:, c * 512:(c + 1) * 512],
                                         start=(k == 0), stop=(k == len(w) - 1))
                    return last
                return emit

            def nrm_aux(q, slot):
                if slot == 12:
                    pe.wait_ge(NRM_ACT.sem, NRM_ACT.upto(q, "norm"))
                    for c in range(2):
                        job(q, "NRM", f"t{c}", transposed(xn, c))

            def pre_aux(q, slot):
                us = [u[q.par][:, k, :] for k in range(NH)]
                if slot in (0, 1):
                    if slot == 0:
                        pe.wait_ge(NRM_ACT.sem, NRM_ACT.upto(q, "t1"))
                    h = slot
                    for c in range(2):
                        job(q, "PRE", f"xh{2 * h + c}", projected([w_in[:, h * 128:(h + 1) * 128]], [xnT[:, :]], c))
                if slot in (4, 5):
                    h = slot - 4
                    for c in range(2):
                        job(q, "PRE", f"z{2 * h + c}", projected([w_in[:, DI + h * 128:DI + (h + 1) * 128]], [xnT[:, :]], c))
                if slot in (6, 7):
                    if slot == 6:
                        pe.wait_ge(PRE_ACT.sem, PRE_ACT.upto(q, "u1"))
                    job(q, "PRE", f"b{slot - 6}", projected([w_b[:, k, :] for k in range(NH)], us, slot - 6, 96))
                if slot in (8, 9, 10, 11):
                    j = slot - 8
                    h, c = j // 2, j % 2
                    job(q, "PRE", f"dt{j}", projected([w_dt[:, k, h * 128:(h + 1) * 128] for k in range(NH)], us, c))

            def post_aux(q, slot):
                if slot in (2, 3):
                    pe.wait_ge(POST_DVE.sem, POST_DVE.upto(q, "yz1"))
                    for c in (slot - 2,):
                        def emit(out):
                            pe.matmul(out.rearrange("p (k d) -> p k d", d=D), ones3[:, :], three(0, D, 4), start=True, stop=False)
                            for k in range(4):
                                o = out[:, k * 128:(k + 1) * 128]
                                for h in range(NH):
                                    last = pe.matmul(o, yz[:, h, (4 * c + k) * 128:(4 * c + k + 1) * 128], w_out[:, h, :],
                                                     start=False, stop=(k == 3 and h == NH - 1))
                            return last
                        job(q, "POST", f"out{c}", emit)
                if slot in (8, 9):
                    pe.wait_ge(POST_ACT.sem, POST_ACT.upto(q, "norm"))
                    for c in (slot - 8,):
                        job(q, "POST", f"t{c}", transposed(xn2, c))
                if slot == 10:
                    pe.wait_ge(POST_ACT.sem, POST_ACT.upto(q, "t1"))

                    def emit(out):
                        for k in range(KT):
                            last = pe.matmul(out[:, k * E:(k + 1) * E], xn2T[:, k * 128:(k + 1) * 128], rt_w[:, :], start=True, stop=True)
                        return last
                    job(q, "POST", "logits", emit)
                if slot == 14:
                    pe.wait_ge(POST_DVE.sem, POST_DVE.upto(q, "oh"))
                    pe.wait_ge(POST_POOL.sem, POST_POOL.upto(q, f"pre{KT - 1}"))

                    def emit(out):
                        pe.matmul(out[:, 0:KT * E], tri[:, :], oh[:, :, :].rearrange("p k e -> p (k e)"), start=True, stop=False)
                        return pe.matmul(out[:, 0:KT * E], ones[:, :], pre[:, 0:KT, :].rearrange("p k e -> p (k e)"),
                                         start=False, stop=True)
                    job(q, "POST", "cum", emit)
            run_groups(pe, main, [("POST", post_aux), ("PRE", pre_aux), ("NRM", nrm_aux)])

            def unit(t):
                if not t.least(1):
                    turn(t)
                up(t)
                turn(t + 1)
                if t.least(1):
                    down(t - 1)

            def turn(t):
                pe.wait_ge(s_xe[t.par], (t // 2 + 1) * 16)
                if t.least(2):
                    pe.wait_ge(e_xT, (t - 1) * 1)
                for k in range(4):
                    last = pe.transpose(pT[t.par][:, k * 128:(k + 1) * 128], xe[t.par][:, k, :], ident[:, :])
                last.then_inc(e_T, 1)

            def up(t):
                par = (t // UE).par
                pe.wait_ge(e_xT, (t + 1) * 1)
                if t.off % UE == 0:
                    pe.wait_ge(s_we[par], (t // UE // 2 + 1) * 64)
                for k in range(KF):
                    if t.least(1):
                        pe.wait_ge(e_gelu, (t - 1) * KF + k + 1)
                    pe.matmul(pH[k][:, :], w1[par][:, k * 128:(k + 1) * 128], xeT[t.par][:, :], start=True, stop=True).then_inc(e_h, 1)

            def down(t):
                par = (t // UE).par
                pe.wait_ge(e_gelu, (t + 1) * KF)
                if t.least(2):
                    pe.wait_ge(e_add, (t - 1) * 1)
                for i in range(4):
                    for k in range(KF):
                        last = pe.matmul(pE[t.par][:, i * 128:(i + 1) * 128], he[t.par][:, k, i * 128:(i + 1) * 128], w2[par][:, k, :],
                                         start=(k == 0), stop=(k == KF - 1))
                last.then_inc(e_y, 1)

            def unit_last(t):
                if t.least(UNITS - 1) and t.reg is None:
                    up(t)
                    down(t - 1)
                else:
                    unit(t)
            run_units(pe, unit_last, lambda t: down(t - 1))

            pe.wait_ge(s_w3, 16 * 7)
            pe.wait_ge(s_wk, 1)

            def job(j, name):
                i, kind, n = A_JOBS.index(name), name[0], int(name[1])
                o = pA[i % 2]
                if kind == "t":
                    pe.wait_ge(A_NRM.sem, A_NRM.upto(j, f"norm{n}"))
                if i >= 2:
                    pe.wait_ge(A_ACT.sem, A_ACT.upto(j, A_JOBS[i - 2]))
                elif j >= 1:
                    pe.wait_ge(A_ACT.sem, A_ACT.upto(j - 1, A_JOBS[-1]))
                if kind == "t":
                    for m in range(4):
                        last = pe.transpose(o[:, m * 128:(m + 1) * 128], xnA[:, 4 * n + m, :], ident[:, :])
                if kind == "g":
                    for m in range(4):
                        last = pe.transpose(o[:, m * 128:(m + 1) * 128],
                                            xnA[:, :, :].rearrange("p l (c g) -> p g (l c)", c=C8)[:, 4 * n + m, :], ident[:, :])
                if kind == "q":
                    pe.wait_ge(A_ACT.sem, A_ACT.upto(j, f"t{2 * n + 1}"))
                    pe.matmul(o[:, :].rearrange("p (m c) -> p m c", c=QD), ones3[:, :], three(2 * D, QD, 8), start=True, stop=False)
                    for m in range(8):
                        last = pe.matmul(o[:, m * QD:(m + 1) * QD], xnAT[:, 8 * n + m, :], wq[:, :], start=False, stop=(m == 7))
                if kind == "v":
                    if n == 0:
                        pe.wait_ge(A_ACT.sem, A_ACT.upto(j, "g3"))
                    for m in range(min(7, D // C8 - 7 * n)):
                        last = pe.matmul(o[:, m * C8 * SL:(m + 1) * C8 * SL], xnG[:, 7 * n + m, :],
                                         wk[:, :, :].rearrange("p c s -> p (c s)"), start=True, stop=True)
                if kind == "r":
                    if n == 0:
                        pe.wait_ge(A_ACT.sem, A_ACT.upto(j, "q1"))
                    for m in range(4):
                        last = pe.transpose(o[:, m * 128:(m + 1) * 128],
                                            q[j % 2][:, :, :].rearrange("p l (c g) -> p g (l c)", c=C8)[:, 4 * n + m, :], ident[:, :])
                if kind == "k":
                    pe.wait_ge(A_ACT.sem, A_ACT.upto(j, "r1"))
                    for m in range(4):
                        last = pe.matmul(o[:, m * C8 * SL:(m + 1) * C8 * SL], qG[:, 4 * n + m, :],
                                         wk[:, :, :].rearrange("p c s -> p (c s)"), start=True, stop=True)
                last.then_inc(A_PE.sem, 1)

            def turn_o(t):
                pe.wait_ge(T_DVE.sem, T_DVE.upto(t, "norm"))
                if t >= 1:
                    pe.wait_ge(B_ACT.sem, B_ACT.upto(t - 1, "xT"))
                for i in range(BQ):
                    last = pe.transpose(pT3[:, i * 128:(i + 1) * 128], on[t % 2][:, i, :], ident[:, :])
                last.then_inc(B_PE.sem, 1)

            def proj(t):
                pe.wait_ge(B_ACT.sem, B_ACT.upto(t, "oT"))
                if t >= 1:
                    pe.wait_ge(B_DVE.sem, B_DVE.upto(t - 1, "x3"))
                pe.matmul(pP[:, :].rearrange("p (i d) -> p i d", d=D), ones3[:, :], three(D, D, BQ), start=True, stop=False)
                for i in range(BQ):
                    last = pe.matmul(pP[:, i * 128:(i + 1) * 128], oT[:, i * 128:(i + 1) * 128], wo[:, :],
                                     start=False, stop=(i == BQ - 1))
                last.then_inc(B_PE.sem, 1)

            def turn_x(t):
                pe.wait_ge(B_ACT.sem, B_ACT.upto(t, "norm"))
                for i in range(BQ):
                    last = pe.transpose(pT3[:, i * 128:(i + 1) * 128], xnB[:, i, :], ident[:, :])
                last.then_inc(B_PE.sem, 1)

            def gate(t, k):
                if k == 0:
                    pe.wait_ge(B_ACT.sem, B_ACT.upto(t, "xT"))
                if k >= 1 or t >= 1:
                    pe.wait_ge(F_ACT.sem, F_ACT.upto(t - (k == 0), f"silu{(k - 1) % KH}"))
                pe.matmul(pG[:, :], wg[:, k * 128:(k + 1) * 128], xnBT[t % 2][:, :], start=True, stop=True).then_inc(F_PE.sem, 1)

            def up3(t, k):
                if k >= 2 or t >= 1:
                    pe.wait_ge(F_DVE.sem, F_DVE.upto(t - (k < 2), f"h{(k - 2) % KH}"))
                pe.matmul(pU[(KH * t + k) % 2][:, :], wup[:, k * 128:(k + 1) * 128], xnBT[t % 2][:, :],
                          start=True, stop=True).then_inc(F_PE.sem, 1)

            def down3(t):
                pe.wait_ge(F_DVE.sem, F_DVE.upto(t, f"h{KH - 1}"))
                if t >= 1:
                    pe.wait_ge(F_DVE.sem, F_DVE.upto(t - 1, "x4"))
                for i in range(BQ):
                    for k in range(KH):
                        last = pe.matmul(pD[:, i * 128:(i + 1) * 128], hh[:, k, i * 128:(i + 1) * 128], wd[:, k, :],
                                         start=(k == 0), stop=(k == KH - 1))
                last.then_inc(D_PE.sem, 1)

            def last_unit(t, row_chunk, jobs):
                attn, ffn = 1 <= t <= TU, t >= 2
                if attn:
                    turn_o(t - 1)
                if ffn:
                    up3(t - 2, 1)
                if attn:
                    proj(t - 1)
                if ffn:
                    gate(t - 2, 2)
                jobs(0)
                if ffn:
                    up3(t - 2, 2)
                if attn:
                    turn_x(t - 1)
                jobs(1)
                if attn:
                    gate(t - 1, 0)
                    up3(t - 1, 0)
                jobs(2)
                if attn:
                    gate(t - 1, 1)
                if ffn:
                    down3(t - 2)
                jobs(3)
            run_last(lambda j, i: None, job, last_unit)


_NAMES = ["L0_attn_x", "L0_attn_W_in", "L0_attn_W_dt", "L0_attn_W_x", "L0_attn_W_out", "L0_ffn_b1",
          "L0_ffn_w1", "L0_ffn_w2", "L0_ffn_b2"]


def kernel(**inputs):
    import numpy as _np
    import concourse.bacc as _bacc
    from concourse import mybir as _mybir
    from concourse.bass_utils import run_bass_kernel_spmd as _run

    nc = _bacc.Bacc("TRN2", target_bir_lowering=False, num_devices=1)
    a = {k: _np.ascontiguousarray(v) for k, v in inputs.items()}
    put = {n: a[n] for n in _NAMES}
    cont = _np.ascontiguousarray
    by_col = lambda v: v.reshape(-1, 128).T
    b_x = _np.tile(_np.tile(a["L0_attn_b_x"][16:32], 2), 4).reshape(128, 1)
    put["cols"] = cont(_np.concatenate([
        by_col(a["L0_attn_b_in"]), by_col(a["L0_attn_conv_b"]), by_col(a["L0_attn_b_dt"]), by_col(a["L0_attn_D"]), b_x,
        a["L0_attn_conv_w"].reshape(2, 128, 4).transpose(1, 0, 2).reshape(128, 8),
        a["L0_attn_A_log"].reshape(2, 128, 16).transpose(1, 0, 2).reshape(128, 32),
        -(_np.arange(128)[:, None] >= _np.array([32, 64, 1, 2])).astype(_np.float32)], axis=1))
    put["bias3"] = _np.tile(_np.concatenate([a["L0_attn_b_out"], a["L1_attn_b_out"], a["L1_attn_b_q"]]), (3, 1))
    put["router_wT"] = cont(a["L0_ffn_router_w"].T)
    put["b1T"] = cont(a["L0_ffn_b1"].reshape(8, 4, 128).transpose(0, 2, 1))
    put["w_qT"] = cont(a["L1_attn_w_q"].T)
    put["w_outT"] = cont(a["L1_attn_w_out"].T)
    put["wkr"] = cont(_np.repeat(a["L1_attn_w_kv"][0:9, 0:16].T, 8, axis=0))
    put["mask8"] = _np.tile(_np.eye(8, dtype=_np.float32), (16, 1))
    put["w_gateT"] = cont(a["L1_ffn_w_gate"].T)
    put["w_upT"] = cont(a["L1_ffn_w_up"].T)
    put["w_downT"] = cont(a["L1_ffn_w_down"].T)
    P = {n: nc.dram_tensor(f"in_{n}_dram", v.shape, _mybir.dt.from_np(v.dtype), kind="ExternalInput").ap() for n, v in put.items()}
    P["out"] = nc.dram_tensor("out_0_dram", (16, 512, 128), _mybir.dt.float32, kind="ExternalOutput").ap()
    P["n_weights"] = 12
    prog(nc, P)
    r = _run(nc, [{f"in_{n}_dram": v for n, v in put.items()}], core_ids=[0])
    return r.results[0]["out_0_dram"]
```

```python
import concourse.bass as bass
from concourse import mybir
from contextlib import ExitStack


class Steps:

    def __init__(self, sem, names):
        self.sem, self.names, self.per = sem, list(names), len(names)

    def upto(self, group, name):
        return group * self.per + self.names.index(name) + 1


class Group:

    def __init__(self, off, reg=None, stride=2):
        self.off, self.reg, self.stride, self.par = off, reg, stride, off % 2

    def __add__(self, k):
        return Group(self.off + k, self.reg, self.stride)

    def __sub__(self, k):
        return self + -k

    def __mul__(self, k):
        return k * self.off if self.reg is None else self.reg * (self.stride * k) + k * self.off

    __rmul__ = __mul__

    def __floordiv__(self, k):
        return Group(self.off // k, self.reg, self.stride // k)

    def least(self, k):
        return self.off >= k


def prog(nc, P):
    fp32 = mybir.dt.float32
    bf16 = mybir.dt.bfloat16
    i32 = mybir.dt.int32
    u32 = mybir.dt.uint32
    ALU = mybir.AluOpType
    ACT = mybir.ActivationFunctionType
    AX = mybir.AxisListType

    x = P["L0_attn_x"]
    B, L, D = x.shape
    DI = P["L0_attn_W_dt"].shape[0]
    NH = DI // 128
    N = 16
    TOK = B * L
    TILES = TOK // 128
    E, FF = P["L0_ffn_b1"].shape
    CAP = -(-3 * TOK // (2 * E))
    SLOTS = E * CAP
    EPS = 1e-5
    SEQ = 2
    G = B // SEQ
    GT = SEQ * L
    KT = GT // 128
    TAPS = 4
    PAD = TAPS - 1

    HG = P["w_gateT"].shape[1]
    KH, KF = HG // 128, FF // 128
    HEADS = 16
    QD = D // 2
    QH, DV = QD // HEADS, D // HEADS
    SL = B // 2 + 1
    C8 = 8
    TB = L // 128
    BQ = 4

    ctx = ExitStack()
    with ctx:
        here = [ctx]

        def sb(n, s, d=fp32):
            return here[0].enter_context(nc.sbuf_tensor(n, s, d))

        def pb(n, s, d=fp32):
            return here[0].enter_context(nc.psum_tensor(n, s, d))

        def sem(n):
            return ctx.enter_context(nc.semaphore(n))

        slots_in = nc.dram_tensor("slots_in", (SLOTS, D), fp32, kind="Internal").ap()
        slots_out = nc.dram_tensor("slots_out", (SLOTS, D), fp32, kind="Internal").ap()

        xres = sb("xres", [128, TILES, D])
        halfs = sb("halfs", [128, B])
        gidx = sb("gidx", [128, TILES], i32)
        gwt = sb("gwt", [128, TILES])
        ident = sb("ident", [128, 128])
        ones = sb("ones", [128, 128])
        ones3 = sb("ones3", [3, 128], bf16)
        bias3 = sb("bias3", [3, 2 * D + D // 2], bf16)
        three = lambda at, n, times: bias3[:, at:at + n].unsqueeze(1).to_broadcast([3, times, n])

        here[0] = ExitStack()
        NA, NB = 8, 4
        dA = [sb(f"dA{i}", [128, SEQ, L]) for i in range(NA)]
        dB = [sb(f"dB{i}", [128, GT]) for i in range(NH)]
        hs = [sb(f"hs{i}", [128, GT]) for i in range(NB)]
        w_in = sb("w_in", [128, 2 * DI])
        w_dt = sb("w_dt", [128, NH, DI])
        w_b = sb("w_b", [128, NH, 96])
        w_out = sb("w_out", [128, NH, D])
        cols = sb("cols", [128, P["cols"].shape[1]])
        c_bin = lambda c: cols[:, c:c + 1]
        c_cb = lambda h: cols[:, 4 + h:5 + h]
        c_bdt = lambda h: cols[:, 6 + h:7 + h]
        c_D = lambda h: cols[:, 8 + h:9 + h]
        c_bx = cols[:, 10:11]
        c_cw = lambda h, k: cols[:, 11 + TAPS * h + k:12 + TAPS * h + k]
        c_alog = cols[:, 19:19 + NH * N]
        c_row = [cols[0:3, 53 + i:54 + i] for i in range(2)]
        c_cut = [cols[:, 51 + i:52 + i] for i in range(2)]
        rt_w = sb("rt_w", [128, E])
        A = sb("A", [128, NH * N])
        tapb = sb("tapb", [128, NH])
        tri = sb("tri", [128, 128])
        sel = sb("sel", [96, N, 128], bf16)
        half = halfs[:, 0:KT]
        w8 = sb("w8", [128, E])

        stat = sb("stat", [128, KT, 6])
        mv = sb("mv", [128, KT, 2])
        veps = sb("veps", [128, KT])
        nmean = sb("nmean", [128, KT])
        rstd = sb("rstd", [128, KT])
        nmr = sb("nmr", [128, KT])
        xn = sb("xn", [128, KT, D])
        xnT = sb("xnT", [128, GT])
        xhp = sb("xhp", [128, NH, SEQ, PAD + L])
        acc = sb("acc", [128, NH, SEQ, L])
        biasf = acc[0:3, 0, 0, 0:2 * D + D // 2]
        Bf = acc[0:96, 0, :, :].rearrange("p b t -> p (b t)")
        Br = acc[0:96, 1, :, :].rearrange("p b t -> p (b t)")
        u = [sb(f"u{i}", [128, NH, GT]) for i in range(2)]
        zs = [sb(f"zs{i}", [128, NH, GT]) for i in range(2)]
        dl = [sb(f"dl{i}", [128, NH, GT]) for i in range(2)]
        wu = [sb(f"wu{i}", [128, NH, GT]) for i in range(2)]
        Bs = [sb(f"Bs{i}", [96, GT], bf16) for i in range(2)]
        yz = sb("yz", [128, NH, GT])
        zero = yz[:, :, :].rearrange("p h t -> p (h t)")[:, 0:SLOTS // 8 * D // 128]
        stat2 = sb("stat2", [128, KT, 6])
        mv2 = sb("mv2", [128, KT, 2])
        veps2 = sb("veps2", [128, KT])
        nmean2 = sb("nmean2", [128, KT])
        rstd2 = sb("rstd2", [128, KT])
        nmr2 = sb("nmr2", [128, KT])
        xn2 = sb("xn2", [128, KT, D])
        xn2T = xn[:, :, :].rearrange("p k d -> p (k d)")
        mx = sb("mx", [128, KT])
        lm = sb("lm", [128, KT, E])
        ex = sb("ex", [128, KT, E])
        sm = sb("sm", [128, KT])
        pr = sb("pr", [128, KT])
        sc = sb("sc", [128, KT, E])
        ms = sb("ms", [128, KT])
        oh = sb("oh", [128, KT, E])
        pre = sb("pre", [128, KT + 1, E])
        oc = sb("oc", [128, KT, E])
        rank = sb("rank", [128, KT])
        base = sb("base", [128, KT])
        lost = sb("lost", [128, KT])
        kept = sb("kept", [128, KT])
        srow = sb("srow", [128, KT])
        grow = sb("grow", [128, KT])
        sidx = sb("sidx", [128, KT], i32)

        pY = [pb(f"pY{h}", [128, GT]) for h in range(NH)]
        pB = pb("pB", [128, GT])
        pJ = [pb(f"pJ{i}", [128, 512]) for i in range(2)]

        here[0].close()

        here[0] = ctx
        wq = sb("wq", [128, QD])
        wo = sb("wo", [128, D])
        wkr = sb("wkr", [128, SL])
        mask8 = sb("mask8", [128, C8])
        wk = sb("wk", [128, C8, SL])
        gi = sb("gi", [128, HG], i32)
        ui = sb("ui", [128, HG], i32)
        di = sb("di", [128, KH, D], i32)
        wg = sb("wg", [128, HG])
        wup = sb("wup", [128, HG])
        wd = sb("wd", [128, KH, D])

        here[0] = ExitStack()
        w1 = [sb(f"w1{i}", [128, FF]) for i in range(2)]
        w2 = [sb(f"w2{i}", [128, KF, D]) for i in range(2)]
        b1 = [sb(f"b1{i}", [128, KF]) for i in range(2)]
        b2 = [sb(f"b2{i}", [128, D]) for i in range(2)]
        xe = [sb(f"xe{i}", [128, 4, D]) for i in range(2)]
        xeT = [sb(f"xeT{i}", [128, 512]) for i in range(2)]
        he = [sb(f"he{i}", [128, KF, 512]) for i in range(2)]
        ye = [sb(f"ye{i}", [128, 4, D]) for i in range(2)]
        pT = [pb(f"pT{i}", [128, 512]) for i in range(2)]
        pH = [pb(f"pH{i}", [128, 512]) for i in range(KF)]
        pE = [pb(f"pE{i}", [128, 512]) for i in range(2)]
        here[0].close()

        here[0] = ExitStack()
        gx = sb("gx", [128, B, D])
        stA = sb("stA", [128, B, 6])
        mvA = sb("mvA", [128, B, 2])
        veA = sb("veA", [128, B])
        nmA = sb("nmA", [128, B])
        rsA = sb("rsA", [128, B])
        nrA = sb("nrA", [128, B])
        xnA = sb("xnA", [128, B, D])
        xnAT = sb("xnAT", [128, B, 128])
        xnG = sb("xnG", [128, D // C8, 128])
        q = [sb(f"q{i}", [128, B, QD]) for i in range(2)]
        qG = sb("qG", [128, QD // C8, 128])
        kk = [sb(f"kk{i}", [128, QD, SL]) for i in range(2)]
        vv = [sb(f"vv{i}", [128, D, SL]) for i in range(2)]
        qk = [sb(f"qk{i}", [128, BQ, HEADS, SL]) for i in range(QH)]
        at = [sb(f"at{i}", [128, BQ * HEADS, SL]) for i in range(2)]
        am = sb("am", [128, BQ * HEADS])
        ad = sb("ad", [128, BQ * HEADS])
        ar = sb("ar", [128, BQ * HEADS])
        pv = [sb(f"pv{i}", [128, DV, HEADS, SL]) for i in range(BQ)]
        ON_DVE = (0, 3)
        on = [sb(f"on{i}", [128, BQ, D]) for i in range(2)]
        oT = sb("oT", [128, BQ * 128])
        stB = sb("stB", [128, BQ, 6])
        mvB = sb("mvB", [128, BQ, 2])
        veB = sb("veB", [128, BQ])
        nmB = sb("nmB", [128, BQ])
        rsB = sb("rsB", [128, BQ])
        nrB = sb("nrB", [128, BQ])
        xnB = sb("xnB", [128, BQ, D])
        xnBT = [sb(f"xnBT{i}", [128, BQ * 128]) for i in range(2)]
        sg = [sb(f"sg{i}", [128, BQ * 128]) for i in range(KH)]
        hh = sb("hh", [128, KH, BQ * 128])
        pA = [pb(f"pA{i}", [128, 512]) for i in range(2)]
        pO, pT3, pP, pD, pG, pU = (pb(n, [128, 512]) for n in ("pO", "pT3", "pP", "pD", "pG", "pU"))
        here[0].close()
        here[0] = ctx

        s_w = sem("s_w")
        s_passed = sem("s_passed")
        s_x = sem("s_x")
        s_zero = sem("s_zero")
        s_cst = sem("s_cst")
        s_A = sem("s_A")
        s_sel = sem("s_sel")
        s_ident = sem("s_ident")
        s_bias = sem("s_bias")
        s_zr = sem("s_zr")
        s_out = sem("s_out")
        s_scat = sem("s_scat")

        NRM_DVE = Steps(sem("nrm_dve"), ["stats", "aggr", "center"])
        NRM_POOL = Steps(sem("nrm_pool"), ["rstd", "nmr"])
        NRM_ACT = Steps(sem("nrm_act"), ["norm", "t0", "t1"])
        NRM_PE = Steps(sem("nrm_pe"), ["t0", "t1"])
        PRE_DVE = Steps(sem("pre_dve"), [f"conv{h}_{k}" for h in range(NH) for k in range(TAPS - 1)] +
                        ["delta0", "delta1", "w0", "w1"])
        PRE_POOL = Steps(sem("pre_pool"), ["part2", "cut2", "part3", "cast3"])
        PRE_ACT = Steps(sem("pre_act"), ["xh0", "xh1", "xh2", "xh3", "z0", "z1", "z2", "z3", "u0", "u1", "b0", "b1", "cut1",
                                         "dt0", "dt1", "spexp0", "dt2", "dt3", "spexp1", "spln0", "spln1"])
        PRE_PE = Steps(sem("pre_pe"), ["xh0", "xh1", "xh2", "xh3", "z0", "z1", "z2", "z3", "b0", "b1",
                                       "dt0", "dt1", "dt2", "dt3"])
        Z_ACT = Steps(sem("z_act"), ["silu"])
        POST_DVE = Steps(sem("post_dve"), ["yt0", "yt1", "yz0", "yz1", "res0", "res1", "stats", "aggr", "center",
                                           "mx", "lm", "sm", "pr", "eq", "ms", "oh", "oc", "rank",
                                           "base", "kept", "lost", "srow", "sidx", "grow", "gidx", "gw"])
        POST_POOL = Steps(sem("post_pool"), ["rstd", "nmr", "carry"] + [f"pre{k}" for k in range(KT)])
        POST_ACT = Steps(sem("post_act"), ["norm", "t0", "t1", "ex"])
        POST_PE = Steps(sem("post_pe"), ["out0", "out1", "t0", "t1", "logits", "cum"])
        m_exp, m_mul, m_scan, m_bc, m_sum = (sem(n) for n in ("m_exp", "m_mul", "m_scan", "m_bc", "m_sum"))
        NS = NH * N

        UE = CAP // 512
        UNITS = E * UE
        s_we = [sem(f"s_we{i}") for i in range(2)]
        s_xe = [sem(f"s_xe{i}") for i in range(2)]
        s_ye = [sem(f"s_ye{i}") for i in range(2)]
        e_T, e_xT, e_h, e_gelu, e_y, e_add = (sem(n) for n in ("e_T", "e_xT", "e_h", "e_gelu", "e_y", "e_add"))

        s_w3 = sem("s_w3")
        s_wk = sem("s_wk")
        s_gx = [sem(f"s_gx{i}") for i in range(B // BQ)]
        s_fin = sem("s_fin")
        A_JOBS = "t0 t1 q0 t2 t3 q1 r0 r1 k0 k1 g0 g1 g2 g3 v0 v1 v2".split()
        A_DVE = Steps(sem("a_dve"), [f"{n}{i}" for i in range(B // BQ) for n in ("x2_", "stats", "aggr", "center")])
        A_POOL = Steps(sem("a_pool"), [f"{n}{i}" for i in range(B // BQ) for n in ("rstd", "nmr")])
        A_NRM = Steps(sem("a_nrm"), [f"norm{i}" for i in range(B // BQ)])
        A_ACT = Steps(sem("a_act"), A_JOBS)
        A_PE = Steps(sem("a_pe"), A_JOBS)
        T_DVE = Steps(sem("t_dve"), [f"qk{d}" for d in range(QH)] + ["s01", "s23", "s", "max", "sub", "den", "rden"] +
                      ["an"] + [n + str(l) for l in range(BQ) for n in ("pv", "o") if n == "pv" or l in ON_DVE])
        O_PE = Steps(sem("o_pe"), [f"o{l}" for l in range(BQ)])
        T_ACT = Steps(sem("t_act"), ["exp"])
        B_DVE = Steps(sem("b_dve"), ["stats", "aggr", "center"])
        B_POOL = Steps(sem("b_pool"), ["rstd", "nmr"])
        B_ACT = Steps(sem("b_act"), ["oT", "norm", "x3", "xT"])
        B_PE = Steps(sem("b_pe"), ["proj", "xT"])
        F_PE = Steps(sem("f_pe"), ["g0", "u0", "g1", "g2", "u1", "u2"])
        D_PE = Steps(sem("d_pe"), ["down"])
        F_ACT = Steps(sem("f_act"), [f"silu{k}" for k in range(KH)])
        F_DVE = Steps(sem("f_dve"), [f"h{k}" for k in range(KH)])
        X_ACT = Steps(sem("x_act"), ["x4"])
        TU = B // BQ * TB

        def run_units(eng, unit, last):
            body = 2 * UE
            for k in range(body):
                unit(Group(k))
            with eng.Fori(0, UNITS // body - 2) as i:
                for k in range(body):
                    unit(Group(body + k, i, body))
            for k in range(UNITS - body, UNITS):
                unit(Group(k))
            last(Group(UNITS))

        A_PLACES = [["", "", "t0 t1", "q0 t2 t3"], ["q1", "r0 r1", "k0 k1", "g0 g1"], ["g2 g3", "v0", "", ""], ["v1", "v2", "", ""]]

        def run_last(chunk, job, unit, rows_ahead=0):
            for i in range(B // BQ):
                chunk(0, i)
                for name in ["t0", "t1 q0", "t2", "t3"][i].split():
                    job(0, name)
            for i in range(rows_ahead):
                chunk(1, i)
            for name in A_JOBS[A_JOBS.index("q1"):-2]:
                job(0, name)

            def places(t):
                nxt, c = t // BQ + 1, t % BQ

                def row_chunk(i):
                    if t == 0:
                        for k in (2 * i, 2 * i + 1):
                            if k >= rows_ahead:
                                chunk(1, k)
                    if nxt + 1 < TB and c >= 2:
                        chunk(nxt + 1, 2 * (c - 2) + i)

                def jobs(place):
                    if t == 0 and place == 0:
                        for name in A_JOBS[-2:]:
                            job(0, name)
                    if nxt < TB:
                        for name in A_PLACES[c][place].split():
                            job(nxt, name)
                return row_chunk, jobs

            for t in range(TU + 2):
                unit(t, *places(t))

        NW = P["n_weights"]
        block = ctx.enter_context(nc.Block())

        def tiles_of(t):
            j, c = t // BQ, t % BQ
            return xres[:, :, :].rearrange("p (b j) d -> p b j d", j=TB)[:, BQ * c:BQ * c + BQ, j, :]

        def tiles(ap):
            return ap.rearrange("b (j p) d -> p (b j) d", p=128)

        pre_job = lambda name, at: ("PRE", name, at, PRE_ACT, name)
        JOBS = [pre_job("xh0", 0), pre_job("xh1", 1), pre_job("xh2", 0), pre_job("xh3", 1),
                ("POST", "out0", 0, POST_DVE, "res0"), pre_job("z0", 1), pre_job("z1", 1), pre_job("z2", 1),
                ("POST", "out1", 1, POST_DVE, "res1"), pre_job("z3", 0),
                pre_job("b0", 0), pre_job("b1", 1), pre_job("dt0", 1),
                ("POST", "t0", 0, POST_ACT, "t0"), ("POST", "t1", 0, POST_ACT, "t1"), pre_job("dt1", 1),
                ("POST", "logits", 0, POST_DVE, "lm"), pre_job("dt2", 1), pre_job("dt3", 1),
                ("NRM", "t0", 0, NRM_ACT, "t0"), ("NRM", "t1", 1, NRM_ACT, "t1"),
                ("POST", "cum", 0, POST_DVE, "oc")]
        AHEAD = {"POST": -1, "PRE": 1, "NRM": 2, "Z": 0}
        JOB_AT = {(j[0], j[1]): i for i, j in enumerate(JOBS)}

        def bank(stage, name):
            return pJ[JOBS[JOB_AT[stage, name]][2]][:, :]

        def after(eng, period, stage, name):
            at = JOB_AT[stage, name]
            back = [(period, j) for j in JOBS[:at][::-1]] + [(period - 1, j) for j in JOBS[::-1]] + [(period - 2, j) for j in JOBS[::-1]] + [(period - 3, j) for j in JOBS[::-1]]
            for p, j in back:
                q = p + AHEAD[j[0]]
                exists = q.off >= 0 and (p.reg is not None or q.off < G)
                if j[2] == JOBS[at][2] and exists:
                    eng.wait_ge(j[3].sem, j[3].upto(q, j[4]))
                    return

        def settle(eng):
            eng.sem_inc(s_passed, 1)

        def run_groups(eng, main, stages, lead=0, early=()):
            def period(g):
                for n in range(N):
                    for stage, aux in early:
                        q = g + AHEAD[stage]
                        if q.off >= 0 and (q.reg is not None or q.off < G):
                            aux(q, n)
                    at = g + (n + lead) // N
                    if main and (at.reg is not None or 0 <= at.off < G):
                        main(at, (n + lead) % N)
                    for stage, aux in stages:
                        q = g + AHEAD[stage]
                        if q.off >= 0 and (q.reg is not None or q.off < G):
                            aux(q, n)

            for g in range(-2, 2):
                period(Group(g))
            with eng.Fori(0, (G - 4) // 2) as pair:
                period(Group(2, pair))
                period(Group(3, pair))
            for g in range(G - 2, G + 1):
                period(Group(g))

        @block.sync
        def _(sp):
            sp.dma_start(xres[:, 0:KT, :], tiles(x)[:, 0:KT, :]).then_inc(s_x, 16)
            sp.dma_start(cols[:, :], P["cols"]).then_inc(s_w, 16)
            sp.dma_start(w_in[:, :], P["L0_attn_W_in"]).then_inc(s_w, 16)
            sp.dma_start(w_dt[:, :, :], P["L0_attn_W_dt"].rearrange("(k p) n -> p k n", p=128)).then_inc(s_w, 16)
            for c in range(3):
                sp.dma_start(w_b[:, :, 32 * c:32 * c + N],
                             P["L0_attn_W_x"][:, N:2 * N].rearrange("(k p) n -> p k n", p=128)).then_inc(s_w, 16)
                sp.dma_start(w_b[:, :, 32 * c + N:32 * c + 2 * N],
                             P["L0_attn_W_x"][:, N:2 * N].rearrange("(k p) n -> p k n", p=128)).then_inc(s_w, 16)
            sp.dma_start(w_out[:, :, :], P["L0_attn_W_out"].rearrange("(k p) n -> p k n", p=128)).then_inc(s_w, 16)
            sp.dma_start(biasf, P["bias3"]).then_inc(s_w, 16)
            sp.dma_start(rt_w[:, :], P["router_wT"]).then_inc(s_w, 16)
            with sp.Fori(1, G) as g:
                sp.wait_ge(s_x, 16 * g)
                sp.dma_start(xres[:, bass.ds(g * KT, KT), :], tiles(x)[:, bass.ds(g * KT, KT), :]).then_inc(s_x, 16)
            sp.wait_ge(s_zr, 1)
            for k in range(8):
                sp.dma_start(slots_in[k * (SLOTS // 8):(k + 1) * (SLOTS // 8), :].rearrange("(p r) d -> p (r d)", p=128),
                             zero).then_inc(s_zero, 16)
            sp.wait_ge(m_scan, G * NS)
            sp.wait_ge(m_sum, G * NS)

            def weights(e):
                par = e.par
                if e.least(2):
                    sp.wait_ge(e_add, (e - 1) * UE)
                one = lambda n: P[n][bass.ds(e * 1, 1)]
                sp.dma_start(w1[par][:, :], one("L0_ffn_w1").rearrange("a d f -> d (a f)")).then_inc(s_we[par], 16)
                sp.dma_start(w2[par][:, :, :], one("L0_ffn_w2").rearrange("a (k p) d -> p (a k) d", p=128)).then_inc(s_we[par], 16)
                sp.dma_start(b1[par][:, :], one("b1T").rearrange("a p k -> p (a k)")).then_inc(s_we[par], 16)
                sp.dma_start(b2[par][:, :], one("L0_ffn_b2").to_broadcast([128, D])).then_inc(s_we[par], 16)

            def load(t):
                if t.least(2):
                    sp.wait_ge(e_T, (t - 2) * 1 + 1)
                sp.dma_start(xe[t.par][:, :, :], slots_in[bass.ds(t * 512, 512), :].rearrange("(k p) d -> p k d", p=128)
                             ).then_inc(s_xe[t.par], 16)

            def unit(t):
                load(t)
                if t.off % UE == 2 and (t.reg is not None or t.off < UNITS - UE):
                    weights(t // UE + 1)
            weights(Group(0))
            load_w3 = [(wq, "w_qT"), (wo, "w_outT"), (wkr, "wkr"), (mask8, "mask8"), (gi, "w_gateT"), (ui, "w_upT")]
            for dst, name in load_w3:
                sp.dma_start(dst[:, :], P[name]).then_inc(s_w3, 16)
            sp.dma_start(di[:, :, :], P["w_downT"].rearrange("(k p) d -> p k d", p=128)).then_inc(s_w3, 16)
            sp.wait_ge(s_scat, 16 * TILES)
            run_units(sp, unit, lambda t: None)
            for t in range(TU):
                j, c = t // BQ, t % BQ
                sp.wait_ge(X_ACT.sem, X_ACT.upto(t, "x4"))
                sp.dma_start(P["out"][BQ * c:BQ * c + BQ, 128 * j:128 * j + 128, :].rearrange("b p d -> p b d"), tiles_of(t)).then_inc(s_out, 16)
            sp.wait_ge(s_out, 16 * TU)

        @block.gpsimd
        def _(pool):
            pool.memset(ident[:, :], 0.0)
            pool.memset(tri[:, :], 1.0)
            pool.memset(ones[:, :], 1.0)
            pool.memset(ones3[:, :], 1.0)
            pool.memset(halfs[:, :], -0.5)
            pool.memset(sel[:, :, :], 0.0)
            pool.memset(pre[:, :, :], 0.0)
            for h in range(NH):
                pool.memset(xhp[:, h, :, 0:PAD], 0.0)
            for b in range(NA):
                pool.memset(dA[b][:, :, 0:1], 0.0)
            pool.iota(w8[:, :], pattern=[[-1, E]], base=E, channel_multiplier=0,
                      allow_small_or_imprecise_dtypes=True).then_inc(s_cst, 1)
            pool.memset(zero, 0.0).then_inc(s_zr, 1)
            pool.wait_ge(s_cst, 1)
            pool.affine_select(out=ident[:, :], in_=ident[:, :], compare_op=ALU.not_equal, fill=1.0,
                               base=0, pattern=[[-1, 128]], channel_multiplier=1)
            pool.affine_select(out=tri[:, :], in_=tri[:, :], compare_op=ALU.is_ge, fill=0.0,
                               base=0, pattern=[[1, 128]], channel_multiplier=-1).then_inc(s_ident, 1)

            def nrm_aux(q, slot):
                if slot == 10:
                    pool.wait_ge(NRM_DVE.sem, NRM_DVE.upto(q, "center"))
                    pool.tensor_tensor(rstd[:, :], veps[:, :], half, ALU.pow).then_inc(NRM_POOL.sem, 1)
                    pool.wait_ge(NRM_POOL.sem, NRM_POOL.upto(q, "rstd"))
                    pool.tensor_tensor(nmr[:, :], nmean[:, :], rstd[:, :], ALU.mult).then_inc(NRM_POOL.sem, 1)
                if slot == 10 and not q.least(1):
                    for c in range(3):
                        if c:
                            pool.wait_ge(s_sel, c)
                        last = pool.affine_select(out=sel[:, :, :], in_=sel[:, :, :], compare_op=ALU.not_equal, fill=1.0,
                                                  base=-32 * c, pattern=[[-1, N], [0, 128]], channel_multiplier=1)
                        last.then_inc(s_sel, 1)

            def pre_aux(q, slot):
                if slot == 6:
                    own = lambda name: pool.wait_ge(PRE_POOL.sem, PRE_POOL.upto(q, name))
                    done = lambda i: i.then_inc(PRE_POOL.sem, 1)
                    bs = Bs[q.par]
                    pool.wait_ge(PRE_ACT.sem, PRE_ACT.upto(q, "cut1"))
                    done(pool.tensor_tensor(Br, Bf, bs[:, :], ALU.add))
                    own("part2")
                    settle(pool)
                    done(pool.tensor_scalar(bs[:, :], Br, c_cut[1][0:96], None, ALU.mult))
                    own("cut2")
                    done(pool.tensor_tensor(Br, Br, bs[:, :], ALU.add))
                    own("part3")
                    settle(pool)
                    done(pool.tensor_copy(bs[:, :], Br))

            def post_aux(q, slot):
                if slot == 5:
                    pool.wait_ge(POST_DVE.sem, POST_DVE.upto(q, "center"))
                    pool.tensor_tensor(rstd2[:, :], veps2[:, :], half, ALU.pow).then_inc(POST_POOL.sem, 1)
                    pool.wait_ge(POST_POOL.sem, POST_POOL.upto(q, "rstd"))
                    pool.tensor_tensor(nmr2[:, :], nmean2[:, :], rstd2[:, :], ALU.mult).then_inc(POST_POOL.sem, 1)
                if slot == 13:
                    pool.wait_ge(POST_DVE.sem, POST_DVE.upto(q, "oh"))
                    if q.least(1):
                        pool.wait_ge(POST_PE.sem, POST_PE.upto(q - 1, "cum"))
                        pool.wait_ge(POST_POOL.sem, POST_POOL.upto(q - 1, f"pre{KT - 1}"))
                    settle(pool)
                    pool.tensor_copy(pre[:, 0, :], pre[:, KT, :]).then_inc(POST_POOL.sem, 1)
                    for k in range(KT):
                        pool.wait_ge(POST_POOL.sem, POST_POOL.upto(q, f"pre{k - 1}" if k else "carry"))
                        pool.tensor_tensor(pre[:, k + 1, :], pre[:, k, :], oh[:, k, :], ALU.add).then_inc(POST_POOL.sem, 1)
                if slot == 15:
                    if not q.least(1):
                        pool.wait_ge(s_zero, 16 * 8)
                    pool.wait_ge(POST_ACT.sem, POST_ACT.upto(q, "norm"))
                    pool.wait_ge(POST_DVE.sem, POST_DVE.upto(q, "sidx"))
                    settle(pool)
                    for k in range(KT):
                        pool.indirect_dma_start(out=slots_in, out_offset=bass.IndirectOffsetOnAxis(ap=sidx[:, k:k + 1], axis=0),
                                                in_=xn2[:, k, :], in_offset=None,
                                                bounds_check=SLOTS - 1, oob_is_err=False).then_inc(s_scat, 16)
            run_groups(pool, None, [("POST", post_aux), ("PRE", pre_aux), ("NRM", nrm_aux)])

            def unit(t):
                if t.least(1):
                    store(t - 1)

            def store(t):
                pool.wait_ge(e_add, (t + 1) * 1)
                settle(pool)
                pool.dma_start(slots_out[bass.ds(t * 512, 512), :].rearrange("(k p) d -> p k d", p=128),
                               ye[t.par][:, :, :]).then_inc(s_ye[t.par], 16)
            run_units(pool, unit, lambda t: store(t - 1))

            pool.wait_ge(s_ye[0], 16 * (UNITS // 2))
            pool.wait_ge(s_ye[1], 16 * (UNITS // 2))

            def gather(j, i):
                if j >= 1:
                    pool.wait_ge(A_DVE.sem, A_DVE.upto(j - 1, f"x2_{i}"))
                for l in range(BQ * i, BQ * i + BQ):
                    pool.indirect_dma_start(out=gx[:, l, :], out_offset=None, in_=slots_out,
                                            in_offset=bass.IndirectOffsetOnAxis(ap=gidx[:, TB * l + j:TB * l + j + 1], axis=0),
                                            bounds_check=SLOTS - 1, oob_is_err=False).then_inc(s_gx[i], 16)

            def chunk(j, i):
                four = slice(BQ * i, BQ * i + BQ)
                pool.wait_ge(A_DVE.sem, A_DVE.upto(j, f"center{i}"))
                if j >= 1:
                    pool.wait_ge(A_NRM.sem, A_NRM.upto(j - 1, f"norm{i}"))
                pool.tensor_tensor(rsA[:, four], veA[:, four], halfs[:, four], ALU.pow).then_inc(A_POOL.sem, 1)
                pool.wait_ge(A_POOL.sem, A_POOL.upto(j, f"rstd{i}"))
                pool.tensor_tensor(nrA[:, four], nmA[:, four], rsA[:, four], ALU.mult).then_inc(A_POOL.sem, 1)
                if j == 0:
                    if i < 2:
                        gather(0, i + 2)
                    if i == 3:
                        for k in range(4):
                            gather(1, k)
                elif j < TB - 1:
                    gather(j + 1, i)

            def norm_b(t):
                pool.wait_ge(B_DVE.sem, B_DVE.upto(t, "center"))
                pool.tensor_tensor(rsB[:, :], veB[:, :], halfs[:, 0:BQ], ALU.pow).then_inc(B_POOL.sem, 1)
                pool.wait_ge(B_POOL.sem, B_POOL.upto(t, "rstd"))
                pool.tensor_tensor(nrB[:, :], nmB[:, :], rsB[:, :], ALU.mult).then_inc(B_POOL.sem, 1)

            def last_unit(t, row_chunk, jobs):
                if 1 <= t <= TU:
                    norm_b(t - 1)
                row_chunk(0)
                row_chunk(1)
            gather(0, 0)
            gather(0, 1)
            run_last(chunk, lambda j, name: None, last_unit)

        @block.scalar
        def _(act):
            act.wait_ge(s_w, 16 * NW)
            act.activation(A[:, :], c_alog, ACT.Exp).then_inc(s_A, 1)
            act.wait_ge(s_A, 1)
            act.mul(A[:, :], A[:, :], -1.0)
            for h in range(NH):
                last = act.mul(tapb[:, h:h + 1], c_bin(h), c_cw(h, TAPS - 1))
            last.then_inc(s_A, 1)
            act.wait_ge(s_A, 2)
            act.wait_ge(s_cst, 1)

            def main(g, n):
                for h in range(NH):
                    s = NH * n + h
                    if s == 0:
                        act.wait_ge(PRE_DVE.sem, PRE_DVE.upto(g, "delta1"))
                    if g.least(1) or s >= NA:
                        act.wait_ge(m_scan, g * NS + s - NA + 1)
                    act.activation(dA[s % NA][:, :, 1:L], dl[g.par][:, h, :].rearrange("p (b t) -> p b t", b=SEQ)[:, :, 1:L],
                                   ACT.Exp, scale=A[:, N * h + n:N * h + n + 1]).then_inc(m_exp, 1)

            def nrm_aux(q, slot):
                done = lambda i: i.then_inc(NRM_ACT.sem, 1)
                if slot == 12:
                    act.wait_ge(NRM_POOL.sem, NRM_POOL.upto(q, "nmr"))
                    if q.least(3):
                        act.wait_ge(POST_PE.sem, POST_PE.upto(q - 3, "logits"))
                    for k in range(KT):
                        last = act.activation(xn[:, k, :], xres[:, bass.ds(q * KT + k, 1), :], ACT.Identity,
                                              bias=nmr[:, k:k + 1], scale=rstd[:, k:k + 1])
                    done(last)
                if slot == 14:
                    for c in range(2):
                        act.wait_ge(NRM_PE.sem, NRM_PE.upto(q, f"t{c}"))
                        if q.least(1):
                            act.wait_ge(PRE_PE.sem, PRE_PE.upto(q - 1, "z3"))
                        done(act.copy(xnT[:, c * 512:(c + 1) * 512], bank("NRM", f"t{c}")))

            def z_aux(q, slot):
                if slot == 3:
                    act.wait_ge(PRE_ACT.sem, PRE_ACT.upto(q, "z3"))
                    act.activation(zs[q.par][:, :, :], zs[q.par][:, :, :], ACT.Silu).then_inc(Z_ACT.sem, 1)

            def pre_aux(q, slot):
                par = q.par
                done = lambda i: i.then_inc(PRE_ACT.sem, 1)
                if slot in (0, 1):
                    if slot == 0 and not q.least(1):
                        act.wait_ge(s_bias, 5)
                    if slot == 0 and q.least(1):
                        act.wait_ge(PRE_POOL.sem, PRE_POOL.upto(q - 1, "cast3"))
                    for j in (2 * slot, 2 * slot + 1):
                        h, c = j // 2, j % 2
                        act.wait_ge(PRE_PE.sem, PRE_PE.upto(q, f"xh{j}"))
                        act.activation(xhp[:, h, c, PAD:PAD + L], bank("PRE", f"xh{j}"), ACT.Identity, bias=c_bin(h))
                        done(act.activation(acc[:, h, c, :], bank("PRE", f"xh{j}"), ACT.Identity, bias=tapb[:, h:h + 1],
                                            scale=c_cw(h, TAPS - 1)))
                for j in {1: [0], 2: [1, 2], 3: [3]}.get(slot, []):
                    if j == 0 and q.least(2):
                        act.wait_ge(POST_DVE.sem, POST_DVE.upto(q - 2, "yz1"))
                    h, c = j // 2, j % 2
                    act.wait_ge(PRE_PE.sem, PRE_PE.upto(q, f"z{j}"))
                    done(act.activation(zs[par][:, h, c * 512:(c + 1) * 512], bank("PRE", f"z{j}"), ACT.Identity, bias=c_bin(2 + h)))
                if slot == 3:
                    act.wait_ge(PRE_DVE.sem, PRE_DVE.upto(q, f"conv{NH - 1}_{TAPS - 2}"))
                    for h in range(NH):
                        done(act.activation(u[par][:, h, :].rearrange("p (b t) -> p b t", b=SEQ), acc[:, h, :, :],
                                            ACT.Silu, bias=c_cb(h)))

                def b_out(c):
                    act.wait_ge(PRE_PE.sem, PRE_PE.upto(q, f"b{c}"))
                    done(act.activation(Bf[:, c * 512:(c + 1) * 512], bank("PRE", f"b{c}")[0:96, :], ACT.Identity, bias=c_bx[0:96]))

                def dt_out(j):
                    h, c = j // 2, j % 2
                    act.wait_ge(PRE_PE.sem, PRE_PE.upto(q, f"dt{j}"))
                    act.activation(dl[par][:, h, c * 512:(c + 1) * 512], bank("PRE", f"dt{j}"), ACT.Abs, bias=c_bdt(h))
                    done(act.activation(wu[par][:, h, c * 512:(c + 1) * 512], bank("PRE", f"dt{j}"), ACT.Relu, bias=c_bdt(h)))

                def softplus(h, func, scale, bias, wait):
                    d = dl[par][:, h, :]
                    act.wait_ge(PRE_ACT.sem, PRE_ACT.upto(q, wait))
                    done(act.activation(d, d, func, scale=scale, bias=bias))
                if slot == 4:
                    act.wait_ge(PRE_ACT.sem, PRE_ACT.upto(q, "u1"))
                    b_out(0)
                if slot == 5:
                    b_out(1)
                    act.wait_ge(PRE_ACT.sem, PRE_ACT.upto(q, "b1"))
                    if q.least(2):
                        act.wait_ge(m_bc, (q - 1) * N)
                    done(act.activation(Bs[par][:, :], Bf, ACT.Copy, scale=c_cut[0][0:96]))
                if slot == 7:
                    if q.least(2):
                        act.wait_ge(m_mul, (q - 1) * NS)
                    dt_out(0)
                if slot == 10:
                    dt_out(1)
                    softplus(0, ACT.Exp, -1.0, 0.0, "dt1")
                if slot == 11:
                    dt_out(2)
                if slot == 12:
                    dt_out(3)
                    softplus(1, ACT.Exp, -1.0, 0.0, "dt3")
                    for h in range(NH):
                        softplus(h, ACT.Ln, 1.0, 1.0, f"spexp{h}")

            def post_aux(q, slot):
                done = lambda i: i.then_inc(POST_ACT.sem, 1)
                if slot == 6:
                    act.wait_ge(POST_POOL.sem, POST_POOL.upto(q, "nmr"))
                    if q.least(1):
                        act.wait_ge(s_scat, 16 * KT * q)
                    for k in range(KT):
                        last = act.activation(xn2[:, k, :], xres[:, bass.ds(q * KT + k, 1), :], ACT.Identity,
                                              bias=nmr2[:, k:k + 1], scale=rstd2[:, k:k + 1])
                    done(last)
                if slot in (8, 9):
                    for c in (slot - 8,):
                        act.wait_ge(POST_PE.sem, POST_PE.upto(q, f"t{c}"))
                        done(act.copy(xn2T[:, c * 512:(c + 1) * 512], bank("POST", f"t{c}")))
                if slot == 12:
                    act.wait_ge(POST_DVE.sem, POST_DVE.upto(q, "lm"))
                    done(act.activation(ex[:, :, :], lm[:, :, :], ACT.Exp))
            run_groups(act, main, [("POST", post_aux), ("PRE", pre_aux), ("Z", z_aux), ("NRM", nrm_aux)], lead=2)

            def unit(t):
                if t.off % UE == 0:
                    act.wait_ge(s_we[(t // UE).par], (t // UE // 2 + 1) * 64)
                if t.least(2):
                    act.wait_ge(e_y, (t - 1) * 1)
                for k in range(KF):
                    act.wait_ge(e_h, t * KF + k + 1)
                    act.activation(he[t.par][:, k, :], pH[k][:, :], ACT.Gelu,
                                   bias=b1[(t // UE).par][:, k:k + 1]).then_inc(e_gelu, 1)
            run_units(act, unit, lambda t: None)

            def chunk(j, i):
                act.wait_ge(A_POOL.sem, A_POOL.upto(j, f"nmr{i}"))
                for l in range(BQ * i, BQ * i + BQ):
                    last = act.activation(xnA[:, l, :], xres[:, TB * l + j, :], ACT.Identity,
                                          bias=nrA[:, l:l + 1], scale=rsA[:, l:l + 1])
                last.then_inc(A_NRM.sem, 1)

            def job(j, name):
                kind, n = name[0], int(name[1])
                four = slice(4 * n, 4 * n + 4)
                scale, size = 1.0, 512
                if kind == "t":
                    dst = xnAT[:, four, :].rearrange("p l b -> p (l b)")
                if kind == "g":
                    dst = xnG[:, four, :].rearrange("p l b -> p (l b)")
                if kind == "q":
                    dst = q[j % 2][:, 8 * n:8 * n + 8, :].rearrange("p l c -> p (l c)")
                if kind == "r":
                    dst = qG[:, four, :].rearrange("p g b -> p (g b)")
                if kind == "v":
                    w = min(7 * C8, D - 7 * C8 * n)
                    dst, size = vv[j % 2][:, 7 * C8 * n:7 * C8 * n + w, :].rearrange("p c s -> p (c s)"), w * SL
                if kind == "k":
                    dst = kk[j % 2][:, :, :].rearrange("p (c g) s -> p g c s", c=C8)[:, four, :, :]
                    scale, size = float(DV) ** -0.5, 32 * SL
                act.wait_ge(A_PE.sem, A_PE.upto(j, name))
                if name == "q0" and j >= 2:
                    act.wait_ge(T_DVE.sem, T_DVE.upto(BQ * (j - 1) - 1, T_DVE.names[-1]))
                src = pA[A_JOBS.index(name) % 2][:, 0:size]
                if kind == "k":
                    src = src.rearrange("p (g c s) -> p g c s", c=C8, s=SL)
                act.activation(dst, src, ACT.Copy, scale=scale).then_inc(A_ACT.sem, 1)

            def exp(t):
                act.wait_ge(T_DVE.sem, T_DVE.upto(t, "sub"))
                act.activation(at[t % 2][:, :, :], at[t % 2][:, :, :], ACT.Exp).then_inc(T_ACT.sem, 1)

            def turned(t):
                act.wait_ge(O_PE.sem, O_PE.upto(t, f"o{BQ - 1}"))
                act.copy(oT[:, :], pO[:, :]).then_inc(B_ACT.sem, 1)

            def norm(t):
                act.wait_ge(B_POOL.sem, B_POOL.upto(t, "nmr"))
                for i in range(BQ):
                    last = act.activation(xnB[:, i, :], pP[:, i * D:(i + 1) * D], ACT.Identity, bias=nrB[:, i:i + 1], scale=rsB[:, i:i + 1])
                last.then_inc(B_ACT.sem, 1)
                act.wait_ge(B_PE.sem, B_PE.upto(t, "proj"))
                act.copy(tiles_of(t), pP[:, :].rearrange("p (l d) -> p l d", d=D)).then_inc(B_ACT.sem, 1)

            def x4(t):
                act.wait_ge(D_PE.sem, D_PE.upto(t, "down"))
                act.copy(tiles_of(t), pD[:, :].rearrange("p (l d) -> p l d", d=D)).then_inc(X_ACT.sem, 1)

            def norm_turned(t):
                act.wait_ge(B_PE.sem, B_PE.upto(t, "xT"))
                act.copy(xnBT[t % 2][:, :], pT3[:, :]).then_inc(B_ACT.sem, 1)

            def silu(t, k):
                act.wait_ge(F_PE.sem, F_PE.upto(t, f"g{k}"))
                if t >= 1:
                    act.wait_ge(F_DVE.sem, F_DVE.upto(t - 1, f"h{k}"))
                act.activation(sg[k][:, :], pG[:, :], ACT.Silu).then_inc(F_ACT.sem, 1)

            def last_unit(t, row_chunk, jobs):
                attn = 1 <= t <= TU
                if attn:
                    turned(t - 1)
                if t >= 2:
                    silu(t - 2, 2)
                if t < TU:
                    exp(t)
                if t >= 3:
                    x4(t - 3)
                if attn:
                    norm(t - 1)
                jobs(0)
                row_chunk(0)
                if attn:
                    norm_turned(t - 1)
                jobs(1)
                if attn:
                    silu(t - 1, 0)
                jobs(2)
                if attn:
                    silu(t - 1, 1)
                row_chunk(1)
                jobs(3)
                if t == TU + 1:
                    x4(t - 2)
            run_last(chunk, job, last_unit)

        @block.vector
        def _(dve):
            def stats(src, st, m, ve, nm, S, q):
                done = lambda i: i.then_inc(S.sem, 1)
                settle(dve)
                for k in range(KT):
                    last = dve.bn_stats(st[:, k, :], src(k))
                done(last)
                dve.wait_ge(S.sem, S.upto(q, "stats"))
                settle(dve)
                for k in range(KT):
                    last = dve.bn_aggr(m[:, k, :], st[:, k, :])
                done(last)
                dve.wait_ge(S.sem, S.upto(q, "aggr"))
                dve.tensor_scalar(ve[:, :], m[:, :, 1], EPS, None, ALU.add)
                done(dve.tensor_scalar(nm[:, :], m[:, :, 0], -1.0, None, ALU.mult))

            def main(g, n):
                par = g.par
                dve.wait_ge(m_bc, g * N + n + 1)
                if n == 0:
                    dve.wait_ge(PRE_DVE.sem, PRE_DVE.upto(g, "w1"))
                for h in range(NH):
                    if g.least(1) or n:
                        dve.wait_ge(m_scan, g * NS + NH * (n - 1) + h + 1)
                    dve.tensor_tensor(dB[h][:, :], wu[par][:, h, :], pB[:, :], ALU.mult).then_inc(m_mul, 1)
                for h in range(NH):
                    s = NH * n + h
                    dve.wait_ge(m_exp, g * NS + s + 1)
                    dve.wait_ge(m_mul, g * NS + s + 1)
                    if g.least(1) or s >= NB:
                        dve.wait_ge(m_sum, g * NS + s - NB + 1)
                    dve.tensor_tensor_scan(hs[s % NB][:, :], dA[s % NA][:, :, :].rearrange("p b t -> p (b t)"), dB[h][:, :], 0.0,
                                           ALU.mult, ALU.add).then_inc(m_scan, 1)

            def nrm_aux(q, slot):
                if slot == 10:
                    dve.wait_ge(s_x, 16 * (q + 1))
                    stats(lambda k: xres[:, bass.ds(q * KT + k, 1), :], stat, mv, veps, nmean, NRM_DVE, q)

            def pre_aux(q, slot):
                par = q.par
                done = lambda i: i.then_inc(PRE_DVE.sem, 1)
                if slot == 0 and not q.least(1):
                    dve.wait_ge(s_w, 16 * NW)
                    dve.wait_ge(s_cst, 1)
                    for i in range(2):
                        if i:
                            dve.wait_ge(s_bias, 2 * i)
                        dve.tensor_copy(bias3[:, :], biasf).then_inc(s_bias, 1)
                        dve.wait_ge(s_bias, 2 * i + 1)
                        dve.scalar_tensor_tensor(out=biasf, in0=bias3[:, :], scalar=c_row[i], in1=biasf,
                                                 op0=ALU.mult, op1=ALU.add).then_inc(s_bias, 1)
                    dve.wait_ge(s_bias, 4)
                    dve.tensor_copy(bias3[:, :], biasf).then_inc(s_bias, 1)
                if slot in (1, 2):
                    h = slot - 1
                    dve.wait_ge(PRE_ACT.sem, PRE_ACT.upto(q, f"xh{2 * h + 1}"))
                    for k in range(TAPS - 1):
                        if k:
                            dve.wait_ge(PRE_DVE.sem, PRE_DVE.upto(q, f"conv{h}_{k - 1}"))
                        done(dve.scalar_tensor_tensor(out=acc[:, h, :, :], in0=xhp[:, h, :, k:k + L], scalar=c_cw(h, k),
                                                      in1=acc[:, h, :, :], op0=ALU.mult, op1=ALU.add))
                if slot == 14:
                    for h in range(NH):
                        dve.wait_ge(PRE_ACT.sem, PRE_ACT.upto(q, f"spln{h}"))
                        done(dve.tensor_tensor(dl[par][:, h, :], dl[par][:, h, :], wu[par][:, h, :], ALU.add))
                    for h in range(NH):
                        dve.wait_ge(PRE_DVE.sem, PRE_DVE.upto(q, f"delta{h}"))
                        done(dve.tensor_tensor(wu[par][:, h, :], dl[par][:, h, :], u[par][:, h, :], ALU.mult))

            def post_aux(q, slot):
                par = q.par
                done = lambda i: i.then_inc(POST_DVE.sem, 1)
                own = lambda name: dve.wait_ge(POST_DVE.sem, POST_DVE.upto(q, name))
                row = slice(None)
                here = bass.ds(q * KT, KT)
                if slot == 0:
                    dve.wait_ge(m_sum, (q + 1) * NS)
                    if not q.least(1):
                        dve.wait_ge(s_zero, 16 * 8)
                    if q.least(1):
                        dve.wait_ge(POST_PE.sem, POST_PE.upto(q - 1, "out1"))
                    dve.wait_ge(Z_ACT.sem, Z_ACT.upto(q, "silu"))
                    for h in range(NH):
                        done(dve.scalar_tensor_tensor(out=yz[:, h, :], in0=u[par][:, h, :], scalar=c_D(h), in1=pY[h][:, :],
                                                      op0=ALU.mult, op1=ALU.add))
                    for h in range(NH):
                        own(f"yt{h}")
                        done(dve.tensor_tensor(yz[:, h, :], yz[:, h, :], zs[par][:, h, :], ALU.mult))
                if slot in (2, 3):
                    for c in (slot - 2,):
                        dve.wait_ge(POST_PE.sem, POST_PE.upto(q, f"out{c}"))
                        xs = xres[:, bass.ds(q * KT + 4 * c, 4), :]
                        done(dve.tensor_tensor(xs, xs, bank("POST", f"out{c}").rearrange("p (k d) -> p k d", d=D), ALU.add))
                if slot == 4:
                    own("res1")
                    stats(lambda k: xres[:, bass.ds(q * KT + k, 1), :], stat2, mv2, veps2, nmean2, POST_DVE, q)
                by_expert = lambda name: bank("POST", name)[:, 0:KT * E].rearrange("p (k e) -> p k e", e=E)
                bc = lambda t: t[:, :].unsqueeze(2).to_broadcast([128, KT, E])
                if slot == 11:
                    pL = by_expert("logits")
                    dve.wait_ge(POST_PE.sem, POST_PE.upto(q, "logits"))
                    done(dve.tensor_reduce(mx[:, :], pL, AX.X, ALU.max))
                    own("mx")
                    done(dve.tensor_tensor(lm[:, :, :], pL, bc(mx), ALU.subtract))
                if slot == 13:
                    dve.wait_ge(POST_ACT.sem, POST_ACT.upto(q, "ex"))
                    done(dve.tensor_reduce(sm[:, :], ex[:, :, :], AX.X, ALU.add))
                    own("sm")
                    done(dve.reciprocal(pr[:, :], sm[:, :]))
                    own("lm")
                    done(dve.scalar_tensor_tensor(out=sc[:, :, :], in0=ex[:, :, :], scalar=1.0,
                                                  in1=w8[:, :].unsqueeze(1).to_broadcast([128, KT, E]),
                                                  op0=ALU.is_ge, op1=ALU.mult))
                    own("eq")
                    done(dve.tensor_reduce(ms[:, :], sc[:, :, :], AX.X, ALU.max))
                    own("ms")
                    done(dve.tensor_tensor(oh[:, :, :], sc[:, :, :], bc(ms), ALU.is_equal))
                if slot == 15:
                    dve.wait_ge(POST_PE.sem, POST_PE.upto(q, "cum"))
                    done(dve.tensor_tensor(oc[:, :, :], oh[:, :, :], by_expert("cum"), ALU.mult))
                    own("oc")
                    done(dve.tensor_reduce(rank[:, :], oc[:, :, :], AX.X, ALU.add))
                    done(dve.tensor_scalar(base[:, :], ms[:, :], float(-CAP), float(E * CAP - 1), ALU.mult, ALU.add))
                    own("base")
                    done(dve.tensor_scalar(kept[:, :], rank[:, :], float(CAP), None, ALU.is_le))
                    done(dve.tensor_scalar(lost[:, :], rank[:, :], float(CAP), float(SLOTS), ALU.is_gt, ALU.mult))
                    done(dve.tensor_tensor(srow[:, :], base[:, :], rank[:, :], ALU.add))
                    own("srow")
                    if q.least(1):
                        dve.wait_ge(s_scat, 16 * KT * q)
                    done(dve.tensor_tensor(sidx[:, :], srow[:, :], lost[:, :], ALU.add))
                    done(dve.scalar_tensor_tensor(out=grow[:, :], in0=rank[:, :], scalar=float(CAP), in1=base[:, :],
                                                  op0=ALU.min, op1=ALU.add))
                    own("grow")
                    done(dve.tensor_copy(gidx[:, here], grow[:, :]))
                    done(dve.tensor_tensor(gwt[:, here], pr[:, :], kept[:, :], ALU.mult))
            run_groups(dve, main, [("PRE", pre_aux), ("POST", post_aux), ("NRM", nrm_aux)])

            def unit(t):
                if not t.least(1):
                    rows_in(t)
                rows_in(t + 1)
                if t.least(1):
                    rows_out(t - 1)

            def rows_in(t):
                dve.wait_ge(e_T, (t + 1) * 1)
                if t.least(2):
                    dve.wait_ge(e_h, (t - 1) * KF)
                dve.tensor_copy(xeT[t.par][:, :], pT[t.par][:, :]).then_inc(e_xT, 1)

            def rows_out(t):
                dve.wait_ge(e_y, (t + 1) * 1)
                if t.least(2):
                    dve.wait_ge(s_ye[t.par], t // 2 * 16)
                dve.tensor_tensor(ye[t.par][:, :, :], pE[t.par][:, :].rearrange("p (k d) -> p k d", d=D),
                                  b2[(t // UE).par][:, :].unsqueeze(1).to_broadcast([128, 4, D]), ALU.add).then_inc(e_add, 1)

            def unit_last(t):
                if t.least(UNITS - 1) and t.reg is None:
                    rows_out(t - 1)
                else:
                    unit(t)
            run_units(dve, unit_last, lambda t: rows_out(t - 1))

            dve.wait_ge(s_w3, 16 * 7)
            dve.tensor_scalar(wg[:, :], gi[:, :], 1.0 / 127.0, None, ALU.mult)
            dve.tensor_scalar(wup[:, :], ui[:, :], 1.0 / 127.0, None, ALU.mult)
            dve.tensor_scalar(wd[:, :, :], di[:, :, :], 1.0 / 127.0, None, ALU.mult)
            dve.tensor_tensor(wk[:, :, :], mask8[:, :].unsqueeze(2).to_broadcast([128, C8, SL]),
                              wkr[:, :].unsqueeze(1).to_broadcast([128, C8, SL]), ALU.mult).then_inc(s_wk, 1)

            def block_stats(S, j, part, rows, st, m, ve, nm):
                done = lambda i: i.then_inc(S.sem, 1)
                for i in range(BQ):
                    last = dve.bn_stats(st[:, i, :], rows(i))
                done(last)
                dve.wait_ge(S.sem, S.upto(j, "stats" + part))
                for i in range(BQ):
                    last = dve.bn_aggr(m[:, i, :], st[:, i, :])
                done(last)
                dve.wait_ge(S.sem, S.upto(j, "aggr" + part))
                dve.tensor_scalar(ve, m[:, :, 1], EPS, None, ALU.add)
                done(dve.tensor_scalar(nm, m[:, :, 0], -1.0, None, ALU.mult))

            def chunk(j, i):
                dve.wait_ge(s_gx[i], 16 * BQ * (j + 1))
                for l in range(BQ * i, BQ * i + BQ):
                    at_ = TB * l + j
                    last = dve.scalar_tensor_tensor(out=xres[:, at_, :], in0=gx[:, l, :], scalar=gwt[:, at_:at_ + 1],
                                                    in1=xres[:, at_, :], op0=ALU.mult, op1=ALU.add)
                last.then_inc(A_DVE.sem, 1)
                dve.wait_ge(A_DVE.sem, A_DVE.upto(j, f"x2_{i}"))
                if j >= 1:
                    dve.wait_ge(A_POOL.sem, A_POOL.upto(j - 1, f"nmr{i}"))
                four = slice(BQ * i, BQ * i + BQ)
                block_stats(A_DVE, j, str(i), lambda k: xres[:, TB * (BQ * i + k) + j, :], stA[:, four, :], mvA[:, four, :], veA[:, four], nmA[:, four])

            def scores(t):
                j, c = t // BQ, t % BQ
                done = lambda i: i.then_inc(T_DVE.sem, 1)
                own = lambda n: dve.wait_ge(T_DVE.sem, T_DVE.upto(t, n))
                dve.wait_ge(A_ACT.sem, A_ACT.upto(j, "k1"))
                if t >= 1:
                    dve.wait_ge(T_DVE.sem, T_DVE.upto(t - 1, T_DVE.names[-1]))
                for d in range(QH):
                    qd = q[j % 2][:, BQ * c:BQ * c + BQ, :].rearrange("p l (h d) -> p l h d", d=QH)[:, :, :, d]
                    kd = kk[j % 2][:, HEADS * d:HEADS * d + HEADS, :]
                    done(dve.tensor_tensor(qk[d][:, :, :, :], qd.unsqueeze(3).to_broadcast([128, BQ, HEADS, SL]),
                                           kd.unsqueeze(1).to_broadcast([128, BQ, HEADS, SL]), ALU.mult))
                flat = lambda x_: x_[:, :, :, :].rearrange("p l h s -> p (l h s)")
                own("qk1")
                done(dve.tensor_tensor(flat(qk[0]), flat(qk[0]), flat(qk[1]), ALU.add))
                own("qk3")
                done(dve.tensor_tensor(flat(qk[2]), flat(qk[2]), flat(qk[3]), ALU.add))
                own("s23")
                done(dve.tensor_tensor(flat(qk[0]), flat(qk[0]), flat(qk[2]), ALU.add))
                own("s")
                s_ = qk[0][:, :, :, :].rearrange("p l h s -> p (l h) s")
                done(dve.tensor_reduce(am[:, :], s_, AX.X, ALU.max))
                own("max")
                done(dve.tensor_tensor(at[t % 2][:, :, :], s_, am[:, :].unsqueeze(2).to_broadcast([128, BQ * HEADS, SL]), ALU.subtract))

            def softmax(t):
                done = lambda i: i.then_inc(T_DVE.sem, 1)
                own = lambda n: dve.wait_ge(T_DVE.sem, T_DVE.upto(t, n))
                a = at[t % 2][:, :, :]
                dve.wait_ge(T_ACT.sem, T_ACT.upto(t, "exp"))
                done(dve.tensor_reduce(ad[:, :], a, AX.X, ALU.add))
                own("den")
                done(dve.reciprocal(ar[:, :], ad[:, :]))
                own("rden")
                done(dve.tensor_tensor(a, a, ar[:, :].unsqueeze(2).to_broadcast([128, BQ * HEADS, SL]), ALU.mult))

            def weigh(t, l):
                done = lambda i: i.then_inc(T_DVE.sem, 1)
                own = lambda n: dve.wait_ge(T_DVE.sem, T_DVE.upto(t, n))
                if l == 0:
                    dve.wait_ge(A_ACT.sem, A_ACT.upto(t // BQ, "v2"))
                    own("an")
                if l not in ON_DVE and t >= 1:
                    dve.wait_ge(O_PE.sem, O_PE.upto(t - 1, f"o{l}"))
                done(dve.tensor_tensor(pv[l][:, :, :, :].rearrange("p v h s -> p h v s"),
                                       at[t % 2][:, HEADS * l:HEADS * l + HEADS, :].unsqueeze(2).to_broadcast([128, HEADS, DV, SL]),
                                       vv[t // BQ % 2][:, :, :].rearrange("p (h v) s -> p h v s", h=HEADS), ALU.mult))
                if l in ON_DVE:
                    own(f"pv{l}")
                    if t >= 2:
                        dve.wait_ge(O_PE.sem, O_PE.upto(t - 2, f"o{l}"))
                    done(dve.tensor_reduce(on[t % 2][:, l, :], pv[l][:, :, :, :].rearrange("p v h s -> p (v h) s"), AX.X, ALU.add))

            def norm(t):
                dve.wait_ge(B_PE.sem, B_PE.upto(t, "proj"))
                if t >= 1:
                    dve.wait_ge(B_POOL.sem, B_POOL.upto(t - 1, "nmr"))
                block_stats(B_DVE, t, "", lambda i: pP[:, i * D:(i + 1) * D], stB[:, :, :], mvB[:, :, :], veB[:, :], nmB[:, :])

            def hidden(t, k):
                dve.wait_ge(F_ACT.sem, F_ACT.upto(t, f"silu{k}"))
                dve.wait_ge(F_PE.sem, F_PE.upto(t, f"u{k}"))
                if k == 0 and t >= 1:
                    dve.wait_ge(D_PE.sem, D_PE.upto(t - 1, "down"))
                dve.tensor_tensor(hh[:, k, :], sg[k][:, :], pU[:, :], ALU.mult).then_inc(F_DVE.sem, 1)

            def last_unit(t, row_chunk, jobs):
                if t < TU:
                    scores(t)
                if t >= 2:
                    hidden(t - 2, 0)
                if 1 <= t <= TU:
                    norm(t - 1)
                if t >= 2:
                    hidden(t - 2, 1)
                row_chunk(0)
                if t < TU:
                    softmax(t)
                if t >= 2:
                    hidden(t - 2, 2)
                for l in range(BQ):
                    if t < TU:
                        weigh(t, l)
                    if l == 1:
                        row_chunk(1)
            run_last(chunk, lambda j, name: None, last_unit, rows_ahead=3)

        @block.tensor
        def _(pe):
            pe.wait_ge(s_ident, 1)

            def bcast(g, n):
                if g.least(1) or n:
                    pe.wait_ge(m_mul, g * NS + NH * n)
                if n == 0 and not g.least(1):
                    pe.wait_ge(s_sel, 3)
                    pe.wait_ge(s_bias, 5)
                if n == 0:
                    pe.wait_ge(PRE_POOL.sem, PRE_POOL.upto(g, "cast3"))
                for c in range(2):
                    last = pe.matmul(pB[:, c * 512:(c + 1) * 512], sel[:, n, :], Bs[g.par][:, c * 512:(c + 1) * 512],
                                     start=True, stop=True)
                last.then_inc(m_bc, 1)

            def main(g, n):
                if n + 1 < N:
                    bcast(g, n + 1)
                elif g.reg is not None or g.off + 1 < G:
                    bcast(g + 1, 0)
                for h in range(NH):
                    if n == 0 and g.least(1):
                        pe.wait_ge(POST_DVE.sem, POST_DVE.upto(g - 1, f"yt{h}"))
                    s = NH * n + h
                    pe.wait_ge(m_scan, g * NS + s + 1)
                    for c in range(2):
                        last = pe.matmul(pY[h][:, c * 512:(c + 1) * 512], ident[:, :], hs[s % NB][:, c * 512:(c + 1) * 512],
                                         start=(n == 0), stop=(n == N - 1))
                    last.then_inc(m_sum, 1)

            def job(q, stage, name, emit):
                after(pe, q - AHEAD[stage], stage, name)
                emit(bank(stage, name)).then_inc({"NRM": NRM_PE, "PRE": PRE_PE, "POST": POST_PE}[stage].sem, 1)

            def transposed(src, c):
                def emit(out):
                    for k in range(4):
                        last = pe.transpose(out[:, k * 128:(k + 1) * 128], src[:, 4 * c + k, :], ident[:, :])
                    return last
                return emit

            def projected(w, src, c, rows=128):
                def emit(out):
                    for k in range(len(w)):
                        last = pe.matmul(out[0:rows, :], w[k], src[k][:, c * 512:(c + 1) * 512],
                                         start=(k == 0), stop=(k == len(w) - 1))
                    return last
                return emit

            def nrm_aux(q, slot):
                if slot == 13:
                    pe.wait_ge(NRM_ACT.sem, NRM_ACT.upto(q, "norm"))
                    for c in range(2):
                        job(q, "NRM", f"t{c}", transposed(xn, c))

            def xh_early(q, slot):
                if slot == 0:
                    if not q.least(1):
                        pe.wait_ge(s_w, 16 * NW)
                    pe.wait_ge(NRM_ACT.sem, NRM_ACT.upto(q, "t1"))
                    for j in range(4):
                        h, c = j // 2, j % 2
                        job(q, "PRE", f"xh{j}", projected([w_in[:, h * 128:(h + 1) * 128]], [xnT[:, :]], c))

            def pre_aux(q, slot):
                us = [u[q.par][:, k, :] for k in range(NH)]
                for j in {1: [0], 2: [1, 2], 3: [3]}.get(slot, []):
                    h, c = j // 2, j % 2
                    job(q, "PRE", f"z{j}", projected([w_in[:, DI + h * 128:DI + (h + 1) * 128]], [xnT[:, :]], c))
                if slot in (4, 5):
                    if slot == 4:
                        pe.wait_ge(PRE_ACT.sem, PRE_ACT.upto(q, "u1"))
                    job(q, "PRE", f"b{slot - 4}", projected([w_b[:, k, :] for k in range(NH)], us, slot - 4, 96))
                if slot in (6, 9, 10, 11):
                    j = max(slot - 8, 0)
                    h, c = j // 2, j % 2
                    job(q, "PRE", f"dt{j}", projected([w_dt[:, k, h * 128:(h + 1) * 128] for k in range(NH)], us, c))
                if slot == 12 and not q.least(1):
                    bcast(q, 0)

            def post_aux(q, slot, late=0):
                if slot in (1, 2) and slot - 1 == late:
                    pe.wait_ge(POST_DVE.sem, POST_DVE.upto(q, "yz1"))
                    for c in (slot - 1,):
                        def emit(out):
                            pe.matmul(out.rearrange("p (k d) -> p k d", d=D), ones3[:, :], three(0, D, 4), start=True, stop=False)
                            for k in range(4):
                                o = out[:, k * 128:(k + 1) * 128]
                                for h in range(NH):
                                    last = pe.matmul(o, yz[:, h, (4 * c + k) * 128:(4 * c + k + 1) * 128], w_out[:, h, :],
                                                     start=False, stop=(k == 3 and h == NH - 1))
                            return last
                        job(q, "POST", f"out{c}", emit)
                if slot in (7, 8):
                    pe.wait_ge(POST_ACT.sem, POST_ACT.upto(q, "norm"))
                    for c in (slot - 7,):
                        job(q, "POST", f"t{c}", transposed(xn2, c))
                if slot == 10:
                    pe.wait_ge(POST_ACT.sem, POST_ACT.upto(q, "t1"))

                    def emit(out):
                        for k in range(KT):
                            last = pe.matmul(out[:, k * E:(k + 1) * E], xn2T[:, k * 128:(k + 1) * 128], rt_w[:, :], start=True, stop=True)
                        return last
                    job(q, "POST", "logits", emit)
                if slot == 14:
                    pe.wait_ge(POST_DVE.sem, POST_DVE.upto(q, "oh"))
                    pe.wait_ge(POST_POOL.sem, POST_POOL.upto(q, f"pre{KT - 1}"))

                    def emit(out):
                        pe.matmul(out[:, 0:KT * E], tri[:, :], oh[:, :, :].rearrange("p k e -> p (k e)"), start=True, stop=False)
                        return pe.matmul(out[:, 0:KT * E], ones[:, :], pre[:, 0:KT, :].rearrange("p k e -> p (k e)"),
                                         start=False, stop=True)
                    job(q, "POST", "cum", emit)

            def out_late(q, slot):
                if slot == 2:
                    post_aux(q, slot, 1)

            run_groups(pe, main, [("POST", post_aux), ("PRE", pre_aux), ("POST", out_late), ("NRM", nrm_aux)],
                       early=[("PRE", xh_early)])

            def unit(t):
                if not t.least(1):
                    turn(t)
                up(t)
                turn(t + 1)
                if t.least(1):
                    down(t - 1)

            def turn(t):
                pe.wait_ge(s_xe[t.par], (t // 2 + 1) * 16)
                if t.least(2):
                    pe.wait_ge(e_xT, (t - 1) * 1)
                for k in range(4):
                    last = pe.transpose(pT[t.par][:, k * 128:(k + 1) * 128], xe[t.par][:, k, :], ident[:, :])
                last.then_inc(e_T, 1)

            def up(t):
                par = (t // UE).par
                pe.wait_ge(e_xT, (t + 1) * 1)
                if t.off % UE == 0:
                    pe.wait_ge(s_we[par], (t // UE // 2 + 1) * 64)
                for k in range(KF):
                    if t.least(1):
                        pe.wait_ge(e_gelu, (t - 1) * KF + k + 1)
                    pe.matmul(pH[k][:, :], w1[par][:, k * 128:(k + 1) * 128], xeT[t.par][:, :], start=True, stop=True).then_inc(e_h, 1)

            def down(t):
                par = (t // UE).par
                pe.wait_ge(e_gelu, (t + 1) * KF)
                if t.least(2):
                    pe.wait_ge(e_add, (t - 1) * 1)
                for i in range(4):
                    for k in range(KF):
                        last = pe.matmul(pE[t.par][:, i * 128:(i + 1) * 128], he[t.par][:, k, i * 128:(i + 1) * 128], w2[par][:, k, :],
                                         start=(k == 0), stop=(k == KF - 1))
                last.then_inc(e_y, 1)

            def unit_last(t):
                if t.least(UNITS - 1) and t.reg is None:
                    up(t)
                    down(t - 1)
                else:
                    unit(t)
            run_units(pe, unit_last, lambda t: down(t - 1))

            pe.wait_ge(s_w3, 16 * 7)
            pe.wait_ge(s_wk, 1)

            def job(j, name):
                i, kind, n = A_JOBS.index(name), name[0], int(name[1])
                o = pA[i % 2]
                if kind == "t":
                    pe.wait_ge(A_NRM.sem, A_NRM.upto(j, f"norm{n}"))
                if i >= 2:
                    pe.wait_ge(A_ACT.sem, A_ACT.upto(j, A_JOBS[i - 2]))
                elif j >= 1:
                    pe.wait_ge(A_ACT.sem, A_ACT.upto(j - 1, A_JOBS[-1]))
                if kind == "t":
                    for m in range(4):
                        last = pe.transpose(o[:, m * 128:(m + 1) * 128], xnA[:, 4 * n + m, :], ident[:, :])
                if kind == "g":
                    for m in range(4):
                        last = pe.transpose(o[:, m * 128:(m + 1) * 128],
                                            xnA[:, :, :].rearrange("p l (c g) -> p g (l c)", c=C8)[:, 4 * n + m, :], ident[:, :])
                if kind == "q":
                    pe.wait_ge(A_ACT.sem, A_ACT.upto(j, f"t{2 * n + 1}"))
                    pe.matmul(o[:, :].rearrange("p (m c) -> p m c", c=QD), ones3[:, :], three(2 * D, QD, 8), start=True, stop=False)
                    for m in range(8):
                        last = pe.matmul(o[:, m * QD:(m + 1) * QD], xnAT[:, 8 * n + m, :], wq[:, :], start=False, stop=(m == 7))
                if kind == "v":
                    if n == 0:
                        pe.wait_ge(A_ACT.sem, A_ACT.upto(j, "g3"))
                    for m in range(min(7, D // C8 - 7 * n)):
                        last = pe.matmul(o[:, m * C8 * SL:(m + 1) * C8 * SL], xnG[:, 7 * n + m, :],
                                         wk[:, :, :].rearrange("p c s -> p (c s)"), start=True, stop=True)
                if kind == "r":
                    if n == 0:
                        pe.wait_ge(A_ACT.sem, A_ACT.upto(j, "q1"))
                    for m in range(4):
                        last = pe.transpose(o[:, m * 128:(m + 1) * 128],
                                            q[j % 2][:, :, :].rearrange("p l (c g) -> p g (l c)", c=C8)[:, 4 * n + m, :], ident[:, :])
                if kind == "k":
                    pe.wait_ge(A_ACT.sem, A_ACT.upto(j, "r1"))
                    for m in range(4):
                        last = pe.matmul(o[:, m * C8 * SL:(m + 1) * C8 * SL], qG[:, 4 * n + m, :],
                                         wk[:, :, :].rearrange("p c s -> p (c s)"), start=True, stop=True)
                last.then_inc(A_PE.sem, 1)

            def turned_sum(t, l):
                if l == 0 and t >= 1:
                    pe.wait_ge(B_ACT.sem, B_ACT.upto(t - 1, "oT"))
                o = pO[:, l * 128:(l + 1) * 128]
                if l in ON_DVE:
                    pe.wait_ge(T_DVE.sem, T_DVE.upto(t, f"o{l}"))
                    last = pe.transpose(o, on[t % 2][:, l, :], ident[:, :])
                else:
                    pe.wait_ge(T_DVE.sem, T_DVE.upto(t, f"pv{l}"))
                    for k in range(SL):
                        last = pe.matmul(o, pv[l][:, :, :, :].rearrange("p v h s -> p (v h) s")[:, :, k], ident[:, :],
                                         start=(k == 0), stop=(k == SL - 1))
                last.then_inc(O_PE.sem, 1)

            def residual(t):
                if t >= 1:
                    pe.wait_ge(B_ACT.sem, B_ACT.upto(t - 1, "x3"))
                whole = pP[:, :].rearrange("p (i d) -> p i d", d=D)
                pe.matmul(whole, ident[:, :], tiles_of(t), start=True, stop=False)
                pe.matmul(whole, ones3[:, :], three(D, D, BQ), start=False, stop=False)

            def proj(t):
                pe.wait_ge(B_ACT.sem, B_ACT.upto(t, "oT"))
                for i in range(BQ):
                    last = pe.matmul(pP[:, i * 128:(i + 1) * 128], oT[:, i * 128:(i + 1) * 128], wo[:, :],
                                     start=False, stop=(i == BQ - 1))
                last.then_inc(B_PE.sem, 1)

            def turn_x(t):
                pe.wait_ge(B_ACT.sem, B_ACT.upto(t, "norm"))
                if t >= 1:
                    pe.wait_ge(B_ACT.sem, B_ACT.upto(t - 1, "xT"))
                for i in range(BQ):
                    last = pe.transpose(pT3[:, i * 128:(i + 1) * 128], xnB[:, i, :], ident[:, :])
                last.then_inc(B_PE.sem, 1)

            def gate(t, k):
                if k == 0:
                    pe.wait_ge(B_ACT.sem, B_ACT.upto(t, "xT"))
                if k >= 1 or t >= 1:
                    pe.wait_ge(F_ACT.sem, F_ACT.upto(t - (k == 0), f"silu{(k - 1) % KH}"))
                pe.matmul(pG[:, :], wg[:, k * 128:(k + 1) * 128], xnBT[t % 2][:, :], start=True, stop=True).then_inc(F_PE.sem, 1)

            def up3(t, k):
                if k >= 1 or t >= 1:
                    pe.wait_ge(F_DVE.sem, F_DVE.upto(t - (k == 0), f"h{(k - 1) % KH}"))
                pe.matmul(pU[:, :], wup[:, k * 128:(k + 1) * 128], xnBT[t % 2][:, :], start=True, stop=True).then_inc(F_PE.sem, 1)

            def down3(t):
                if t >= 1:
                    pe.wait_ge(X_ACT.sem, X_ACT.upto(t - 1, "x4"))
                pe.wait_ge(B_ACT.sem, B_ACT.upto(t, "x3"))
                pe.matmul(pD[:, :].rearrange("p (i d) -> p i d", d=D), ident[:, :], tiles_of(t), start=True, stop=False)
                pe.wait_ge(F_DVE.sem, F_DVE.upto(t, f"h{KH - 1}"))
                for i in range(BQ):
                    for k in range(KH):
                        last = pe.matmul(pD[:, i * 128:(i + 1) * 128], hh[:, k, i * 128:(i + 1) * 128], wd[:, k, :],
                                         start=False, stop=(i == BQ - 1 and k == KH - 1))
                last.then_inc(D_PE.sem, 1)

            def last_unit(t, row_chunk, jobs):
                now, attn, ffn = t < TU, 1 <= t <= TU, t >= 2
                if attn:
                    residual(t - 1)
                    turned_sum(t - 1, 3)
                if ffn and t < TU:
                    gate(t - 2, 2)
                if attn:
                    proj(t - 1)
                if ffn and t >= TU:
                    gate(t - 2, 2)
                if ffn:
                    up3(t - 2, 1)
                jobs(0)
                if ffn:
                    up3(t - 2, 2)
                if attn:
                    turn_x(t - 1)
                if ffn:
                    down3(t - 2)
                jobs(1)
                if now:
                    turned_sum(t, 0)
                if attn:
                    gate(t - 1, 0)
                    up3(t - 1, 0)
                jobs(2)
                if now:
                    turned_sum(t, 1)
                if attn:
                    gate(t - 1, 1)
                if now:
                    turned_sum(t, 2)
                jobs(3)
            run_last(lambda j, i: None, job, last_unit)


_NAMES = ["L0_attn_x", "L0_attn_W_in", "L0_attn_W_dt", "L0_attn_W_x", "L0_attn_W_out", "L0_ffn_b1",
          "L0_ffn_w1", "L0_ffn_w2", "L0_ffn_b2"]


def kernel(**inputs):
    import numpy as _np
    import concourse.bacc as _bacc
    from concourse import mybir as _mybir
    from concourse.bass_utils import run_bass_kernel_spmd as _run

    nc = _bacc.Bacc("TRN2", target_bir_lowering=False, num_devices=1)
    a = {k: _np.ascontiguousarray(v) for k, v in inputs.items()}
    put = {n: a[n] for n in _NAMES}
    cont = _np.ascontiguousarray
    by_col = lambda v: v.reshape(-1, 128).T
    b_x = _np.tile(_np.tile(a["L0_attn_b_x"][16:32], 2), 4).reshape(128, 1)
    put["cols"] = cont(_np.concatenate([
        by_col(a["L0_attn_b_in"]), by_col(a["L0_attn_conv_b"]), by_col(a["L0_attn_b_dt"]), by_col(a["L0_attn_D"]), b_x,
        a["L0_attn_conv_w"].reshape(2, 128, 4).transpose(1, 0, 2).reshape(128, 8),
        a["L0_attn_A_log"].reshape(2, 128, 16).transpose(1, 0, 2).reshape(128, 32),
        -(_np.arange(128)[:, None] >= _np.array([32, 64, 1, 2])).astype(_np.float32)], axis=1))
    put["bias3"] = _np.tile(_np.concatenate([a["L0_attn_b_out"], a["L1_attn_b_out"], a["L1_attn_b_q"]]), (3, 1))
    put["router_wT"] = cont(a["L0_ffn_router_w"].T)
    put["b1T"] = cont(a["L0_ffn_b1"].reshape(8, 4, 128).transpose(0, 2, 1))
    put["w_qT"] = cont(a["L1_attn_w_q"].T)
    put["w_outT"] = cont(a["L1_attn_w_out"].T)
    put["wkr"] = cont(_np.repeat(a["L1_attn_w_kv"][0:9, 0:16].T, 8, axis=0))
    put["mask8"] = _np.tile(_np.eye(8, dtype=_np.float32), (16, 1))
    put["w_gateT"] = cont(a["L1_ffn_w_gate"].T)
    put["w_upT"] = cont(a["L1_ffn_w_up"].T)
    put["w_downT"] = cont(a["L1_ffn_w_down"].T)
    P = {n: nc.dram_tensor(f"in_{n}_dram", v.shape, _mybir.dt.from_np(v.dtype), kind="ExternalInput").ap() for n, v in put.items()}
    P["out"] = nc.dram_tensor("out_0_dram", (16, 512, 128), _mybir.dt.float32, kind="ExternalOutput").ap()
    P["n_weights"] = 12
    prog(nc, P)
    r = _run(nc, [{f"in_{n}_dram": v for n, v in put.items()}], core_ids=[0])
    return r.results[0]["out_0_dram"]
```
